# Optimizing a Trainium2 kernel written in Bass

```python
import numpy as np
import jax
import jax.numpy as jnp

def _softmax(x, axis=-1):
    return jax.nn.softmax(x, axis=axis)

def _gelu(x):
    return jax.nn.gelu(x, approximate=True)

def _silu(x):
    return jax.nn.silu(x)

def _sigmoid(x):
    return jax.nn.sigmoid(x)

def _layernorm(x, axis=-1, eps=1e-05):
    m = jnp.mean(x, axis=axis, keepdims=True)
    v = jnp.var(x, axis=axis, keepdims=True)
    return (x - m) / jnp.sqrt(v + eps)

def _scatter_add(tgt, idx, src, axis=0):
    return tgt.at[idx].add(src)

def _segment_sum(src, seg, n):
    return jax.ops.segment_sum(src, seg, n)
kernel_name = 'mk_flamingo_gated_d2_seqx_r8_5139f5'

def setup_inputs(seed: int=0):
    np.random.seed(seed)
    _w = jnp.asarray

    def _rec_inputs():
        import jax
        import jax.numpy as jnp
        _rk = jax.random.key(seed)
        x = 7.22e-05 + 1 * jax.random.normal(jax.random.fold_in(_rk, 1), (4, 256, 256), jnp.float32)
        _lenS = 256 - jax.random.randint(jax.random.fold_in(_rk, 7), (4,), 0, max(1, 256 // 4) + 1, jnp.int32)
        _lenS2 = 256 - jax.random.randint(jax.random.fold_in(_rk, 8), (4,), 0, max(1, 256 // 4) + 1, jnp.int32)
        _ctx_1024P = jax.random.normal(jax.random.fold_in(_rk, 11), (4, 16, 128), jnp.float32)
        _ctx_1024c = jax.random.dirichlet(jax.random.fold_in(_rk, 511), 0.3 * jnp.ones((16,), jnp.float32), (4, 256))
        _ctx_1024t = jnp.einsum('bsk,bkd->bsd', _ctx_1024c, _ctx_1024P)
        _ctx_1024t = _ctx_1024t * jax.lax.rsqrt(jnp.mean(jnp.square(_ctx_1024t)) + 1e-12) * 0.953939
        ctx_1024 = 2.81802e-05 + 1.00001 * (_ctx_1024t + 0.3 * jax.random.normal(jax.random.fold_in(_rk, 611), (4, 256, 128), jnp.float32))
        _g = jax.random.normal(jax.random.fold_in(_rk, 9001), (2, 2), jnp.float32)
        _g = jnp.sign(_g) * jnp.maximum(jnp.abs(_g), 1.0) + (_g == 0) * 1.0
        g_xattn = _g[0]
        g_ffn = _g[1]
        return (x, ctx_1024, g_xattn, g_ffn)
    x, ctx_1024, g_xattn, g_ffn = _rec_inputs()

    def _L0_xattn_setup():
        import jax, jax.numpy as jnp
        import numpy as np
        key = jax.random.key(seed)
        ks = jax.random.split(key, 6)
        B, L, N, C, D = (8, 64, 256, 128, 128)
        return {'teacher_logits': jax.random.normal(ks[0], (B, L, N), dtype=jnp.float32), 'teacher_features': jax.random.normal(ks[1], (B, N, C), dtype=jnp.float32), 'Wq': jax.random.normal(ks[2], (D, C), dtype=jnp.float32) * (1.0 / np.sqrt(C)), 'bq': jnp.zeros((D,), dtype=jnp.float32), 'Wk': jax.random.normal(ks[3], (D, C), dtype=jnp.float32) * (1.0 / np.sqrt(C)), 'bk': jnp.zeros((D,), dtype=jnp.float32)}
    _L0_xattn_all = _L0_xattn_setup()
    _L0_xattn_in = {k: v for k, v in _L0_xattn_all.items() if k in ('Wq', 'bq', 'Wk', 'bk')}
    del _L0_xattn_all

    def _L0_ffn_setup():
        import jax, jax.numpy as jnp
        import numpy as np
        NUM_EXPERTS = 32
        TOP_K = 8
        THRESHOLD = 0.8
        HIDDEN = 256
        INTER = 96
        key = jax.random.key(seed)
        k1, k2, k3, k4 = jax.random.split(key, 4)
        hidden_states = jax.random.normal(k1, (2, 128, HIDDEN), jnp.float32)
        gate_weight = jax.random.normal(k2, (NUM_EXPERTS, HIDDEN), jnp.float32) * 0.02
        gate_up_proj = jax.random.normal(k3, (NUM_EXPERTS, 2 * INTER, HIDDEN), jnp.float32) * 0.02
        down_proj = jax.random.normal(k4, (NUM_EXPERTS, HIDDEN, INTER), jnp.float32) * 0.02
        return {'hidden_states': hidden_states, 'gate_weight': gate_weight, 'gate_up_proj': gate_up_proj, 'down_proj': down_proj}
    _L0_ffn_all = _L0_ffn_setup()
    _L0_ffn_in = {k: v for k, v in _L0_ffn_all.items() if k in ('gate_weight', 'gate_up_proj', 'down_proj')}
    del _L0_ffn_all

    def _L1_xattn_setup():
        import jax, jax.numpy as jnp
        import numpy as np
        EPS = 1e-05

        def rmsnorm(x, g, eps=EPS):
            var = jnp.mean(jnp.square(x), axis=-1, keepdims=True)
            return x * jax.lax.rsqrt(var + eps) * g
        key = jax.random.key(seed)
        ks = jax.random.split(key, 8)
        B, Sq, Skv = (2, 512, 64)
        dim, cdim, H, D = (256, 128, 16, 128)
        inner = H * D
        s = lambda f: 1.0 / np.sqrt(f)
        return {'hidden_states': jax.random.normal(ks[0], (B, Sq, dim), jnp.float32), 'encoder_hidden_states': jax.random.normal(ks[1], (B, Skv, cdim), jnp.float32), 'Wq': jax.random.normal(ks[2], (dim, inner), jnp.float32) * s(dim), 'Wk': jax.random.normal(ks[3], (cdim, inner), jnp.float32) * s(cdim), 'Wv': jax.random.normal(ks[4], (cdim, inner), jnp.float32) * s(cdim), 'Wo': jax.random.normal(ks[5], (inner, dim), jnp.float32) * s(inner), 'gq': jnp.ones((D,), jnp.float32), 'gk': jnp.ones((D,), jnp.float32)}
    _L1_xattn_all = _L1_xattn_setup()
    _L1_xattn_in = {k: v for k, v in _L1_xattn_all.items() if k in ('Wq', 'Wk', 'Wv', 'Wo', 'gq', 'gk')}
    del _L1_xattn_all

    def _L1_ffn_setup():
        import jax, jax.numpy as jnp
        import numpy as np
        HIDDEN = 256
        INTER = 704
        B, S = (2, 256)

        def _ternary(key, shape):
            return jax.random.randint(key, shape, -1, 2).astype(jnp.float32)
        key = jax.random.key(seed)
        ks = jax.random.split(key, 7)
        x = jax.random.normal(ks[0], (B, S, HIDDEN), dtype=jnp.float32)
        gate_w = _ternary(ks[1], (INTER, HIDDEN))
        up_w = _ternary(ks[2], (INTER, HIDDEN))
        down_w = _ternary(ks[3], (HIDDEN, INTER))
        gate_s = jax.random.uniform(ks[4], (INTER,), minval=0.01, maxval=0.1, dtype=jnp.float32)
        up_s = jax.random.uniform(ks[5], (INTER,), minval=0.01, maxval=0.1, dtype=jnp.float32)
        down_s = jax.random.uniform(ks[6], (HIDDEN,), minval=0.01, maxval=0.1, dtype=jnp.float32)
        return {'x': x, 'gate_w': gate_w, 'up_w': up_w, 'down_w': down_w, 'gate_s': gate_s, 'up_s': up_s, 'down_s': down_s}
    _L1_ffn_all = _L1_ffn_setup()
    _L1_ffn_in = {k: v for k, v in _L1_ffn_all.items() if k in ('gate_w', 'up_w', 'down_w', 'gate_s', 'up_s', 'down_s')}
    del _L1_ffn_all
    return {'x': x, 'ctx_1024': ctx_1024, 'g_xattn': g_xattn, 'g_ffn': g_ffn, 'L0_xattn_Wq': _L0_xattn_in['Wq'], 'L0_xattn_bq': _L0_xattn_in['bq'], 'L0_xattn_Wk': _L0_xattn_in['Wk'], 'L0_xattn_bk': _L0_xattn_in['bk'], 'L0_ffn_gate_weight': _L0_ffn_in['gate_weight'], 'L0_ffn_gate_up_proj': _L0_ffn_in['gate_up_proj'], 'L0_ffn_down_proj': _L0_ffn_in['down_proj'], 'L1_xattn_Wq': _L1_xattn_in['Wq'], 'L1_xattn_Wk': _L1_xattn_in['Wk'], 'L1_xattn_Wv': _L1_xattn_in['Wv'], 'L1_xattn_Wo': _L1_xattn_in['Wo'], 'L1_xattn_gq': _L1_xattn_in['gq'], 'L1_xattn_gk': _L1_xattn_in['gk'], 'L1_ffn_gate_w': _L1_ffn_in['gate_w'], 'L1_ffn_up_w': _L1_ffn_in['up_w'], 'L1_ffn_down_w': _L1_ffn_in['down_w'], 'L1_ffn_gate_s': _L1_ffn_in['gate_s'], 'L1_ffn_up_s': _L1_ffn_in['up_s'], 'L1_ffn_down_s': _L1_ffn_in['down_s']}

def reference(x, ctx_1024, g_xattn, g_ffn, L0_xattn_Wq, L0_xattn_bq, L0_xattn_Wk, L0_xattn_bk, L0_ffn_gate_weight, L0_ffn_gate_up_proj, L0_ffn_down_proj, L1_xattn_Wq, L1_xattn_Wk, L1_xattn_Wv, L1_xattn_Wo, L1_xattn_gq, L1_xattn_gk, L1_ffn_gate_w, L1_ffn_up_w, L1_ffn_down_w, L1_ffn_gate_s, L1_ffn_up_s, L1_ffn_down_s):
    import jax
    import jax.numpy as jnp

    def _L0_xattn_ref(teacher_logits, teacher_features, Wq, bq, Wk, bk):
        import jax, jax.numpy as jnp
        import numpy as np
        query = jnp.einsum('bnc,dc->bnd', teacher_features, Wq) + bq
        key = jnp.einsum('bnc,dc->bnd', teacher_features, Wk) + bk
        energy = jnp.einsum('bnd,bmd->bnm', query, key)
        attention = jax.nn.softmax(energy, axis=-1)
        x_m = jnp.einsum('bln,bmn->blm', teacher_logits, attention)
        return x_m

    def _L0_ffn_ref(hidden_states, gate_weight, gate_up_proj, down_proj):
        import jax, jax.numpy as jnp
        import numpy as np
        NUM_EXPERTS = 32
        TOP_K = 8
        THRESHOLD = 0.8
        HIDDEN = 256
        INTER = 96
        B, S, H = hidden_states.shape
        x = hidden_states.reshape(-1, H)
        logits = x @ gate_weight.T
        probs = jax.nn.softmax(logits.astype(jnp.float32), axis=-1).astype(logits.dtype)
        top_vals, top_idx = jax.lax.top_k(probs, TOP_K)
        renorm = top_vals / jnp.clip(jnp.sum(top_vals, axis=-1, keepdims=True), 1e-12)
        cum = jnp.cumsum(renorm, axis=-1)
        num_keep = jnp.minimum(jnp.sum((cum < THRESHOLD).astype(jnp.int32), axis=-1) + 1, TOP_K)
        active = jnp.arange(TOP_K)[None, :] < num_keep[:, None]
        rw = top_vals * active.astype(top_vals.dtype)
        rw = rw / jnp.clip(jnp.sum(rw, axis=-1, keepdims=True), 1e-12)
        combine = jnp.sum(jax.nn.one_hot(top_idx, NUM_EXPERTS, dtype=rw.dtype) * rw[..., None], axis=1)

        def body(acc, params):
            w_gu, w_d, ce = params
            gu = x @ w_gu.T
            g, u = jnp.split(gu, 2, axis=-1)
            h = jax.nn.silu(g) * u
            return (acc + h @ w_d.T * ce[:, None], None)
        out, _ = jax.lax.scan(body, jnp.zeros_like(x), (gate_up_proj, down_proj, combine.T))
        return out.reshape(B, S, H)

    def _L1_xattn_ref(hidden_states, encoder_hidden_states, Wq, Wk, Wv, Wo, gq, gk):
        import jax, jax.numpy as jnp
        import numpy as np
        EPS = 1e-05

        def rmsnorm(x, g, eps=EPS):
            var = jnp.mean(jnp.square(x), axis=-1, keepdims=True)
            return x * jax.lax.rsqrt(var + eps) * g
        B, Sq, _ = hidden_states.shape
        Skv = encoder_hidden_states.shape[1]
        D = gq.shape[0]
        H = Wq.shape[1] // D
        scale = 1.0 / np.sqrt(D)
        q = (hidden_states @ Wq).reshape(B, Sq, H, D)
        k = (encoder_hidden_states @ Wk).reshape(B, Skv, H, D)
        v = (encoder_hidden_states @ Wv).reshape(B, Skv, H, D)
        q = rmsnorm(q, gq)
        k = rmsnorm(k, gk)
        scores = jnp.einsum('bqhd,bkhd->bhqk', q, k) * scale
        attn = jax.nn.softmax(scores, axis=-1)
        out = jnp.einsum('bhqk,bkhd->bqhd', attn, v)
        out = out.reshape(B, Sq, H * D)
        return out @ Wo

    def _L1_ffn_ref(x, gate_w, up_w, down_w, gate_s, up_s, down_s):
        import jax, jax.numpy as jnp
        import numpy as np
        HIDDEN = 256
        INTER = 704
        B, S = (2, 256)

        def _ternary(key, shape):
            return jax.random.randint(key, shape, -1, 2).astype(jnp.float32)
        b, s, h = x.shape
        xf = x.reshape(b * s, h)
        g = jnp.einsum('th,ih->ti', xf, gate_w) * gate_s
        u = jnp.einsum('th,ih->ti', xf, up_w) * up_s
        hdn = jax.nn.silu(g) * u
        out = jnp.einsum('ti,hi->th', hdn, down_w) * down_s
        return out.reshape(b, s, -1)
    x = x + jnp.tanh(g_xattn[0]) * _L0_xattn_ref(_layernorm(x, axis=-1), ctx_1024, L0_xattn_Wq, L0_xattn_bq, L0_xattn_Wk, L0_xattn_bk)
    x = x + jnp.tanh(g_ffn[0]) * _L0_ffn_ref(_layernorm(x, axis=-1), L0_ffn_gate_weight, L0_ffn_gate_up_proj, L0_ffn_down_proj)
    x = x + jnp.tanh(g_xattn[1]) * _L1_xattn_ref(_layernorm(x, axis=-1), ctx_1024, L1_xattn_Wq, L1_xattn_Wk, L1_xattn_Wv, L1_xattn_Wo, L1_xattn_gq, L1_xattn_gk)
    x = x + jnp.tanh(g_ffn[1]) * _L1_ffn_ref(_layernorm(x, axis=-1), L1_ffn_gate_w, L1_ffn_up_w, L1_ffn_down_w, L1_ffn_gate_s, L1_ffn_up_s, L1_ffn_down_s)
    return x

_drawn_inputs = setup_inputs


def setup_inputs(seed=0):
    import zlib

    import numpy as np

    out = dict(_drawn_inputs(seed))
    spreads = {'g_ffn': (-1.0, 0.6),
     'L0_xattn_bq': (0.0, 0.1),
     'L0_xattn_bk': (0.0, 2.0),
     'L1_xattn_gq': (1.0, 0.6),
     'L1_xattn_gk': (1.0, 0.535)}
    factors = {'L0_ffn_gate_weight': 8.0, 'L0_ffn_gate_up_proj': 8.0, 'L0_ffn_down_proj': 8.0}
    for name, (base, spread) in spreads.items():
        noise = np.random.default_rng([zlib.crc32(name.encode()), seed]).standard_normal(out[name].shape)
        drawn = base * np.exp(spread * noise) if base else spread * noise
        out[name] = jnp.asarray(drawn.astype(out[name].dtype))
    for name, factor in factors.items():
        out[name] = (out[name] * factor).astype(out[name].dtype)
    return out
```

```python
from contextlib import ExitStack

import concourse.bass as bass
from concourse import mybir

P = 128
BATCH, SEQ, DIM, CDIM = 4, 256, 256, 128
TOK = BATCH * SEQ
TILES = TOK // P
HALF = 512
HTILES = HALF // P
KT = DIM // P
OT_ = DIM // P
EXPERTS, TOPK, INTER = 32, 8, 96
THRESHOLD = 0.8
GROUP = 4
GROUPS = EXPERTS // GROUP
PARTS = INTER // 32
MW = 3 * DIM
HEADS, HD = 16, 128
FF = 704
FFT = FF // P
FFR = FF - FFT * P
EPS = 1e-5

F32 = mybir.dt.float32
F32R = mybir.dt.float32r
BF16 = mybir.dt.bfloat16
U32 = mybir.dt.uint32
ALU = mybir.AluOpType
ACT = mybir.ActivationFunctionType
AX = mybir.AxisListType

BQ, BK, GQ, GK, DS, GS = 0, 1, 2, 3, 4, 6
US = GS + FFT
TAIL = US + FFT
NCOLS = TAIL + 1


class Signal:

    def __init__(self, sem):
        self.sem, self.n = sem, 0

    def on(self, ins, by=1):
        ins.then_inc(self.sem, by)
        self.n += by
        return self.n


def flamingo(nc, x_d, ctxn_d, ctxT_d, w0_d, cols_d, tailg_d, tailu_d, gates_d, gw_d, moe_d,
             wq_d, wk_d, wv_d, wo_d, w13_d, w2_d, w2t_d, out_d, comb_d):
    ctx = ExitStack()
    with ctx:
        base = (nc.sbuf_base + 31) // 32 * 32
        top = [0]

        def place(name, shape, dt=F32, at=None):
            size = 4 if dt != BF16 else 2
            for s in shape[1:]:
                size *= s
            size = (size + 31) // 32 * 32
            off = top[0] if at is None else at
            if at is None:
                top[0] += size
            ends[name] = off + size
            assert base + off + size <= nc.sbuf_usable_end, (name, off + size)
            return nc.alloc_sbuf_tensor_at(name, list(shape), dt, offset=base + off)

        ends = {}

        def sem(name):
            return ctx.enter_context(nc.semaphore(name))

        bank = [ctx.enter_context(nc.psum_tensor(f"bank{i}", [P, 512], F32)) for i in range(8)]
        x = place("x", [P, TILES, DIM])
        lnat = top[0]
        xln = place("xln", [P, TILES, DIM])
        OT = [place(f"OT{h}", [P, OT_, HALF], at=lnat + h * 4096) for h in range(2)]
        XThi = place("XThi", [P, KT, TOK], F32R)
        XTlo = place("XTlo", [P, KT, TOK], F32R)
        ctxn = place("ctxn", [P, TILES, CDIM])
        krat = top[0]
        kraw = place("kraw", [P, TILES, HEADS * HD])
        phat = top[0]
        PHhi = place("PHhi", [P, HEADS, DIM], F32R)
        PHlo = place("PHlo", [P, HEADS, DIM], F32R)
        cols = place("cols", [P, NCOLS])
        gates = place("gates", [P, 4])
        tg = place("tg", [P, 4])
        ident = place("ident", [P, P])
        mhalf = place("mhalf", [P, TILES])
        gain = place("gain", [P, 1])
        dscale = place("dscale", [P, OT_])
        ones = place("ones", [P, 1])
        stats = place("stats", [P, TILES, 6])
        mv = place("mv", [P, TILES, 2])
        veps = place("veps", [P, TILES])
        rstd = place("rstd", [P, TILES])
        kss = place("kss", [P, TILES, HEADS])
        rk = place("rk", [P, TILES, HEADS])
        asum = place("asum", [P, TILES])
        nmax = place("nmax", [P, TILES])
        rsum = place("rsum", [P, TILES])
        gwraw = place("gwraw", [P, KT, EXPERTS])
        gwhi = place("gwhi", [P, KT, EXPERTS], F32R)
        gwlo = place("gwlo", [P, KT, EXPERTS], F32R)
        zeros = place("zeros", [P, 512], BF16)
        R = top[0]
        q0 = place("q0", [P, TOK], at=phat)
        k0 = place("k0", [P, TOK], at=phat + 4096)
        XT0 = place("XT0", [P, BATCH, 2, SEQ], at=phat + 8192)
        A = place("A", [P, TILES, SEQ], at=phat + 16384)
        AT = place("AT", [P, BATCH, 2, SEQ], at=phat + 24576)
        ctxT = place("ctxT", [P, TOK], at=R)
        w0 = place("w0", [P, 2 * CDIM], at=R + 4096)
        wk = place("wk", [P, HEADS * HD], at=R + 5120)
        wkhi = place("wkhi", [P, HEADS * HD], F32R, at=R + 13312)
        wklo = place("wklo", [P, HEADS * HD], F32R, at=R + 21504)
        ctxThi = place("ctxThi", [P, TOK], F32R, at=R + 29696)
        ctxTlo = place("ctxTlo", [P, TOK], F32R, at=R + 33792)
        E8 = [P, TILES, TOPK]
        eq = place("eq", [P, TILES, EXPERTS, TOPK], at=phat)
        o = phat + 8192
        lg = place("lg", [P, TILES, EXPERTS], at=o)
        comb = place("comb", [P, TILES, EXPERTS], at=o + 1024)
        iota32 = place("iota32", [P, EXPERTS], at=o + 2048)
        iota8 = place("iota8", [P, TOPK], at=o + 2176)
        keep8 = place("keep8", E8, at=o + 2304)
        top8 = place("top8", E8, at=o + 2560)
        idx8 = place("idx8", E8, U32, at=o + 2816)
        idxf = place("idxf", E8, at=o + 3072)
        ren8 = place("ren8", E8, at=o + 3328)
        cum8 = place("cum8", E8, at=o + 3584)
        rw8 = place("rw8", E8, at=o + 3840)
        s8 = place("s8", [P, TILES], at=o + 4096)
        r8 = place("r8", [P, TILES], at=o + 4128)
        combT = place("combT", [EXPERTS, TOK], at=o + 4608)
        CE = place("CE", [P, GROUPS, TOK], at=phat)
        whi = [place(f"whi{t}", [P, MW], F32R, at=R + 3072 * t) for t in range(PARTS)]
        wlo = [place(f"wlo{t}", [P, MW], F32R, at=R + 9216 + 3072 * t) for t in range(PARTS)]
        act = [place(f"act{h}", [P, HALF], at=R + 18432 + 2048 * h) for h in range(2)]
        hid = [place(f"hid{h}", [P, HALF], at=R + 22528 + 2048 * h) for h in range(2)]
        hidhi = [place(f"hidhi{h}", [P, HALF], F32R, at=R + 26624 + 2048 * h) for h in range(2)]
        hidlo = [place(f"hidlo{h}", [P, HALF], F32R, at=R + 30720 + 2048 * h) for h in range(2)]
        ksq = place("ksq", [P, 4 * HD], at=R + 34816)
        wraw = [place(f"wraw{t}", [P, MW], at=R + 37888 + 3072 * t) for t in range(PARTS)]
        wv = place("wv", [P, HEADS, CDIM], at=R + 47104)
        wo = place("wo", [P, HEADS, DIM], at=R + 55296)
        a3 = [R]

        def put3(name, shape, dt=F32):
            t = place(name, shape, dt, at=a3[0])
            a3[0] = ends[name]
            return t
        ctxhi = put3("ctxhi", [P, TILES, CDIM], F32R)
        ctxlo = put3("ctxlo", [P, TILES, CDIM], F32R)
        qhi = put3("qhi", [P, HALF], F32R)
        qlo = put3("qlo", [P, HALF], F32R)
        qsq = put3("qsq", [P, HALF])
        kn = put3("kn", [P, HTILES, HD])
        khi = put3("khi", [P, HALF], F32R)
        klo = put3("klo", [P, HALF], F32R)
        Pm = put3("Pm", [P, 2, 2, SEQ])
        PThi = put3("PThi", [P, 2, 2, SEQ], F32R)
        PTlo = put3("PTlo", [P, 2, 2, SEQ], F32R)
        ohi = put3("ohi", [P, HALF], F32R)
        olo = put3("olo", [P, HALF], F32R)
        wqraw = put3("wqraw", [P, KT * HD])
        wqhi = put3("wqhi", [P, KT, HD], F32R)
        wqlo = put3("wqlo", [P, KT, HD], F32R)
        phhi = put3("phhi", [P, DIM], F32R)
        phlo = put3("phlo", [P, DIM], F32R)
        qss = put3("qss", [P, HTILES])
        qsc = put3("qsc", [P, HTILES])
        smax = put3("smax", [P, 2, 2])
        nbias = put3("nbias", [P, 2, 2])
        psumr = put3("psumr", [P, 2, 2])
        prec = put3("prec", [P, 2, 2])
        assert a3[0] <= R + 46000, a3[0] - R
        w13 = place("w13", [P, 2 * FFT + 1, KT, P], at=R + 47104)
        w2 = place("w2", [P, FFT + 1, DIM], at=R + 47104 + 11264)
        w13hi = place("w13hi", [P, 2 * FFT + 1, KT, P], F32R, at=krat)
        w13lo = place("w13lo", [P, 2 * FFT + 1, KT, P], F32R, at=krat + 11264)
        w2hi = place("w2hi", [P, FFT + 1, DIM], F32R, at=krat + 22528)
        w2lo = place("w2lo", [P, FFT + 1, DIM], F32R, at=krat + 28672)

        S = {}

        def signal(name):
            if name not in S:
                S[name] = Signal(sem(name))
            return S[name]

        NIT = GROUPS * PARTS
        ld_small, ld_ctxT, ld_x, ld_ctxn, ld_k, ld_gw, ld_v, ld_ff = [
            sem(n) for n in ("ld_small", "ld_ctxT", "ld_x", "ld_ctxn", "ld_k", "ld_gw", "ld_v", "ld_ff")]
        const = sem("const")
        proj = sem("proj"); q0_out = sem("q0_out"); k0_out = sem("k0_out"); energy = sem("energy")
        a_max = sem("a_max"); a_exp = sem("a_exp"); a_norm = sem("a_norm"); tgr = sem("tgr")
        xt0_tr = sem("xt0_tr"); xt0_out = sem("xt0_out"); at_tr = sem("at_tr"); at_out = sem("at_out")
        mix = sem("mix")
        ln_var = sem("ln_var"); ln_rstd = sem("ln_rstd"); ln_out = sem("ln_out")
        xt_tr = sem("xt_tr"); xt_hi = sem("xt_hi"); xt_lo = sem("xt_lo"); x_new = sem("x_new")
        ot_a = sem("ot_a"); ot_v = sem("ot_v"); ot_tr = sem("ot_tr")
        vch = sem("vch")
        pch = sem("pch")
        csp_a = sem("csp_a"); csp_p = sem("csp_p"); kmm = sem("kmm"); k_out = sem("k_out")
        gws = sem("gws"); logits = sem("logits"); lg_sub = sem("lg_sub"); lg_exp = sem("lg_exp")
        comb_ok = sem("comb_ok"); comb_tr = sem("comb_tr"); combT_out = sem("combT_out")
        comb_st = sem("comb_st"); ce_ld = sem("ce_ld")
        w_ld = [sem(f"w_ld{t}") for t in range(PARTS)]
        w_hi = sem("w_hi"); w_lo = sem("w_lo")
        g_mm = sem("g_mm"); u_mm = sem("u_mm"); silu = sem("silu"); weighted = sem("weighted")
        h_ok = sem("h_ok"); h_hi = sem("h_hi"); h_lo = sem("h_lo"); down = sem("down")
        sq_ok = sem("sq_ok"); sq_sum = sem("sq_sum"); rk_ok = sem("rk_ok")
        pmm = sem("pmm"); p_hi = sem("p_hi"); p_lo = sem("p_lo")
        csp = sem("csp"); wq_ld = sem("wq_ld"); wq_h = sem("wq_h"); wq_s = sem("wq_s"); ph_ld = sem("ph_ld")
        kn_ok = sem("kn_ok"); kt_tr = sem("kt_tr"); k_hi = sem("k_hi"); k_lo = sem("k_lo")
        q_mm = sem("q_mm"); q_hi = sem("q_hi"); q_lo = sem("q_lo"); q_sq = sem("q_sq")
        q_ss = sem("q_ss"); q_ssout = sem("q_ssout"); q_sc = sem("q_sc")
        s_mm = sem("s_mm"); s_max = sem("s_max"); s_bias = sem("s_bias"); s_exp = sem("s_exp")
        s_rec = sem("s_rec"); s_norm = sem("s_norm"); pt_tr = sem("pt_tr"); pt_hi = sem("pt_hi")
        pt_lo = sem("pt_lo"); av = sem("av"); o_hi = sem("o_hi"); o_lo = sem("o_lo"); omm = sem("omm")
        fsp = sem("fsp"); f_g = sem("f_g"); f_u = sem("f_u"); f_silu = sem("f_silu"); f_h = sem("f_h")
        f_hi = sem("f_hi"); f_lo = sem("f_lo"); f_down = sem("f_down"); st_out = sem("st_out")

        def f32(ap):
            return ap.bitcast(F32)

        def three(mm, out, whi_, wlo_, mhi, mlo, start, stop):
            mm(out, wlo_, mhi, start=start, stop=False, skip_group_check=True)
            mm(out, whi_, mhi, start=False, stop=False, skip_group_check=True)
            return mm(out, whi_, mlo, start=False, stop=stop, skip_group_check=True)

        def apart(engine, sem_, value):
            engine.wait_ge(sem_, value)

        def tile_cols(i, n=P):
            return slice(i * n, (i + 1) * n)

        block = ctx.enter_context(nc.Block())

        @block.sync
        def _(sp):
            sp.dma_start(ctxT[:], ctxT_d).then_inc(ld_ctxT, 16)
            sp.dma_start(w0[:], w0_d).then_inc(ld_ctxT, 16)
            sp.dma_start(cols[:, 0:TAIL], cols_d).then_inc(ld_small, 16)
            sp.dma_start(cols[0:FFR, TAIL:NCOLS], tailg_d).then_inc(ld_small, 16)
            sp.dma_start(cols[FFR:2 * FFR, TAIL:NCOLS], tailu_d).then_inc(ld_small, 16)
            sp.dma_start(gates[:], gates_d.partition_broadcast(P)).then_inc(ld_small, 16)
            sp.dma_start(x[:], x_d.rearrange("(t p) d -> p t d", p=P)).then_inc(ld_x, 16)
            sp.dma_start(wk[:], wk_d).then_inc(ld_k, 16)
            sp.dma_start(gwraw[:], gw_d.rearrange("(k p) e -> p k e", p=P)).then_inc(ld_gw, 16)
            sp.dma_start(ctxn[:], ctxn_d.rearrange("(t p) d -> p t d", p=P)).then_inc(ld_ctxn, 16)

            def load_expert_tile(m, t, first):
                if not first:
                    apart(sp, ld_x, 16)
                    sp.wait_ge(w_lo, (m - 1) * PARTS + t + 1)
                sp.dma_start(wraw[t][:], moe_d[bass.ts(m * PARTS + t, P), :]).then_inc(w_ld[t], 16)

            for t in range(PARTS):
                load_expert_tile(0, t, True)
            sp.dma_start(wv[:].rearrange("p h c -> p (h c)"), wv_d).then_inc(ld_v, 16)
            sp.dma_start(wo[:].rearrange("p h c -> p (h c)"), wo_d).then_inc(ld_v, 16)
            sp.wait_ge(combT_out, 2)
            sp.dma_start(comb_d, combT[:]).then_inc(comb_st, 16)
            sp.wait_ge(comb_st, 16)
            for m in range(GROUPS):
                src = comb_d[m * GROUP:(m + 1) * GROUP, :].unsqueeze(1).broadcast_to([GROUP, 32, TOK])
                sp.dma_start(CE[:, m, :], src).then_inc(ce_ld, 16)
            with sp.Fori(1, GROUPS) as m:
                for t in range(PARTS):
                    load_expert_tile(m, t, False)

            def load_wq(N, n):
                if N is not None:
                    apart(sp, ld_x, 16)
                    sp.wait_ge(wq_s, N)
                sp.dma_start(wqraw[:], wq_d[:, bass.ts(n, KT * HD)]).then_inc(wq_ld, 16)

            def load_ph(N, n):
                if N is not None:
                    apart(sp, ld_x, 16)
                    sp.wait_ge(omm, N)
                for dst, src in ((phhi, PHhi), (phlo, PHlo)):
                    sp.dma_start(f32(dst[:]), f32(src[:].rearrange("p h o -> p (h o)")[:, bass.ts(n, DIM)])).then_inc(ph_ld, 16)

            sp.wait_ge(down, 2 * NIT)
            load_wq(None, 0)
            sp.wait_ge(p_hi, 8)
            sp.wait_ge(p_lo, 8)
            load_ph(None, 0)
            sp.dma_start(w13[:].rearrange("p a b c -> p (a b c)"), w13_d).then_inc(ld_ff, 16)
            sp.dma_start(w2[:, 0:FFT, :].rearrange("p a b -> p (a b)"), w2_d).then_inc(ld_ff, 16)
            sp.dma_start(w2[FFR:2 * FFR, FFT, :], w2t_d).then_inc(ld_ff, 16)
            load_wq(1, 1)
            load_wq(2, 2)
            with sp.Fori(1, HEADS - 2) as n:
                load_wq(n + 2, n + 2)
                load_ph(n, n)
            for N in range(HEADS - 2, HEADS + 1):
                load_wq(N + 2, (N + 2) % HEADS)
                load_ph(N, N % HEADS)
            with sp.Fori(1, HEADS - 2) as n:
                load_wq(n + HEADS + 2, n + 2)
                load_ph(n + HEADS, n)
            for n in range(HEADS - 2, HEADS):
                load_ph(n + HEADS, n)
            for i in range(4):
                sp.wait_ge(x_new, 4 * 3 + i + 1)
                sp.dma_start(out_d.rearrange("(t p) d -> p t d", p=P)[:, 2 * i:2 * i + 2, :],
                             x[:, 2 * i:2 * i + 2, :]).then_inc(st_out, 16)
            sp.wait_ge(st_out, 64)

        @block.gpsimd
        def _(pool):
            nc.gpsimd.memset(ident[:], 0.0).then_inc(pch, 1)
            nc.gpsimd.memset(mhalf[:], -0.5).then_inc(const, 1)
            nc.gpsimd.memset(ones[:], 1.0).then_inc(const, 1)
            pool.wait_ge(pch, 1)
            nc.gpsimd.affine_select(out=ident[:], in_=ident[:], compare_op=ALU.not_equal, fill=1.0, base=0,
                                    pattern=[[-1, P]], channel_multiplier=1).then_inc(const, 1)
            pool.wait_ge(csp_a, 1)
            nc.gpsimd.tensor_tensor(ctxTlo[:], ctxT[:], f32(ctxThi[:]), ALU.subtract).then_inc(csp_p, 1)
            pool.wait_ge(csp_a, 2)
            nc.gpsimd.tensor_tensor(wklo[:], wk[:], f32(wkhi[:]), ALU.subtract).then_inc(csp_p, 1)
            ch = [1]

            def rstd_of(group):
                k, tt = group
                pool.wait_ge(ln_var, k + 1)
                nc.gpsimd.tensor_scalar(veps[:, tt:tt + 2], mv[:, tt:tt + 2, 1], EPS, 1.0, ALU.add, ALU.mult).then_inc(pch, 1)
                ch[0] += 1
                pool.wait_ge(pch, ch[0])
                nc.gpsimd.tensor_tensor(rstd[:, tt:tt + 2], veps[:, tt:tt + 2], mhalf[:, 0:2], ALU.pow).then_inc(ln_rstd, 1)

            for b in range(BATCH):
                rstd_of((b, 2 * b))
            for b in range(BATCH):
                rstd_of((4 + b, 2 * b))

            def hidden_low(n2, h):
                pool.wait_ge(h_hi, n2 + 1)
                nc.gpsimd.tensor_tensor(hidlo[h][:], hid[h][:], f32(hidhi[h][:]), ALU.subtract).then_inc(h_lo, 1)

            def split_low(it, t):
                pool.wait_ge(w_hi, it + 1)
                nc.gpsimd.tensor_tensor(wlo[t][:], wraw[t][:], f32(whi[t][:]), ALU.subtract).then_inc(w_lo, 1)

            def moe_pool(m, first=False, last=False):
                for t in range(PARTS):
                    it = m * PARTS + t
                    if not (first and t == 0):
                        hidden_low(it * 2 - 1, 1)
                    hidden_low(it * 2, 0)
                    if not (last and t > 0):
                        split_low(it + 2, (t + 2) % PARTS)
                    for c in ([t] if t < PARTS - 1 else [t, t + 1]):
                        if not (first and t == 0):
                            pool.wait_ge(sq_sum, m * 4 + c)
                        kv = kraw[:, bass.ds(m, 1), c * 512:(c + 1) * 512].rearrange("p a b -> p (a b)")
                        nc.gpsimd.tensor_tensor(ksq[:], kv, kv, ALU.mult).then_inc(sq_ok, 1)

            for t in range(2):
                split_low(t, t)
            pool.wait_ge(k_out, 32)
            moe_pool(0, first=True)
            with pool.Fori(1, GROUPS - 1) as m:
                moe_pool(m)
            moe_pool(GROUPS - 1, last=True)
            hidden_low(2 * NIT - 1, 1)
            pool.wait_ge(sq_sum, 4 * TILES)
            nc.gpsimd.tensor_scalar(kss[:], kss[:], 1.0 / HD, EPS, ALU.mult, ALU.add).then_inc(pch, 1)
            ch[0] += 1
            pool.wait_ge(pch, ch[0])
            nc.gpsimd.tensor_tensor(rk[:].rearrange("p t h -> p (t h)"), kss[:].rearrange("p t h -> p (t h)"),
                                    mhalf[:, 0:1].broadcast_to([P, TILES * HEADS]), ALU.pow).then_inc(pch, 1)
            ch[0] += 1
            pool.wait_ge(pch, ch[0])
            pool.wait_ge(csp, 1)
            nc.gpsimd.tensor_tensor(ctxlo[:], ctxn[:], f32(ctxhi[:]), ALU.subtract).then_inc(csp, 1)
            for b in range(BATCH):
                rstd_of((8 + b, 2 * b))

            def norm_keys(H, n, N):
                nc.gpsimd.tensor_tensor(
                    kn[:], kraw[:, H * HTILES:(H + 1) * HTILES, bass.ts(n, HD)],
                    rk[:, H * HTILES:(H + 1) * HTILES, bass.ds(n, 1)].broadcast_to([P, HTILES, HD]),
                    ALU.mult).then_inc(kn_ok, 1)

            def query_scale(N):
                if not (isinstance(N, int) and N == 0):
                    pool.wait_ge(s_exp, 4 * N)
                pool.wait_ge(q_ssout, N + 1)
                nc.gpsimd.tensor_tensor(qsc[:], qss[:], mhalf[:, 0:HTILES], ALU.pow).then_inc(q_sc, 1)

            for H in range(2):
                N0 = H * HEADS
                if H:
                    pool.wait_ge(kt_tr, N0)
                norm_keys(H, 0, N0)
                query_scale(N0)
                pool.wait_ge(kt_tr, N0 + 1)
                norm_keys(H, 1, N0 + 1)
                with pool.Fori(0, HEADS - 2) as n:
                    query_scale(n + N0 + 1)
                    pool.wait_ge(kt_tr, n + N0 + 2)
                    norm_keys(H, n + 2, n + N0 + 2)
                query_scale(N0 + HEADS - 1)
            for b in range(BATCH):
                rstd_of((12 + b, 2 * b))

        @block.scalar
        def _(s):
            act_ = nc.scalar.activation
            s.wait_ge(ld_ctxT, 32)
            act_(ctxThi[:], ctxT[:], ACT.Copy).then_inc(csp_a, 1)
            s.wait_ge(ld_small, 64)
            for h in range(2):
                s.wait_ge(proj, h + 1)
                act_(q0[:, tile_cols(h, HALF)], bank[h][:], ACT.Identity, bias=cols[:, BQ:BQ + 1]).then_inc(q0_out, 1)
            act_(tg[:], gates[:], ACT.Tanh).then_inc(tgr, 1)
            for b in range(BATCH):
                s.wait_ge(a_max, b + 1)
                for i in range(2):
                    tt = 2 * b + i
                    act_(A[:, tt, :], bank[4 + b][:, tile_cols(i, SEQ)], ACT.Exp, bias=nmax[:, tt:tt + 1],
                         accum_out=asum[:, tt:tt + 1]).then_inc(a_exp, 1)
                if b == 0:
                    s.wait_ge(ld_k, 16)
                    act_(wkhi[:], wk[:], ACT.Copy).then_inc(csp_a, 1)
            for b in range(BATCH):
                s.wait_ge(at_tr, b + 1)
                act_(AT[:, b].rearrange("p a b -> p (a b)"), bank[b][:], ACT.Copy).then_inc(at_out, 1)

            def key_chunk(ck):
                for tt in range(TILES):
                    s.wait_ge(kmm, ck * TILES + tt + 1)
                    act_(kraw[:, tt, bass.ts(ck, 512)], bank[4 + tt % 4][:], ACT.Copy).then_inc(k_out, 1)

            def xt_high(k, banks, half):
                for kt in range(KT):
                    s.wait_ge(xt_tr, 2 * k + kt + 1)
                    act_(XThi[:, kt, tile_cols(half, HALF)], bank[banks[kt]][:], ACT.Copy).then_inc(xt_hi, 1)

            with s.Fori(0, 2) as ck:
                key_chunk(ck)
            xt_high(0, (0, 1), 0)
            xt_high(1, (2, 3), 1)
            s.wait_ge(lg_sub, 1)
            act_(lg[:], lg[:], ACT.Exp).then_inc(lg_exp, 1)
            with s.Fori(2, 4) as ck:
                key_chunk(ck)

            def moe_act(m, first=False):
                for t in range(PARTS):
                    for h in range(2):
                        n2 = (m * PARTS + t) * 2 + h
                        s.wait_ge(g_mm, n2 + 1)
                        if not (first and t == 0):
                            s.wait_ge(h_ok, n2 - 1)
                        act_(act[h][:], bank[4 + 2 * h][:], ACT.Silu).then_inc(silu, 1)
                        if first and t == 0 and h == 1:
                            for hh in range(2):
                                s.wait_ge(comb_tr, hh + 1)
                                act_(combT[:, tile_cols(hh, HALF)], bank[1 + hh][0:EXPERTS, :], ACT.Copy).then_inc(combT_out, 1)
                        if not (first and t == 0 and h == 0):
                            split_hidden(n2 - 1, 1 - h, first and n2 <= 2)

            def split_hidden(n2, h, first):
                s.wait_ge(h_ok, n2 + 1)
                if not first:
                    s.wait_ge(down, n2 - 1)
                act_(hidhi[h][:], hid[h][:], ACT.Copy).then_inc(h_hi, 1)

            moe_act(0, first=True)
            with s.Fori(1, GROUPS) as m:
                moe_act(m)
            split_hidden(2 * NIT - 1, 1, False)

            def block_end(k, acc, scale):
                act_(OT[k % 2][:, 0, :], bank[acc][:], ACT.Copy, scale=scale).then_inc(ot_a, 1)

            for h in range(2):
                s.wait_ge(down, 2 * NIT - 1 + h)
                block_end(h, h, tg[:, 1:2])
            act_(ctxhi[:], ctxn[:], ACT.Copy).then_inc(csp, 1)

            def head_products_high(js):
                for j in js:
                    s.wait_ge(pmm, j + 1)
                    act_(PHhi[:, 2 * j:2 * j + 2, :].rearrange("p a b -> p (a b)"), bank[j % 4][:], ACT.Copy).then_inc(p_hi, 1)

            head_products_high(range(4))
            xt_high(2, (4, 5), 0)
            head_products_high(range(4, 8))
            xt_high(3, (6, 7), 1)

            def keys_high(N):
                s.wait_ge(kt_tr, N + 1)
                act_(khi[:], bank[3][:], ACT.Copy, scale=gain[:, 0:1]).then_inc(k_hi, 1)

            def query_high(N):
                s.wait_ge(q_mm, N + 1)
                act_(qhi[:], bank[2][:], ACT.Copy).then_inc(q_hi, 1)
                act_(qsq[:], bank[2][:], ACT.Square).then_inc(q_sq, 1)

            def softmax_exp(N, b):
                s.wait_ge(s_bias, 2 * N + b + 1)
                if not (isinstance(N, int) and N == 0):
                    s.wait_ge(pt_tr, 2 * N - 1 + b)
                for i in range(2):
                    act_(Pm[:, b, i, :], bank[4 + b][:, tile_cols(i, SEQ)], ACT.Exp, bias=nbias[:, b, i:i + 1],
                         scale=qsc[:, 2 * b + i:2 * b + i + 1], accum_out=psumr[:, b, i:i + 1]).then_inc(s_exp, 1)

            def probs_high(N, b):
                s.wait_ge(pt_tr, 2 * N + b + 1)
                act_(PThi[:, b].rearrange("p a b -> p (a b)"), bank[6 + b][:], ACT.Copy).then_inc(pt_hi, 1)

            def out_high(N):
                s.wait_ge(av, N + 1)
                act_(ohi[:], bank[3][:], ACT.Copy).then_inc(o_hi, 1)

            def head_act(N, first=False, last=False):
                if not last:
                    keys_high(N + 1)
                softmax_exp(N, 0)
                if not last:
                    query_high(N + 1)
                softmax_exp(N, 1)
                if not first:
                    out_high(N - 1)
                for b in range(2):
                    probs_high(N, b)

            for H in range(2):
                N0 = H * HEADS
                keys_high(N0)
                query_high(N0)
                head_act(N0, first=True)
                with s.Fori(1, HEADS - 1) as n:
                    head_act(n + N0)
                head_act(N0 + HEADS - 1, last=True)
                out_high(N0 + HEADS - 1)
                s.wait_ge(omm, N0 + HEADS)
                block_end(2 + H, 0, tg[:, 2:3])

            def ff_act(H, i):
                k = H * (FFT + 1) + i
                G, U = 4 + 2 * (i % 2), 5 + 2 * (i % 2)
                s.wait_ge(f_g, k + 1)
                if k >= 2:
                    s.wait_ge(f_h, k - 1)
                if i < FFT:
                    act_(act[i % 2][:], bank[G][:], ACT.Silu, scale=cols[:, GS + i:GS + i + 1]).then_inc(f_silu, 1)
                else:
                    act_(act[i % 2][FFR:2 * FFR, :], bank[G][0:FFR, :], ACT.Silu,
                         scale=cols[0:FFR, TAIL:NCOLS]).then_inc(f_silu, 1)

            def ff_high(H, i):
                k = H * (FFT + 1) + i
                s.wait_ge(f_h, k + 1)
                if k >= 2:
                    s.wait_ge(f_down, k - 1)
                r = slice(0, P) if i < FFT else slice(FFR, 2 * FFR)
                act_(hidhi[i % 2][r, :], hid[i % 2][r, :], ACT.Copy).then_inc(f_hi, 1)

            act_(w13hi[:], w13[:], ACT.Copy).then_inc(fsp, 1)
            xt_high(4, (2, 3), 0)
            for H in range(2):
                for i in range(FFT + 1):
                    ff_act(H, i)
                    ff_high(H, i)
                    if H == 0 and i == 3:
                        xt_high(5, (2, 3), 1)
                s.wait_ge(f_down, (H + 1) * (FFT + 1))
                block_end(4 + H, 0, dscale[:, 0:1])

        @block.vector
        def _(v):
            V = nc.vector
            ch = [0]

            def step(ins):
                ins.then_inc(vch, 1)
                ch[0] += 1

            def settle():
                v.wait_ge(vch, ch[0])

            lnk = [0]

            def ln_stats(tt):
                for t in (tt, tt + 1):
                    step(V.bn_stats(stats[:, t, :], x[:, t, :]))
                settle()
                V.bn_aggr(mv[:, tt, :], stats[:, tt, :]).then_inc(vch, 1)
                V.bn_aggr(mv[:, tt + 1, :], stats[:, tt + 1, :]).then_inc(ln_var, 1)
                ch[0] += 1
                settle()

            def ln_apply(k, tt):
                v.wait_ge(ln_rstd, k + 1)
                for t in (tt, tt + 1):
                    V.tensor_scalar(xln[:, t, :], x[:, t, :], mv[:, t, 0:1], rstd[:, t:t + 1],
                                    ALU.subtract, ALU.mult).then_inc(ln_out, 1)

            def xt_low(k, banks, half):
                for kt in range(KT):
                    v.wait_ge(xt_hi, 2 * k + kt + 1)
                    c = tile_cols(half, HALF)
                    V.tensor_tensor(XTlo[:, kt, c], bank[banks[kt]][:], f32(XThi[:, kt, c]), ALU.subtract).then_inc(xt_lo, 1)

            v.wait_ge(ld_small, 64)
            step(V.tensor_tensor(gain[:], cols[:, GQ:GQ + 1], cols[:, GK:GK + 1], ALU.mult))
            for h in range(2):
                v.wait_ge(proj, 3 + h)
                V.tensor_scalar(k0[:, tile_cols(h, HALF)], bank[2 + h][:], cols[:, BK:BK + 1], None, ALU.add).then_inc(k0_out, 1)
            v.wait_ge(ld_x, 16)
            ln_stats(0)
            for b in range(BATCH):
                v.wait_ge(energy, b + 1)
                V.tensor_reduce(nmax[:, 2 * b:2 * b + 2], bank[4 + b][:].rearrange("p (i m) -> p i m", i=2), AX.X, ALU.max,
                                negate=True).then_inc(a_max, 1)
                if b:
                    ln_stats(2 * b)
            for b in range(BATCH):
                ln_apply(b, 2 * b)
            for b in range(BATCH):
                v.wait_ge(a_exp, 2 * b + 2)
                step(V.reciprocal(rsum[:, 2 * b:2 * b + 2], asum[:, 2 * b:2 * b + 2]))
                settle()
                for i in range(2):
                    tt = 2 * b + i
                    V.tensor_scalar(A[:, tt, :], A[:, tt, :], rsum[:, tt:tt + 1], None, ALU.mult).then_inc(a_norm, 1)
                v.wait_ge(xt0_tr, b + 1)
                V.tensor_copy(XT0[:, b].rearrange("p a b -> p (a b)"), bank[4 + b][:]).then_inc(xt0_out, 1)
            v.wait_ge(tgr, 1)
            V.tensor_scalar(dscale[:], cols[:, DS:DS + 2], tg[:, 3:4], None, ALU.mult).then_inc(vch, 1)
            ch[0] += 1
            for b in range(BATCH):
                v.wait_ge(mix, b + 1)
                xb = x[:, 2 * b:2 * b + 2, :].rearrange("p a b -> p (a b)")
                V.scalar_tensor_tensor(out=xb, in0=bank[b][:], scalar=tg[:, 0:1], in1=xb, op0=ALU.mult,
                                       op1=ALU.add).then_inc(x_new, 1)
                v.wait_ge(x_new, b + 1)
                ln_stats(2 * b)
                if b:
                    ln_apply(4 + b - 1, 2 * b - 2)
            ln_apply(7, 6)
            v.wait_ge(ld_gw, 16)
            step(V.tensor_copy(gwhi[:], gwraw[:]))
            settle()
            V.tensor_tensor(gwlo[:], gwraw[:], f32(gwhi[:]), ALU.subtract).then_inc(gws, 1)
            xt_low(0, (0, 1), 0)
            xt_low(1, (2, 3), 1)

            def bc(ap, shape):
                return ap.unsqueeze(2).broadcast_to(shape)

            v.wait_ge(logits, TILES)
            step(V.tensor_copy(lg[:].rearrange("p a b -> p (a b)"), bank[0][:, 0:TILES * EXPERTS]))
            settle()
            step(V.tensor_reduce(s8[:], lg[:], AX.X, ALU.max))
            settle()
            V.tensor_tensor(lg[:], lg[:], bc(s8[:], [P, TILES, EXPERTS]), ALU.subtract).then_inc(lg_sub, 1)
            step(V.memset(keep8[:], 1.0))
            step(V.memset(iota32[:], 1.0))
            settle()
            step(V.memset(keep8[:, :, 0:1], 0.0))
            step(V.tensor_tensor_scan(iota32[:], iota32[:], iota32[:], -1.0, ALU.mult, ALU.add))
            settle()
            v.wait_ge(lg_exp, 1)
            step(V.tensor_reduce(s8[:], lg[:], AX.X, ALU.add))
            settle()
            step(V.reciprocal(r8[:], s8[:]))
            settle()
            step(V.tensor_tensor(lg[:], lg[:], bc(r8[:], [P, TILES, EXPERTS]), ALU.mult))
            settle()
            for tt in range(TILES):
                step(V.max(top8[:, tt, :], lg[:, tt, :]))
            settle()
            for tt in range(TILES):
                step(V.max_index(idx8[:, tt, :], top8[:, tt, :], lg[:, tt, :]))
            step(V.tensor_reduce(s8[:], top8[:], AX.X, ALU.add))
            settle()
            step(V.tensor_scalar(s8[:], s8[:], 1e-12, None, ALU.max))
            step(V.tensor_copy(idxf[:], idx8[:]))
            settle()
            step(V.reciprocal(r8[:], s8[:]))
            settle()
            step(V.tensor_tensor(ren8[:], top8[:], bc(r8[:], E8), ALU.mult))
            settle()
            step(V.tensor_tensor_scan(cum8[:].rearrange("p a b -> p (a b)"), keep8[:].rearrange("p a b -> p (a b)"),
                                      ren8[:].rearrange("p a b -> p (a b)"), 0.0, ALU.mult, ALU.add))
            settle()
            step(V.tensor_scalar(cum8[:], cum8[:], THRESHOLD, None, ALU.is_lt))
            settle()
            step(V.tensor_reduce(s8[:], cum8[:], AX.X, ALU.add))
            settle()
            step(V.tensor_scalar(s8[:], s8[:], 1.0, float(TOPK), ALU.add, ALU.min))
            settle()
            step(V.tensor_tensor(cum8[:], iota32[:, 0:TOPK].unsqueeze(1).broadcast_to(E8), bc(s8[:], E8), ALU.is_lt))
            settle()
            step(V.tensor_tensor(rw8[:], top8[:], cum8[:], ALU.mult))
            settle()
            step(V.tensor_reduce(s8[:], rw8[:], AX.X, ALU.add))
            settle()
            step(V.tensor_scalar(s8[:], s8[:], 1e-12, None, ALU.max))
            settle()
            step(V.reciprocal(r8[:], s8[:]))
            settle()
            step(V.tensor_tensor(rw8[:], rw8[:], bc(r8[:], E8), ALU.mult))
            settle()
            full = [P, TILES, EXPERTS, TOPK]
            step(V.tensor_tensor(eq[:], idxf[:].unsqueeze(2).broadcast_to(full),
                                 iota32[:].unsqueeze(1).unsqueeze(3).broadcast_to(full), ALU.is_equal))
            settle()
            step(V.tensor_tensor(eq[:], eq[:], rw8[:].unsqueeze(2).broadcast_to(full), ALU.mult))
            settle()
            V.tensor_reduce(comb[:], eq[:], AX.X, ALU.add).then_inc(comb_ok, 1)

            def split_high(it, t, m, free):
                v.wait_ge(w_ld[t], 16 * (m + 1))
                if free:
                    v.wait_ge(down, it * 2 - 4)
                V.tensor_copy(whi[t][:], wraw[t][:]).then_inc(w_hi, 1)

            def hidden(m, n2, h, first):
                v.wait_ge(silu, n2 + 1)
                V.tensor_tensor(act[h][:], act[h][:], CE[:, bass.ds(m, 1), tile_cols(h, HALF)].rearrange("p a b -> p (a b)"),
                                ALU.mult).then_inc(weighted, 1)
                v.wait_ge(u_mm, n2 + 1)
                v.wait_ge(weighted, n2 + 1)
                if not first:
                    v.wait_ge(h_lo, n2 - 1)
                V.tensor_tensor(hid[h][:], bank[5 + 2 * h][:], act[h][:], ALU.mult).then_inc(h_ok, 1)

            def moe_vec(m, first=False, last=False):
                for t in range(PARTS):
                    it = m * PARTS + t
                    for h in range(2):
                        hidden(m, it * 2 + h, h, first and t == 0)
                    if not (last and t > 0):
                        nx = t + 2
                        split_high(it + 2, nx % PARTS, m + nx // PARTS, not (first and t == 0))
                    for c in ([t] if t < PARTS - 1 else [t, t + 1]):
                        v.wait_ge(sq_ok, m * 4 + c + 1)
                        V.tensor_reduce(kss[:, bass.ds(m, 1), c * 4:(c + 1) * 4], ksq[:].rearrange("p (h d) -> p h d", d=HD),
                                        AX.X, ALU.add).then_inc(sq_sum, 1)

            v.wait_ge(kmm, 32)
            v.wait_ge(csp_p, 2)
            step(V.memset(zeros[:].bitcast(F32), 0.0))
            settle()
            for t in range(2):
                split_high(t, t, 0, False)
            v.wait_ge(ce_ld, 16 * GROUPS)
            moe_vec(0, first=True)
            with v.Fori(1, GROUPS - 1) as m:
                moe_vec(m)
            moe_vec(GROUPS - 1, last=True)

            def block_end(k, acc, scale):
                V.tensor_scalar(OT[k % 2][:, 1, :], bank[acc][:], scale, None, ALU.mult).then_inc(ot_v, 1)

            def residual(k, banks):
                for i in range(2):
                    tt = (k % 2) * HTILES + 2 * i
                    v.wait_ge(ot_tr, 2 * k + i + 1)
                    xb = x[:, tt:tt + 2, :].rearrange("p a b -> p (a b)")
                    V.tensor_tensor(xb, bank[banks[i]][:], xb, ALU.add).then_inc(x_new, 1)
                    v.wait_ge(x_new, 4 + 2 * k + i + 1)

            def ln_half(k):
                tt = (k % 2) * HTILES
                for i in range(2):
                    ln_stats(tt + 2 * i)
                for i in range(2):
                    ln_apply(2 * k + 4 + i, tt + 2 * i)

            for h in range(2):
                v.wait_ge(down, 2 * NIT - 1 + h)
                block_end(h, 2 + h, tg[:, 1:2])

            def head_products_low(js):
                for j in js:
                    v.wait_ge(p_hi, j + 1)
                    ph = PHhi[:, 2 * j:2 * j + 2, :].rearrange("p a b -> p (a b)")
                    pl = PHlo[:, 2 * j:2 * j + 2, :].rearrange("p a b -> p (a b)")
                    V.tensor_tensor(pl, bank[j % 4][:], f32(ph), ALU.subtract).then_inc(p_lo, 1)

            residual(0, (4, 5))
            ln_half(2)
            head_products_low(range(4))
            xt_low(2, (4, 5), 0)
            residual(1, (6, 7))
            ln_half(3)
            head_products_low(range(4, 8))
            xt_low(3, (6, 7), 1)

            def split_query_weights(N, ld):
                v.wait_ge(wq_ld, ld)
                if not (isinstance(N, int) and N == 0):
                    v.wait_ge(q_mm, N)
                w = wqhi[:].rearrange("p a b -> p (a b)")
                V.tensor_copy(w, wqraw[:]).then_inc(wq_h, 1)
                v.wait_ge(wq_h, N + 1)
                V.tensor_tensor(wqlo[:].rearrange("p a b -> p (a b)"), wqraw[:], f32(w), ALU.subtract).then_inc(wq_s, 1)

            def keys_low(N):
                v.wait_ge(k_hi, N + 1)
                V.scalar_tensor_tensor(out=klo[:], in0=bank[3][:], scalar=gain[:, 0:1], in1=f32(khi[:]),
                                       op0=ALU.mult, op1=ALU.subtract).then_inc(k_lo, 1)

            def query_low(N):
                v.wait_ge(q_sq, N + 1)
                V.tensor_tensor(qlo[:], bank[2][:], f32(qhi[:]), ALU.subtract).then_inc(q_lo, 1)

            def query_squares(N):
                v.wait_ge(q_ss, N + 1)
                V.tensor_scalar(qss[:], bank[2][:, 0:HTILES], HD * EPS, None, ALU.add).then_inc(q_ssout, 1)

            def softmax_bias(N, b):
                v.wait_ge(s_mm, 2 * N + b + 1)
                V.tensor_reduce(smax[:, b, :], bank[4 + b][:].rearrange("p (i m) -> p i m", i=2), AX.X,
                                ALU.max).then_inc(s_max, 1)
                v.wait_ge(s_max, 2 * N + b + 1)
                v.wait_ge(q_sc, N + 1)
                V.scalar_tensor_tensor(out=nbias[:, b, :], in0=smax[:, b, :], scalar=-1.0, in1=qsc[:, 2 * b:2 * b + 2],
                                       op0=ALU.mult, op1=ALU.mult).then_inc(s_bias, 1)

            def softmax_norm(N, b):
                v.wait_ge(s_exp, 4 * N + 2 * b + 2)
                V.reciprocal(prec[:, b, :], psumr[:, b, :]).then_inc(s_rec, 1)
                v.wait_ge(s_rec, 2 * N + b + 1)
                for i in range(2):
                    V.tensor_scalar(Pm[:, b, i, :], Pm[:, b, i, :], prec[:, b, i:i + 1], None, ALU.mult).then_inc(s_norm, 1)

            def probs_low(N, b):
                v.wait_ge(pt_hi, 2 * N + b + 1)
                V.tensor_tensor(PTlo[:, b].rearrange("p a b -> p (a b)"), bank[6 + b][:],
                                f32(PThi[:, b].rearrange("p a b -> p (a b)")), ALU.subtract).then_inc(pt_lo, 1)

            def out_low(N):
                v.wait_ge(o_hi, N + 1)
                V.tensor_tensor(olo[:], bank[3][:], f32(ohi[:]), ALU.subtract).then_inc(o_lo, 1)

            def head_vec(N, first=False, last=False, ld=None):
                softmax_bias(N, 0)
                softmax_bias(N, 1)
                if not last:
                    keys_low(N + 1)
                softmax_norm(N, 0)
                if not last:
                    query_low(N + 1)
                if ld is not None:
                    split_query_weights(N + 2, ld)
                softmax_norm(N, 1)
                if not first:
                    out_low(N - 1)
                if not last:
                    query_squares(N + 1)
                for b in range(2):
                    probs_low(N, b)

            for H in range(2):
                N0 = H * HEADS
                if H == 0:
                    split_query_weights(0, 16)
                keys_low(N0)
                query_low(N0)
                split_query_weights(N0 + 1, 16 * (N0 + 2))
                query_squares(N0)
                head_vec(N0, first=True, ld=16 * (N0 + 3))
                with v.Fori(1, HEADS - 2) as n:
                    head_vec(n + N0, ld=16 * (n + N0 + 3))
                head_vec(N0 + HEADS - 2, ld=16 * (N0 + HEADS + 1) if H == 0 else None)
                head_vec(N0 + HEADS - 1, last=True, ld=None)
                out_low(N0 + HEADS - 1)
                v.wait_ge(omm, N0 + HEADS)
                block_end(2 + H, 1, tg[:, 2:3])

            v.wait_ge(ld_ff, 48)
            v.wait_ge(fsp, 1)
            V.tensor_copy(w2hi[:, 0:FFT, :], w2[:, 0:FFT, :]).then_inc(fsp, 1)
            V.tensor_copy(w2hi[FFR:2 * FFR, FFT, :], w2[FFR:2 * FFR, FFT, :]).then_inc(fsp, 1)
            V.tensor_tensor(w13lo[:], w13[:], f32(w13hi[:]), ALU.subtract).then_inc(fsp, 1)
            v.wait_ge(fsp, 4)
            V.tensor_tensor(w2lo[:, 0:FFT, :], w2[:, 0:FFT, :], f32(w2hi[:, 0:FFT, :]), ALU.subtract).then_inc(fsp, 1)
            V.tensor_tensor(w2lo[FFR:2 * FFR, FFT, :], w2[FFR:2 * FFR, FFT, :], f32(w2hi[FFR:2 * FFR, FFT, :]),
                            ALU.subtract).then_inc(fsp, 1)
            residual(2, (4, 5))
            ln_half(4)
            xt_low(4, (2, 3), 0)
            residual(3, (6, 7))
            ln_half(5)

            def ff_vec(H, i):
                k = H * (FFT + 1) + i
                G, U = 4 + 2 * (i % 2), 5 + 2 * (i % 2)
                if i < FFT:
                    v.wait_ge(f_u, H * FFT + i + 1)
                v.wait_ge(f_silu, k + 1)
                if k >= 2:
                    v.wait_ge(f_hi, k - 1)
                if i < FFT:
                    V.scalar_tensor_tensor(out=hid[i % 2][:], in0=bank[U][:], scalar=cols[:, US + i:US + i + 1],
                                           in1=act[i % 2][:], op0=ALU.mult, op1=ALU.mult).then_inc(f_h, 1)
                else:
                    r = slice(FFR, 2 * FFR)
                    V.scalar_tensor_tensor(out=hid[i % 2][r, :], in0=bank[G][r, :], scalar=cols[r, TAIL:NCOLS],
                                           in1=act[i % 2][r, :], op0=ALU.mult, op1=ALU.mult).then_inc(f_h, 1)
                v.wait_ge(f_hi, k + 1)
                r = slice(0, P) if i < FFT else slice(FFR, 2 * FFR)
                V.tensor_tensor(hidlo[i % 2][r, :], hid[i % 2][r, :], f32(hidhi[i % 2][r, :]), ALU.subtract).then_inc(f_lo, 1)

            for H in range(2):
                for i in range(FFT + 1):
                    ff_vec(H, i)
                    if H == 0 and i == 3:
                        xt_low(5, (2, 3), 1)
                v.wait_ge(f_down, (H + 1) * (FFT + 1))
                block_end(4 + H, 1, dscale[:, 1:2])
            for H in range(2):
                residual(4 + H, (4, 5) if H == 0 else (6, 7))

        @block.tensor
        def _(pe):
            mm, tr = nc.tensor.matmul, nc.tensor.transpose
            pe.wait_ge(ld_ctxT, 32)
            for j in range(4):
                mm(bank[j][:], w0[:, tile_cols(j // 2)], ctxT[:, tile_cols(j % 2, HALF)],
                   start=True, stop=True).then_inc(proj, 1)
            for b in range(BATCH):
                pe.wait_ge(q0_out, b // 2 + 1)
                pe.wait_ge(k0_out, b // 2 + 1)
                for i in range(2):
                    ins = mm(bank[4 + b][:, tile_cols(i, SEQ)], q0[:, tile_cols(2 * b + i)], k0[:, tile_cols(b, SEQ)],
                             start=True, stop=True)
                ins.then_inc(energy, 1)
            pe.wait_ge(const, 3)
            for b in range(BATCH):
                pe.wait_ge(ln_out, 2 * b + 2)
                pe.wait_ge(a_exp, 2 * b + 2)
                for j in range(2):
                    for i in range(2):
                        ins = tr(bank[4 + b][:, j * SEQ + i * P:j * SEQ + (i + 1) * P], xln[:, 2 * b + i, tile_cols(j)], ident[:])
                ins.then_inc(xt0_tr, 1)
                pe.wait_ge(a_norm, 2 * b + 2)
                for j in range(2):
                    for i in range(2):
                        ins = tr(bank[b][:, j * SEQ + i * P:j * SEQ + (i + 1) * P], A[:, 2 * b + i, tile_cols(j)], ident[:])
                ins.then_inc(at_tr, 1)
            for b in range(BATCH):
                pe.wait_ge(xt0_out, b + 1)
                pe.wait_ge(at_out, b + 1)
                for i in range(2):
                    for j in range(2):
                        ins = mm(bank[b][:, tile_cols(i, SEQ)], XT0[:, b, j, tile_cols(i)], AT[:, b, j, :],
                                 start=(j == 0), stop=(j == 1))
                ins.then_inc(mix, 1)

            def key_chunk(ck, first=False):
                for tt in range(TILES):
                    if not (first and tt < 4):
                        pe.wait_ge(k_out, ck * TILES + tt - 3)
                    c = tile_cols(tt)
                    three(mm, bank[4 + tt % 4][:], ctxThi[:, c], ctxTlo[:, c], wkhi[:, bass.ts(ck, 512)],
                          wklo[:, bass.ts(ck, 512)], True, True).then_inc(kmm, 1)

            def xt_transpose(k, banks, half):
                pe.wait_ge(ln_out, 8 + 4 * k + 4)
                for kt in range(KT):
                    for i in range(HTILES):
                        ins = tr(bank[banks[kt]][:, tile_cols(i)], xln[:, half * HTILES + i, tile_cols(kt)], ident[:])
                    ins.then_inc(xt_tr, 1)

            pe.wait_ge(csp_p, 2)
            key_chunk(0, first=True)
            key_chunk(1)
            pe.wait_ge(x_new, 2)
            xt_transpose(0, (0, 1), 0)
            pe.wait_ge(x_new, 4)
            xt_transpose(1, (2, 3), 1)
            pe.wait_ge(gws, 1)
            for tt in range(TILES):
                pe.wait_ge(xt_lo, 2 if tt < HTILES else 4)
                for kt in range(KT):
                    ins = three(mm, bank[0][:, tile_cols(tt, EXPERTS)], XThi[:, kt, tile_cols(tt)], XTlo[:, kt, tile_cols(tt)],
                                gwhi[:, kt, :], gwlo[:, kt, :], kt == 0, kt == KT - 1)
                ins.then_inc(logits, 1)
            with pe.Fori(2, 4) as ck:
                key_chunk(ck)

            def gate_up(it, t, h, first):
                n2 = it * 2 + h
                c = tile_cols(h, HALF)
                if h == 0:
                    pe.wait_ge(w_lo, it + 1)
                for j, free in ((0, silu), (1, h_ok)):
                    if not first:
                        pe.wait_ge(free, n2 - 1)
                    for kt in range(KT):
                        w = slice((kt * 2 + j) * P, (kt * 2 + j + 1) * P)
                        ins = three(mm, bank[4 + 2 * h + j][:], whi[t][:, w], wlo[t][:, w], XThi[:, kt, c], XTlo[:, kt, c],
                                    kt == 0, kt == KT - 1)
                    ins.then_inc(u_mm if j else g_mm, 1)

            def down_half(it, t, h, last):
                n2 = it * 2 + h
                pe.wait_ge(h_lo, n2 + 1)
                for o in range(OT_):
                    w = slice(2 * DIM + o * P, 2 * DIM + (o + 1) * P)
                    ins = three(mm, bank[2 * o + h][:], whi[t][:, w], wlo[t][:, w], hidhi[h][:], hidlo[h][:], False, last)
                ins.then_inc(down, 1)

            pe.wait_ge(k_out, 32)
            gate_up(0, 0, 0, True)
            gate_up(0, 0, 1, True)
            pe.wait_ge(comb_ok, 1)
            for hh in range(2):
                for i in range(HTILES):
                    ins = tr(bank[1 + hh][0:EXPERTS, tile_cols(i)], comb[:, hh * HTILES + i, :], ident[:])
                ins.then_inc(comb_tr, 1)
            pe.wait_ge(combT_out, 2)
            for j in range(4):
                mm(bank[j][:], zeros[:, 0:P], zeros[:], start=True, stop=False, skip_group_check=True)

            def moe_pe(m, last=False):
                for t in range(PARTS):
                    it = m * PARTS + t
                    end = last and t == PARTS - 1
                    for h in range(2):
                        if not end:
                            gate_up(it + 1, (t + 1) % PARTS, h, False)
                        down_half(it, t, h, end)

            with pe.Fori(0, GROUPS - 1) as m:
                moe_pe(m)
            moe_pe(GROUPS - 1, last=True)

            def block_back(k, banks):
                pe.wait_ge(ot_a, k + 1)
                pe.wait_ge(ot_v, k + 1)
                for i in range(HTILES):
                    for o in range(OT_):
                        ins = tr(bank[banks[i // 2]][:, (i % 2) * DIM + o * P:(i % 2) * DIM + (o + 1) * P],
                                 OT[k % 2][:, o, tile_cols(i)], ident[:])
                    if i % 2:
                        ins.then_inc(ot_tr, 1)

            def head_products(js):
                for j in js:
                    if j >= 4:
                        pe.wait_ge(p_lo, j - 3)
                    for i in range(2):
                        ins = mm(bank[j % 4][:, tile_cols(i, DIM)], wv[:, 2 * j + i, :], wo[:, 2 * j + i, :],
                                 start=True, stop=True)
                    ins.then_inc(pmm, 1)

            block_back(0, (4, 5))
            block_back(1, (6, 7))
            pe.wait_ge(ld_v, 32)
            pe.wait_ge(weighted, 2 * NIT)
            head_products(range(4))
            pe.wait_ge(x_new, 6)
            xt_transpose(2, (4, 5), 0)
            head_products(range(4, 8))
            pe.wait_ge(x_new, 8)
            xt_transpose(3, (6, 7), 1)

            def keys_T(N):
                pe.wait_ge(kn_ok, N + 1)
                for i in range(HTILES):
                    ins = tr(bank[3][:, tile_cols(i)], kn[:, i, :], ident[:])
                ins.then_inc(kt_tr, 1)

            def queries(N, H):
                pe.wait_ge(wq_s, N + 1)
                c = tile_cols(H, HALF)
                for kt in range(KT):
                    ins = three(mm, bank[2][:], wqhi[:, kt, :], wqlo[:, kt, :], XThi[:, kt, c], XTlo[:, kt, c],
                                kt == 0, kt == KT - 1)
                ins.then_inc(q_mm, 1)

            def query_squares(N):
                pe.wait_ge(q_sq, N + 1)
                pe.wait_ge(q_lo, N + 1)
                for i in range(HTILES):
                    ins = mm(bank[2][:, i:i + 1], qsq[:, tile_cols(i)], ones[:], start=True, stop=True)
                ins.then_inc(q_ss, 1)

            def scores(N):
                pe.wait_ge(k_lo, N + 1)
                pe.wait_ge(q_lo, N + 1)
                for b in range(2):
                    if not (isinstance(N, int) and N == 0):
                        pe.wait_ge(s_exp, 4 * N - 2 + 2 * b)
                    kc = tile_cols(b, SEQ)
                    for i in range(2):
                        qc = tile_cols(2 * b + i)
                        ins = three(mm, bank[4 + b][:, tile_cols(i, SEQ)], qhi[:, qc], qlo[:, qc], khi[:, kc], klo[:, kc],
                                    True, True)
                    ins.then_inc(s_mm, 1)

            def probs_T(N):
                for b in range(2):
                    pe.wait_ge(s_norm, 4 * N + 2 * b + 2)
                    if not (isinstance(N, int) and N == 0):
                        pe.wait_ge(pt_lo, 2 * N - 1 + b)
                    for j in range(2):
                        for i in range(2):
                            ins = tr(bank[6 + b][:, j * SEQ + i * P:j * SEQ + (i + 1) * P], Pm[:, b, i, tile_cols(j)], ident[:])
                    ins.then_inc(pt_tr, 1)

            def weighted_context(N, H, last):
                if not last:
                    pe.wait_ge(k_lo, N + 3)
                pe.wait_ge(pt_lo, 2 * N + 2)
                for b in range(2):
                    for j in range(2):
                        tt = H * HTILES + 2 * b + j
                        ins = three(mm, bank[3][:, tile_cols(b, SEQ)], ctxhi[:, tt, :], ctxlo[:, tt, :],
                                    PThi[:, b, j, :], PTlo[:, b, j, :], j == 0, j == 1)
                ins.then_inc(av, 1)

            def head_output(N, last):
                pe.wait_ge(o_lo, N + 1)
                pe.wait_ge(ph_ld, 32 * (N + 1))
                for o in range(OT_):
                    ins = three(mm, bank[o][:], phhi[:, tile_cols(o)], phlo[:, tile_cols(o)], ohi[:], olo[:], False, last)
                ins.then_inc(omm, 1)

            def head_pe(N, H, first=False, last=False):
                scores(N)
                if not last:
                    if not (isinstance(N, int) and N <= N0 + 1):
                        pe.wait_ge(o_lo, N - 1)
                    keys_T(N + 1)
                    queries(N + 1, H)
                if not first:
                    weighted_context(N - 1, H, last)
                if not last:
                    query_squares(N + 1)
                probs_T(N)
                if not first:
                    head_output(N - 1, False)

            pe.wait_ge(csp, 2)
            for H in range(2):
                N0 = H * HEADS
                pe.wait_ge(xt_lo, 4 + 2 * (H + 1))
                if H == 0:
                    pe.wait_ge(p_lo, 8)
                else:
                    pe.wait_ge(ot_a, 3)
                    pe.wait_ge(ot_v, 3)
                for o in range(OT_):
                    mm(bank[o][:], zeros[:, 0:P], zeros[:], start=True, stop=False, skip_group_check=True)
                keys_T(N0)
                queries(N0, H)
                query_squares(N0)
                head_pe(N0, H, first=True)
                head_pe(N0 + 1, H)
                with pe.Fori(2, HEADS - 1) as n:
                    head_pe(n + N0, H)
                head_pe(N0 + HEADS - 1, H, last=True)
                weighted_context(N0 + HEADS - 1, H, True)
                head_output(N0 + HEADS - 1, True)

            def ff_gate_up(H, i):
                k = H * (FFT + 1) + i
                G, U = 4 + 2 * (i % 2), 5 + 2 * (i % 2)
                if k >= 2:
                    pe.wait_ge(f_h, k - 1)
                c = tile_cols(H, HALF)
                for j in range(2 if i < FFT else 1):
                    for kt in range(KT):
                        ins = three(mm, bank[(G, U)[j]][:], w13hi[:, 2 * i + j, kt, :], w13lo[:, 2 * i + j, kt, :],
                                    XThi[:, kt, c], XTlo[:, kt, c], kt == 0, kt == KT - 1)
                    ins.then_inc((f_g, f_u)[j], 1)

            def ff_down(H, i):
                k = H * (FFT + 1) + i
                pe.wait_ge(f_lo, k + 1)
                r = slice(0, P) if i < FFT else slice(FFR, 2 * FFR)
                for o in range(OT_):
                    ins = three(mm, bank[o][:], w2hi[r, i, tile_cols(o)], w2lo[r, i, tile_cols(o)],
                                hidhi[i % 2][r, :], hidlo[i % 2][r, :], i == 0, i == FFT)
                ins.then_inc(f_down, 1)

            block_back(2, (4, 5))
            block_back(3, (6, 7))
            xt_transpose(4, (2, 3), 0)
            pe.wait_ge(x_new, 12)
            pe.wait_ge(fsp, 6)
            pe.wait_ge(xt_lo, 10)
            for H in range(2):
                if H == 0:
                    ff_gate_up(0, 0)
                    ff_gate_up(0, 1)
                    xt_transpose(5, (2, 3), 1)
                else:
                    pe.wait_ge(xt_lo, 12)
                    ff_gate_up(1, 0)
                    ff_gate_up(1, 1)
                    pe.wait_ge(ot_a, 5)
                    pe.wait_ge(ot_v, 5)
                for i in range(FFT + 1):
                    ff_down(H, i)
                    if i + 2 <= FFT:
                        ff_gate_up(H, i + 2)
            pe.wait_ge(f_h, 2 * (FFT + 1))
            block_back(4, (4, 5))
            block_back(5, (6, 7))


def kernel(**inputs):
    import numpy as np
    import concourse.bacc as bacc
    from concourse.bass_utils import run_bass_kernel_spmd as run

    a = {k: np.asarray(v) for k, v in inputs.items()}
    T = np.ascontiguousarray
    ctx_tok = a["ctx_1024"].reshape(TOK, CDIM)
    gu = a["L0_ffn_gate_up_proj"].reshape(GROUPS, GROUP, 2, PARTS, 32, KT, P).transpose(0, 3, 6, 5, 2, 1, 4)
    dn = a["L0_ffn_down_proj"].reshape(GROUPS, GROUP, DIM, PARTS, 32).transpose(0, 3, 1, 4, 2)
    moe = np.concatenate([gu.reshape(GROUPS * PARTS * P, 2 * DIM), dn.reshape(GROUPS * PARTS * P, DIM)], axis=1)
    gT, uT = a["L1_ffn_gate_w"].T, a["L1_ffn_up_w"].T
    tiles = []
    for i in range(FFT):
        tiles += [gT[:, i * P:(i + 1) * P], uT[:, i * P:(i + 1) * P]]
    tiles.append(np.concatenate([gT[:, FFT * P:], uT[:, FFT * P:]], axis=1))
    w13 = np.stack([t.reshape(KT, P, P) for t in tiles]).transpose(2, 0, 1, 3).reshape(P, -1)
    dT = a["L1_ffn_down_w"].T
    cols = np.concatenate([
        a["L0_xattn_bq"][:, None], a["L0_xattn_bk"][:, None], a["L1_xattn_gq"][:, None], a["L1_xattn_gk"][:, None],
        a["L1_ffn_down_s"].reshape(2, P).T, a["L1_ffn_gate_s"][:FFT * P].reshape(FFT, P).T,
        a["L1_ffn_up_s"][:FFT * P].reshape(FFT, P).T], axis=1)
    arrays = {
        "x": a["x"].reshape(TOK, DIM),
        "ctxn": ctx_tok,
        "ctxT": ctx_tok.T,
        "w0": np.concatenate([a["L0_xattn_Wq"].T, a["L0_xattn_Wk"].T], axis=1),
        "cols": cols,
        "tailg": a["L1_ffn_gate_s"][FFT * P:, None],
        "tailu": a["L1_ffn_up_s"][FFT * P:, None],
        "gates": np.stack([a["g_xattn"][0], a["g_ffn"][0], a["g_xattn"][1], a["g_ffn"][1]]),
        "gw": a["L0_ffn_gate_weight"].T,
        "moe": moe,
        "wq": a["L1_xattn_Wq"].reshape(KT, P, HEADS, HD).transpose(1, 2, 0, 3).reshape(P, -1),
        "wk": a["L1_xattn_Wk"],
        "wv": a["L1_xattn_Wv"].reshape(CDIM, HEADS, HD).transpose(2, 1, 0).reshape(P, -1),
        "wo": a["L1_xattn_Wo"].reshape(HEADS, HD, DIM).transpose(1, 0, 2).reshape(P, -1),
        "w13": w13,
        "w2": dT[:FFT * P].reshape(FFT, P, DIM).transpose(1, 0, 2).reshape(P, -1),
        "w2t": dT[FFT * P:],
    }
    arrays = {f"in_{k}": T(v) for k, v in arrays.items()}
    nc = bacc.Bacc("TRN2", target_bir_lowering=False, num_devices=1)
    args = [nc.dram_tensor(k, v.shape, F32, kind="ExternalInput").ap() for k, v in arrays.items()]
    args.append(nc.dram_tensor("result", (TOK, DIM), F32, kind="ExternalOutput").ap())
    args.append(nc.dram_tensor("combine", (EXPERTS, TOK), F32, kind="Internal").ap())
    flamingo(nc, *args)
    r = run(nc, [arrays], core_ids=[0])
    return r.results[0]["result"].reshape(BATCH, SEQ, DIM)
```

```python
from contextlib import ExitStack

import concourse.bass as bass
from concourse import mybir

P = 128
BATCH, SEQ, DIM, CDIM = 4, 256, 256, 128
TOK = BATCH * SEQ
TILES = TOK // P
HALF = 512
HTILES = HALF // P
KT = DIM // P
OT_ = DIM // P
EXPERTS, TOPK, INTER = 32, 8, 96
THRESHOLD = 0.8
GROUP = 4
GROUPS = EXPERTS // GROUP
PARTS = INTER // 32
MW = 3 * DIM
HEADS, HD = 16, 128
FF = 704
FFT = FF // P
FFR = FF - FFT * P
EPS = 1e-5

F32 = mybir.dt.float32
F32R = mybir.dt.float32r
BF16 = mybir.dt.bfloat16
U32 = mybir.dt.uint32
ALU = mybir.AluOpType
ACT = mybir.ActivationFunctionType
AX = mybir.AxisListType

BQ, BK, GQ, GK, DS, GS = 0, 1, 2, 3, 4, 6
US = GS + FFT
TAIL = US + FFT
NCOLS = TAIL + 1


class Signal:

    def __init__(self, sem):
        self.sem, self.n = sem, 0

    def on(self, ins, by=1):
        ins.then_inc(self.sem, by)
        self.n += by
        return self.n


def flamingo(nc, x_d, ctxn_d, ctxT_d, w0_d, cols_d, tailg_d, tailu_d, gates_d, gw_d, moe_d,
             wq_d, wk_d, wv_d, wo_d, wff_d, w2t_d, out_d, comb_d):
    ctx = ExitStack()
    with ctx:
        base = (nc.sbuf_base + 31) // 32 * 32
        top = [0]

        def place(name, shape, dt=F32, at=None):
            size = 4 if dt != BF16 else 2
            for s in shape[1:]:
                size *= s
            size = (size + 31) // 32 * 32
            off = top[0] if at is None else at
            if at is None:
                top[0] += size
            ends[name] = off + size
            assert base + off + size <= nc.sbuf_usable_end, (name, off + size)
            return nc.alloc_sbuf_tensor_at(name, list(shape), dt, offset=base + off)

        ends = {}

        def sem(name):
            return ctx.enter_context(nc.semaphore(name))

        bank = [ctx.enter_context(nc.psum_tensor(f"bank{i}", [P, 512], F32)) for i in range(8)]
        x = place("x", [P, TILES, DIM])
        lnat = top[0]
        xln = place("xln", [P, TILES, DIM])
        OT = [place(f"OT{h}", [P, OT_, HALF], at=lnat + h * 4096) for h in range(2)]
        XThi = place("XThi", [P, KT, TOK], F32R)
        XTlo = place("XTlo", [P, KT, TOK], F32R)
        ctxn = place("ctxn", [P, TILES, CDIM])
        krat = top[0]
        kraw = place("kraw", [P, TILES, HEADS * HD])
        phat = top[0]
        PHhi = place("PHhi", [P, HEADS, DIM], F32R)
        PHlo = place("PHlo", [P, HEADS, DIM], F32R)
        cols = place("cols", [P, NCOLS])
        gates = place("gates", [P, 4])
        tg = place("tg", [P, 4])
        ident = place("ident", [P, P])
        mhalf = place("mhalf", [P, TILES])
        gain = place("gain", [P, 1])
        dscale = place("dscale", [P, OT_])
        ones = place("ones", [P, 1])
        stats = place("stats", [P, TILES, 6])
        mv = place("mv", [P, TILES, 2])
        veps = place("veps", [P, TILES])
        rstd = place("rstd", [P, TILES])
        kst = place("kst", [P, 4])
        kss = place("kss", [P, TILES, HEADS])
        rk = place("rk", [P, TILES, HEADS])
        asum = place("asum", [P, TILES])
        nmax = place("nmax", [P, TILES])
        rsum = place("rsum", [P, TILES])
        gwraw = place("gwraw", [P, KT, EXPERTS])
        gwhi = place("gwhi", [P, KT, EXPERTS], F32R)
        gwlo = place("gwlo", [P, KT, EXPERTS], F32R)
        zeros = place("zeros", [P, 512], BF16)
        R = top[0]
        q0 = place("q0", [P, TOK], at=phat)
        k0 = place("k0", [P, TOK], at=phat + 4096)
        XT0 = place("XT0", [P, BATCH, 2, SEQ], at=phat + 8192)
        A = place("A", [P, TILES, SEQ], at=phat + 16384)
        AT = place("AT", [P, BATCH, 2, SEQ], at=phat + 24576)
        ctxT = place("ctxT", [P, TOK], at=R)
        w0 = place("w0", [P, 2 * CDIM], at=R + 4096)
        wk = place("wk", [P, HEADS * HD], at=R + 5120)
        wkhi = place("wkhi", [P, HEADS * HD], F32R, at=R + 13312)
        wklo = place("wklo", [P, HEADS * HD], F32R, at=R + 21504)
        ctxThi = place("ctxThi", [P, TOK], F32R, at=R + 29696)
        ctxTlo = place("ctxTlo", [P, TOK], F32R, at=R + 33792)
        E8 = [P, TILES, TOPK]
        eq = place("eq", [P, TILES, EXPERTS, TOPK], at=phat)
        o = phat + 8192
        lg = place("lg", [P, TILES, EXPERTS], at=o)
        comb = place("comb", [P, TILES, EXPERTS], at=o + 1024)
        iota32 = place("iota32", [P, EXPERTS], at=o + 2048)
        iota8 = place("iota8", [P, TOPK], at=o + 2176)
        keep8 = place("keep8", E8, at=o + 2304)
        top8 = place("top8", E8, at=o + 2560)
        idx8 = place("idx8", E8, U32, at=o + 2816)
        idxf = place("idxf", E8, at=o + 3072)
        ren8 = place("ren8", E8, at=o + 3328)
        cum8 = place("cum8", E8, at=o + 3584)
        rw8 = place("rw8", E8, at=o + 3840)
        s8 = place("s8", [P, TILES], at=o + 4096)
        r8 = place("r8", [P, TILES], at=o + 4128)
        combT = place("combT", [EXPERTS, TOK], at=o + 4608)
        CE = place("CE", [P, GROUPS, TOK], at=phat)
        whi = [place(f"whi{t}", [P, MW], F32R, at=R + 3072 * t) for t in range(PARTS)]
        wlo = [place(f"wlo{t}", [P, MW], F32R, at=R + 9216 + 3072 * t) for t in range(PARTS)]
        act = [place(f"act{h}", [P, HALF], at=R + 18432 + 2048 * h) for h in range(2)]
        hid = [place(f"hid{h}", [P, HALF], at=R + 22528 + 2048 * h) for h in range(2)]
        hidhi = [place(f"hidhi{h}", [P, HALF], F32R, at=R + 26624 + 2048 * h) for h in range(2)]
        hidlo = [place(f"hidlo{h}", [P, HALF], F32R, at=R + 30720 + 2048 * h) for h in range(2)]
        ksq = place("ksq", [P, 4 * HD], at=lnat)
        wraw = [place(f"wraw{t}", [P, MW], at=R + 37888 + 3072 * t) for t in range(PARTS)]
        wv = place("wv", [P, HEADS, CDIM], at=R + 47104)
        wo = place("wo", [P, HEADS, DIM], at=R + 55296)
        a3 = [R]

        def put3(name, shape, dt=F32):
            t = place(name, shape, dt, at=a3[0])
            a3[0] = ends[name]
            return t
        ctxhi = put3("ctxhi", [P, TILES, CDIM], F32R)
        ctxlo = put3("ctxlo", [P, TILES, CDIM], F32R)
        qhi = put3("qhi", [P, HALF], F32R)
        qlo = put3("qlo", [P, HALF], F32R)
        qsq = put3("qsq", [P, HALF])
        kn = put3("kn", [P, HTILES, HD])
        khi = put3("khi", [P, HALF], F32R)
        klo = put3("klo", [P, HALF], F32R)
        Pm = [put3(f"Pm{i}", [P, 2, 2, SEQ]) for i in range(2)]
        PThi = put3("PThi", [P, 2, 2, SEQ], F32R)
        PTlo = put3("PTlo", [P, 2, 2, SEQ], F32R)
        ohi = put3("ohi", [P, HALF], F32R)
        olo = put3("olo", [P, HALF], F32R)
        wqraw = put3("wqraw", [P, KT * HD])
        wqhi = put3("wqhi", [P, KT, HD], F32R)
        wqlo = put3("wqlo", [P, KT, HD], F32R)
        phhi = put3("phhi", [P, DIM], F32R)
        phlo = put3("phlo", [P, DIM], F32R)
        qss = put3("qss", [P, HTILES])
        qsc = [put3(f"qsc{i}", [P, HTILES]) for i in range(2)]
        smax = put3("smax", [P, 2, 2])
        nbias = put3("nbias", [P, 2, 2])
        psumr = put3("psumr", [P, 2, 2])
        prec = [put3(f"prec{i}", [P, 2, 2]) for i in range(2)]
        assert a3[0] <= R + 47104, a3[0] - R
        WFT = 2 * FFT + 1 + FFT
        wff = place("wff", [P, WFT + 1, DIM], at=a3[0])
        wfhi = place("wfhi", [P, WFT + 1, DIM], F32R, at=krat)
        wflo = place("wflo", [P, WFT - 1, DIM], F32R, at=ends["wfhi"])
        wflo2 = place("wflo2", [P, 2, DIM], F32R, at=ends["wff"])
        assert ends["wflo"] <= krat + HTILES * HEADS * HD * 4

        S = {}

        def signal(name):
            if name not in S:
                S[name] = Signal(sem(name))
            return S[name]

        NIT = GROUPS * PARTS
        ld_small, ld_ctxT, ld_ctxn, ld_gw, ld_v, ld_ff = [
            sem(n) for n in ("ld_small", "ld_ctxT", "ld_ctxn", "ld_gw", "ld_v", "ld_ff")]
        ld_x = [sem(f"ld_x{h}") for h in range(2)]
        ld_k = [sem(f"ld_k{h}") for h in range(2)]
        const = sem("const")
        proj = sem("proj"); q0_out = sem("q0_out"); k0_out = sem("k0_out"); energy = sem("energy")
        a_max = sem("a_max"); a_exp = sem("a_exp"); a_norm = sem("a_norm"); tgr = sem("tgr")
        xt0_tr = sem("xt0_tr"); xt0_out = sem("xt0_out"); at_tr = sem("at_tr"); at_out = sem("at_out")
        mix = sem("mix")
        ln_var = sem("ln_var"); ln_rstd = sem("ln_rstd"); ln_out = sem("ln_out")
        xt_tr = sem("xt_tr"); xt_hi = sem("xt_hi"); xt_lo = sem("xt_lo"); x_new = sem("x_new")
        ot_a = sem("ot_a"); ot_v = sem("ot_v"); ot_tr = sem("ot_tr")
        vch = sem("vch")
        pch = sem("pch")
        csp_a = sem("csp_a"); csp_p = sem("csp_p"); kmm = sem("kmm"); k_out = sem("k_out")
        gws = sem("gws"); logits = sem("logits"); lg_sub = sem("lg_sub"); lg_exp = sem("lg_exp")
        comb_ok = sem("comb_ok"); comb_tr = sem("comb_tr"); combT_out = sem("combT_out")
        comb_st = sem("comb_st"); ce_ld = sem("ce_ld")
        w_ld = [sem(f"w_ld{t}") for t in range(PARTS)]
        w_hi = sem("w_hi"); w_lo = sem("w_lo")
        g_mm = sem("g_mm"); u_mm = sem("u_mm"); silu = sem("silu"); weighted = sem("weighted")
        h_ok = sem("h_ok"); h_hi = sem("h_hi"); h_lo = sem("h_lo"); down = sem("down")
        sq_ok = sem("sq_ok"); sq_raw = sem("sq_raw"); sq_sum = sem("sq_sum"); rk_ok = sem("rk_ok")
        pmm = sem("pmm"); p_hi = sem("p_hi"); p_lo = sem("p_lo")
        csp = sem("csp"); wq_ld = sem("wq_ld"); wq_h = sem("wq_h"); wq_s = sem("wq_s"); ph_ld = sem("ph_ld")
        kn_ok = sem("kn_ok"); kt_tr = sem("kt_tr"); k_hi = sem("k_hi"); k_lo = sem("k_lo")
        q_mm = sem("q_mm"); q_hi = sem("q_hi"); q_lo = sem("q_lo"); q_sq = sem("q_sq")
        q_ss = sem("q_ss"); q_ssout = sem("q_ssout"); q_sc = sem("q_sc")
        s_mm = sem("s_mm"); s_max = sem("s_max"); s_bias = sem("s_bias"); s_exp = sem("s_exp")
        s_rec = sem("s_rec"); s_norm = sem("s_norm"); pt_tr = sem("pt_tr"); pt_hi = sem("pt_hi")
        pt_lo = sem("pt_lo"); av = sem("av"); o_hi = sem("o_hi"); o_lo = sem("o_lo"); omm = sem("omm")
        ff_hi = sem("ff_hi"); ff_lo = sem("ff_lo"); f_g = sem("f_g"); f_u = sem("f_u"); f_silu = sem("f_silu"); f_h = sem("f_h")
        f_hi = sem("f_hi"); f_lo = sem("f_lo"); f_down = sem("f_down"); st_out = sem("st_out")

        def f32(ap):
            return ap.bitcast(F32)

        def three(mm, out, wh_, wl_, mhi, mlo, start, stop):
            mm(out, wl_, mhi, start=start, stop=False, skip_group_check=True)
            mm(out, wh_, mhi, start=False, stop=False, skip_group_check=True)
            return mm(out, wh_, mlo, start=False, stop=stop, skip_group_check=True)

        def apart(engine, sem_, value):
            engine.wait_ge(sem_, value)

        def tile_cols(i, n=P):
            return slice(i * n, (i + 1) * n)

        LAST = 2 * HEADS - 1

        def all_heads(engine, step):
            for h in range(2):
                for N in ((0, 1), (HEADS, HEADS + 1))[h]:
                    step(N % HEADS, h, N % 2, N)
                with engine.Fori(1, HEADS // 2 - 2) as pair:
                    for par in range(2):
                        step(2 * pair + par, h, par, None)
                for N in range(h * HEADS + HEADS - 4, (h + 1) * HEADS):
                    step(N % HEADS, h, N % 2, N)

        def ahead(n, h, d):
            N = n + h * HEADS + d
            return (N % HEADS, N // HEADS, N) if isinstance(n, int) else (n + d, h, N)

        BACK = {HEADS - 4: (1, 0), HEADS - 3: (1, 1), 2 * HEADS - 4: (2, 0), 2 * HEADS - 3: (2, 1)}
        TURN = {HEADS - 2: (3, 0), HEADS - 1: (3, 1), 2 * HEADS - 2: (4, 0), 2 * HEADS - 1: (4, 1)}
        PIECE = 384

        HPB = (4, 5, 6, 7, 4, 5, 7, 7)

        block = ctx.enter_context(nc.Block())

        @block.sync
        def _(sp):
            sp.dma_start(ctxT[:], ctxT_d).then_inc(ld_ctxT, 16)
            sp.dma_start(w0[:], w0_d).then_inc(ld_ctxT, 16)
            sp.dma_start(cols[:, 0:TAIL], cols_d).then_inc(ld_small, 16)
            sp.dma_start(cols[0:FFR, TAIL:NCOLS], tailg_d).then_inc(ld_small, 16)
            sp.dma_start(cols[FFR:2 * FFR, TAIL:NCOLS], tailu_d).then_inc(ld_small, 16)
            sp.dma_start(gates[:], gates_d.partition_broadcast(P)).then_inc(ld_small, 16)
            for h in range(2):
                c = slice(h * HTILES, (h + 1) * HTILES)
                sp.dma_start(x[:, c, :], x_d.rearrange("(t p) d -> p t d", p=P)[:, c, :]).then_inc(ld_x[h], 16)
                c = tile_cols(h, HEADS * HD // 2)
                sp.dma_start(wk[:, c], wk_d[:, c]).then_inc(ld_k[h], 16)
            sp.dma_start(gwraw[:], gw_d.rearrange("(k p) e -> p k e", p=P)).then_inc(ld_gw, 16)
            sp.dma_start(ctxn[:], ctxn_d.rearrange("(t p) d -> p t d", p=P)).then_inc(ld_ctxn, 16)

            def load_expert_tile(m, t, first):
                if not first:
                    apart(sp, ld_x[0], 16)
                    sp.wait_ge(w_lo, (m - 1) * PARTS + t + 1)
                sp.dma_start(wraw[t][:], moe_d[bass.ts(m * PARTS + t, P), :]).then_inc(w_ld[t], 16)

            for t in range(PARTS):
                load_expert_tile(0, t, True)
            sp.dma_start(wv[:].rearrange("p h c -> p (h c)"), wv_d).then_inc(ld_v, 16)
            sp.dma_start(wo[:].rearrange("p h c -> p (h c)"), wo_d).then_inc(ld_v, 16)
            sp.wait_ge(combT_out, 2)
            sp.dma_start(comb_d, combT[:]).then_inc(comb_st, 16)
            sp.wait_ge(comb_st, 16)

            def load_combine(m):
                src = comb_d[bass.ds(m * GROUP, GROUP), :].unsqueeze(1).broadcast_to([GROUP, 32, TOK])
                sp.dma_start(CE[:, bass.ds(m, 1), :].rearrange("p a b -> p (a b)"), src).then_inc(ce_ld, 16)

            load_combine(0)
            with sp.Fori(1, GROUPS) as m:
                apart(sp, ld_x[0], 16)
                sp.wait_ge(ce_ld, 16 * m)
                load_combine(m)
                for t in range(PARTS):
                    load_expert_tile(m, t, False)

            def load_wq(n, N):
                if not (isinstance(N, int) and N == 0):
                    apart(sp, ld_x[0], 16)
                    sp.wait_ge(wq_s, N)
                sp.dma_start(wqraw[:], wq_d[:, bass.ts(n, KT * HD)]).then_inc(wq_ld, 16)

            def load_ph(n, N):
                if not (isinstance(N, int) and N == 0):
                    apart(sp, ld_x[0], 16)
                    sp.wait_ge(omm, N)
                for dst, src in ((phhi, PHhi), (phlo, PHlo)):
                    sp.dma_start(f32(dst[:]), f32(src[:].rearrange("p h o -> p (h o)")[:, bass.ts(n, DIM)])).then_inc(ph_ld, 16)

            def head_loads(n, h, par, at):
                n2, _, N2 = ahead(n, h, 2)
                if not isinstance(N2, int) or N2 <= LAST:
                    load_wq(n2, N2)
                if at == 0:
                    sp.wait_ge(p_lo, 4)
                load_ph(n, n + h * HEADS)
                if at == 1:
                    sp.wait_ge(p_lo, 8)
                    sp.dma_start(wff[:, 0:WFT, :].rearrange("p a b -> p (a b)"), wff_d).then_inc(ld_ff, 16)
                    sp.dma_start(wff[FFR:2 * FFR, WFT, :], w2t_d).then_inc(ld_ff, 16)

            sp.wait_ge(down, 2 * NIT)
            load_wq(0, 0)
            load_wq(1, 1)
            all_heads(sp, head_loads)
            for i in range(4):
                sp.wait_ge(x_new, 4 * 3 + i + 1)
                sp.dma_start(out_d.rearrange("(t p) d -> p t d", p=P)[:, 2 * i:2 * i + 2, :],
                             x[:, 2 * i:2 * i + 2, :]).then_inc(st_out, 16)
            sp.wait_ge(st_out, 64)

        @block.gpsimd
        def _(pool):
            nc.gpsimd.memset(ident[:], 0.0).then_inc(pch, 1)
            nc.gpsimd.memset(mhalf[:], -0.5).then_inc(const, 1)
            nc.gpsimd.memset(ones[:], 1.0).then_inc(const, 1)
            nc.gpsimd.memset(zeros[:].bitcast(F32), 0.0).then_inc(const, 1)
            pool.wait_ge(pch, 1)
            nc.gpsimd.affine_select(out=ident[:], in_=ident[:], compare_op=ALU.not_equal, fill=1.0, base=0,
                                    pattern=[[-1, P]], channel_multiplier=1).then_inc(const, 1)
            pool.wait_ge(csp_a, 1)
            nc.gpsimd.tensor_tensor(ctxTlo[:], ctxT[:], f32(ctxThi[:]), ALU.subtract).then_inc(csp_p, 1)

            def key_weights_low(ck):
                pool.wait_ge(csp_a, ck + 2)
                c = tile_cols(ck, 512)
                nc.gpsimd.tensor_tensor(wklo[:, c], wk[:, c], f32(wkhi[:, c]), ALU.subtract).then_inc(csp_p, 1)

            for ck in range(2):
                key_weights_low(ck)
            ch = [1]

            def rstd_of(group):
                k, tt = group
                pool.wait_ge(ln_var, k + 1)
                nc.gpsimd.tensor_scalar(veps[:, tt:tt + 2], mv[:, tt:tt + 2, 1], EPS, 1.0, ALU.add, ALU.mult).then_inc(pch, 1)
                ch[0] += 1
                pool.wait_ge(pch, ch[0])
                nc.gpsimd.tensor_tensor(rstd[:, tt:tt + 2], veps[:, tt:tt + 2], mhalf[:, 0:2], ALU.pow).then_inc(ln_rstd, 1)

            for b in range(BATCH):
                rstd_of((b, 2 * b))
            for ck in range(2, 4):
                key_weights_low(ck)
            for b in range(BATCH):
                rstd_of((4 + b, 2 * b))

            def split_low(it, t):
                pool.wait_ge(w_hi, it + 1)
                nc.gpsimd.tensor_tensor(wlo[t][:], wraw[t][:], f32(whi[t][:]), ALU.subtract).then_inc(w_lo, 1)

            def key_scale(m, c):
                nc.gpsimd.tensor_tensor(rk[:, bass.ds(m, 1), c * 4:(c + 1) * 4].rearrange("p a b -> p (a b)"),
                                        kss[:, bass.ds(m, 1), c * 4:(c + 1) * 4].rearrange("p a b -> p (a b)"),
                                        mhalf[:, 0:4], ALU.pow).then_inc(rk_ok, 1)

            def key_squares(m, c, first=False):
                if not first:
                    pool.wait_ge(sq_sum, m * 4 + c)
                kv = kraw[:, bass.ds(m, 1), c * 512:(c + 1) * 512].rearrange("p a b -> p (a b)")
                nc.gpsimd.tensor_tensor(ksq[:], kv, kv, ALU.mult).then_inc(sq_ok, 1)

            def moe_pool(m, last=False):
                for t in range(PARTS):
                    it = m * PARTS + t
                    if not last:
                        for c in ([t] if t < PARTS - 1 else [t, t + 1]):
                            key_squares(m + 1, c)
                            key_scale(*((m + 1, c - 1) if c else (m, 3)))
                    if not (last and t > 0):
                        split_low(it + 2, (t + 2) % PARTS)

            pool.wait_ge(xt_tr, 4)
            for t in range(2):
                split_low(t, t)
            for c in range(4):
                pool.wait_ge(k_out, 8 * c + 1)
                key_squares(0, c, first=c == 0)
                if c:
                    key_scale(0, c - 1)
            with pool.Fori(0, GROUPS - 1) as m:
                moe_pool(m)
            moe_pool(GROUPS - 1, last=True)
            pool.wait_ge(sq_sum, 4 * TILES)
            key_scale(TILES - 1, 3)
            for b in range(2):
                rstd_of((8 + b, 2 * b))
            pool.wait_ge(csp, 1)
            nc.gpsimd.tensor_tensor(ctxlo[:], ctxn[:], f32(ctxhi[:]), ALU.subtract).then_inc(csp, 1)

            def norm_keys(n, H, N):
                nc.gpsimd.tensor_tensor(
                    kn[:], kraw[:, H * HTILES:(H + 1) * HTILES, bass.ts(n, HD)],
                    rk[:, H * HTILES:(H + 1) * HTILES, bass.ds(n, 1)].broadcast_to([P, HTILES, HD]),
                    ALU.mult).then_inc(kn_ok, 1)

            def query_scale(N, par):
                pool.wait_ge(q_ssout, N + 1)
                nc.gpsimd.tensor_tensor(qsc[par][:], qss[:], mhalf[:, 0:HTILES], ALU.pow).then_inc(q_sc, 1)

            def softmax_norm(N, par, b):
                pool.wait_ge(s_rec, 2 * N + b + 1)
                pm = Pm[par][:, b]
                nc.gpsimd.tensor_tensor(pm, pm, prec[par][:, b, :].unsqueeze(2).broadcast_to([P, 2, SEQ]),
                                        ALU.mult).then_inc(s_norm, 1)

            def query_weights_low(N):
                pool.wait_ge(wq_h, N + 1)
                nc.gpsimd.tensor_tensor(wqlo[:].rearrange("p a b -> p (a b)"), wqraw[:],
                                        f32(wqhi[:].rearrange("p a b -> p (a b)")), ALU.subtract).then_inc(wq_s, 1)

            def head_pool(n, h, par, at):
                N = n + h * HEADS
                if at is None or at + 2 <= LAST:
                    pool.wait_ge(kt_tr, N + 2)
                    norm_keys(*ahead(n, h, 2))
                softmax_norm(N, par, 0)
                if at != LAST:
                    query_scale(N + 1, 1 - par)
                if at is None or at + 2 <= LAST:
                    query_weights_low(N + 2)
                if h == 1 and at is None:
                    pool.wait_ge(ff_hi, n - 1)
                    flat = "p a b -> p (a b)"
                    c = bass.ts(n - 2, PIECE)
                    nc.gpsimd.tensor_tensor(wflo[:].rearrange(flat)[:, c], wff[:].rearrange(flat)[:, c],
                                            f32(wfhi[:].rearrange(flat)[:, c]), ALU.subtract).then_inc(ff_lo, 1)
                if at == 2 * HEADS - 4:
                    pool.wait_ge(ff_hi, 12)
                    nc.gpsimd.tensor_tensor(wflo2[:, 0, :], wff[:, WFT - 1, :], f32(wfhi[:, WFT - 1, :]),
                                            ALU.subtract).then_inc(ff_lo, 1)
                    pool.wait_ge(ff_lo, 11)
                    r = slice(FFR, 2 * FFR)
                    nc.gpsimd.tensor_tensor(wflo2[r, 1, :], wff[r, WFT, :], f32(wfhi[r, WFT, :]),
                                            ALU.subtract).then_inc(ff_lo, 1)
                    pool.wait_ge(ff_lo, 12)
                softmax_norm(N, par, 1)
                if at in BACK:
                    k, piece = BACK[at]
                    rstd_of((8 + 2 * k + piece, (k % 2) * HTILES + 2 * piece))

            pool.wait_ge(rk_ok, 4 * TILES)
            norm_keys(0, 0, 0)
            query_weights_low(0)
            query_weights_low(1)
            query_scale(0, 0)
            pool.wait_ge(kt_tr, 1)
            norm_keys(1, 0, 1)
            all_heads(pool, head_pool)
            for i in range(2):
                rstd_of((14 + i, HTILES + 2 * i))

        @block.scalar
        def _(s):
            act_ = nc.scalar.activation
            s.wait_ge(ld_ctxT, 32)
            act_(ctxThi[:], ctxT[:], ACT.Copy).then_inc(csp_a, 1)
            s.wait_ge(ld_small, 64)
            for h in range(2):
                s.wait_ge(proj, 2 * h + 1)
                act_(q0[:, tile_cols(h, HALF)], bank[h][:], ACT.Identity, bias=cols[:, BQ:BQ + 1]).then_inc(q0_out, 1)
            act_(tg[:], gates[:], ACT.Tanh).then_inc(tgr, 1)

            def key_weights_high(ck):
                s.wait_ge(ld_k[ck // 2], 16)
                c = tile_cols(ck, 512)
                act_(wkhi[:, c], wk[:, c], ACT.Copy).then_inc(csp_a, 1)

            def keys_out(ck, tts, first):
                for tt in tts:
                    s.wait_ge(kmm, ck * TILES + tt + 1)
                    act_(kraw[:, tt, bass.ts(ck, 512)], bank[first + tt % 4][:], ACT.Copy).then_inc(k_out, 1)

            for ck in range(2):
                key_weights_high(ck)
            for b in range(BATCH):
                s.wait_ge(a_max, b + 1)
                for i in range(2):
                    tt = 2 * b + i
                    act_(A[:, tt, :], bank[4 + b][:, tile_cols(i, SEQ)], ACT.Exp, bias=nmax[:, tt:tt + 1],
                         accum_out=asum[:, tt:tt + 1]).then_inc(a_exp, 1)
                keys_out(0, (2 * b, 2 * b + 1), 0)
            for b in range(BATCH):
                s.wait_ge(xt0_tr, b + 1)
                act_(XT0[:, b].rearrange("p a b -> p (a b)"), bank[4 + b][:], ACT.Copy).then_inc(xt0_out, 1)
                s.wait_ge(at_tr, b + 1)
                act_(AT[:, b].rearrange("p a b -> p (a b)"), bank[b][:], ACT.Copy).then_inc(at_out, 1)
                if b < 2:
                    key_weights_high(2 + b)

            def xt_high(k, banks, half, kts=range(KT)):
                for kt in kts:
                    s.wait_ge(xt_tr, 2 * k + kt + 1)
                    act_(XThi[:, kt, tile_cols(half, HALF)], bank[banks[kt]][:], ACT.Copy).then_inc(xt_hi, 1)

            keys_out(1, range(4), 4)
            xt_high(0, (0, 1), 0)
            keys_out(1, range(4, TILES), 4)
            xt_high(1, (2, 3), 1)
            s.wait_ge(lg_sub, 1)
            act_(lg[:], lg[:], ACT.Exp).then_inc(lg_exp, 1)
            with s.Fori(2, 4) as ck:
                keys_out(ck, range(TILES), 4)

            def activate(n2, h, free):
                s.wait_ge(g_mm, n2 + 1)
                if free:
                    s.wait_ge(h_ok, n2 - 1)
                act_(act[h][:], bank[4 + 2 * h][:], ACT.Silu).then_inc(silu, 1)

            def hidden_high(n2, h, free):
                s.wait_ge(h_ok, n2 + 1)
                if free:
                    s.wait_ge(down, n2 - 1)
                act_(hidhi[h][:], hid[h][:], ACT.Copy).then_inc(h_hi, 1)

            def split_high(it, t, m, free):
                s.wait_ge(w_ld[t], 16 * (m + 1))
                if free:
                    s.wait_ge(down, it * 2 - 4)
                act_(whi[t][:], wraw[t][:], ACT.Copy).then_inc(w_hi, 1)

            def moe_act(m, first=False, last=False):
                for t in range(PARTS):
                    it = m * PARTS + t
                    start = first and t == 0
                    for h in range(2):
                        if not start:
                            activate(it * 2 + h, h, True)
                        hidden_high(it * 2 + h, h, not start)
                    if not (last and t > 0):
                        nx = t + 2
                        split_high(it + 2, nx % PARTS, m + nx // PARTS, not start)

            for t in range(2):
                split_high(t, t, 0, False)
            for h in range(2):
                s.wait_ge(comb_tr, h + 1)
                act_(combT[:, tile_cols(h, HALF)], bank[1 + h][0:EXPERTS, :], ACT.Copy).then_inc(combT_out, 1)
            for h in range(2):
                activate(h, h, False)
            moe_act(0, first=True)
            with s.Fori(1, GROUPS - 1) as m:
                moe_act(m)
            moe_act(GROUPS - 1, last=True)

            def block_end(k, acc, scale):
                act_(OT[k % 2][:, 0, :], bank[acc][:], ACT.Copy, scale=scale).then_inc(ot_a, 1)

            for h in range(2):
                s.wait_ge(down, 2 * NIT - 1 + h)
                block_end(h, h, tg[:, 1:2])

            def head_product_high(j):
                s.wait_ge(pmm, j + 1)
                act_(PHhi[:, 2 * j:2 * j + 2, :].rearrange("p a b -> p (a b)"), bank[HPB[j]][:], ACT.Copy).then_inc(p_hi, 1)

            for j in range(4):
                head_product_high(j)
            act_(ctxhi[:], ctxn[:], ACT.Copy).then_inc(csp, 1)
            xt_high(2, (0, 2), 0)

            def keys_high(N):
                s.wait_ge(kt_tr, N + 1)
                act_(khi[:], bank[3][:], ACT.Copy, scale=gain[:, 0:1]).then_inc(k_hi, 1)

            def query_high(N):
                s.wait_ge(q_mm, N + 1)
                act_(qhi[:], bank[2][:], ACT.Copy).then_inc(q_hi, 1)
                act_(qsq[:], bank[2][:], ACT.Square).then_inc(q_sq, 1)

            def softmax_exp(N, par, b, first):
                s.wait_ge(s_bias, 2 * N + b + 1)
                if not first:
                    s.wait_ge(pt_tr, 2 * N - 3 + b)
                for i in range(2):
                    act_(Pm[par][:, b, i, :], bank[4 + b][:, tile_cols(i, SEQ)], ACT.Exp, bias=nbias[:, b, i:i + 1],
                         scale=qsc[par][:, 2 * b + i:2 * b + i + 1], accum_out=psumr[:, b, i:i + 1]).then_inc(s_exp, 1)

            def probs_high(N, b):
                s.wait_ge(pt_tr, 2 * N + b + 1)
                act_(PThi[:, b].rearrange("p a b -> p (a b)"), bank[6 + b][:], ACT.Copy).then_inc(pt_hi, 1)

            def out_high(N):
                s.wait_ge(av, N + 1)
                act_(ohi[:], bank[3][:], ACT.Copy).then_inc(o_hi, 1)

            def head_act(n, h, par, at):
                N = n + h * HEADS
                if at is None or at >= 2:
                    out_high(N - 2)
                softmax_exp(N, par, 0, at in (0, 1))
                if at != LAST:
                    keys_high(N + 1)
                if at in TURN:
                    k, kt = TURN[at]
                    xt_high(k, (2, 2), k % 2, [kt])
                if at == 0:
                    head_product_high(7)
                else:
                    probs_high(N - 1, 0)
                    probs_high(N - 1, 1)
                if at == HEADS + 1:
                    s.wait_ge(omm, HEADS)
                    block_end(2, 0, tg[:, 2:3])
                if at != LAST:
                    query_high(N + 1)
                softmax_exp(N, par, 1, at in (0, 1))

            keys_high(0)
            head_product_high(4)
            head_product_high(5)
            query_high(0)
            head_product_high(6)
            all_heads(s, head_act)
            out_high(LAST - 1)
            for b in range(2):
                probs_high(LAST, b)
            out_high(LAST)
            s.wait_ge(omm, 2 * HEADS)
            block_end(3, 0, tg[:, 2:3])

            def ff_act(H, i):
                k = H * (FFT + 1) + i
                G, U = 4 + 2 * (i % 2), 5 + 2 * (i % 2)
                s.wait_ge(f_g, k + 1)
                if k >= 2:
                    s.wait_ge(f_h, k - 1)
                if i < FFT:
                    act_(act[i % 2][:], bank[G][:], ACT.Silu, scale=cols[:, GS + i:GS + i + 1]).then_inc(f_silu, 1)
                else:
                    act_(act[i % 2][FFR:2 * FFR, :], bank[G][0:FFR, :], ACT.Silu,
                         scale=cols[0:FFR, TAIL:NCOLS]).then_inc(f_silu, 1)

            def ff_high(H, i):
                k = H * (FFT + 1) + i
                s.wait_ge(f_h, k + 1)
                if k >= 2:
                    s.wait_ge(f_down, k - 1)
                r = slice(0, P) if i < FFT else slice(FFR, 2 * FFR)
                act_(hidhi[i % 2][r, :], hid[i % 2][r, :], ACT.Copy).then_inc(f_hi, 1)

            for k in range(2 * (FFT + 1)):
                ff_act(k // (FFT + 1), k % (FFT + 1))
                ff_high(k // (FFT + 1), k % (FFT + 1))
                if k == 3:
                    xt_high(5, (2, 3), 1)
                if k == FFT + 1:
                    s.wait_ge(f_down, FFT + 1)
                    block_end(4, 0, dscale[:, 0:1])
            s.wait_ge(f_down, 2 * (FFT + 1))
            block_end(5, 0, dscale[:, 0:1])

        @block.vector
        def _(v):
            V = nc.vector
            ch = [0]

            def step(ins):
                ins.then_inc(vch, 1)
                ch[0] += 1

            def settle():
                v.wait_ge(vch, ch[0])

            lnk = [0]

            def ln_stats(tt):
                for t in (tt, tt + 1):
                    step(V.bn_stats(stats[:, t, :], x[:, t, :]))
                settle()
                V.bn_aggr(mv[:, tt, :], stats[:, tt, :]).then_inc(vch, 1)
                V.bn_aggr(mv[:, tt + 1, :], stats[:, tt + 1, :]).then_inc(ln_var, 1)
                ch[0] += 1
                settle()

            def ln_apply(k, tt):
                v.wait_ge(ln_rstd, k + 1)
                for t in (tt, tt + 1):
                    V.tensor_scalar(xln[:, t, :], x[:, t, :], mv[:, t, 0:1], rstd[:, t:t + 1],
                                    ALU.subtract, ALU.mult).then_inc(ln_out, 1)

            def xt_low(k, banks, half, kts=range(KT)):
                for kt in kts:
                    v.wait_ge(xt_hi, 2 * k + kt + 1)
                    c = tile_cols(half, HALF)
                    V.tensor_tensor(XTlo[:, kt, c], bank[banks[kt]][:], f32(XThi[:, kt, c]), ALU.subtract).then_inc(xt_lo, 1)

            v.wait_ge(ld_small, 64)
            step(V.scalar_tensor_tensor(out=gain[:], in0=cols[:, GQ:GQ + 1], scalar=float(HD) ** 0.5,
                                        in1=cols[:, GK:GK + 1], op0=ALU.mult, op1=ALU.mult))
            for h in range(2):
                v.wait_ge(proj, 2 * h + 2)
                V.tensor_scalar(k0[:, tile_cols(h, HALF)], bank[2 + h][:], cols[:, BK:BK + 1], None, ALU.add).then_inc(k0_out, 1)
            v.wait_ge(ld_x[0], 16)
            v.wait_ge(ld_x[1], 16)
            ln_stats(0)
            for b in range(BATCH):
                v.wait_ge(energy, b + 1)
                V.tensor_reduce(nmax[:, 2 * b:2 * b + 2], bank[4 + b][:].rearrange("p (i m) -> p i m", i=2), AX.X, ALU.max,
                                negate=True).then_inc(a_max, 1)
                if b:
                    ln_stats(2 * b)

            def normalise(b):
                v.wait_ge(a_exp, 2 * b + 2)
                step(V.reciprocal(rsum[:, 2 * b:2 * b + 2], asum[:, 2 * b:2 * b + 2]))
                settle()
                for i in range(2):
                    tt = 2 * b + i
                    V.tensor_scalar(A[:, tt, :], A[:, tt, :], rsum[:, tt:tt + 1], None, ALU.mult).then_inc(a_norm, 1)

            def add_mix(b):
                v.wait_ge(mix, b + 1)
                xb = x[:, 2 * b:2 * b + 2, :].rearrange("p a b -> p (a b)")
                V.scalar_tensor_tensor(out=xb, in0=bank[b][:], scalar=tg[:, 0:1], in1=xb, op0=ALU.mult,
                                       op1=ALU.add).then_inc(x_new, 1)
                v.wait_ge(x_new, b + 1)
                ln_stats(2 * b)

            v.wait_ge(tgr, 1)
            step(V.tensor_scalar(dscale[:], cols[:, DS:DS + 2], tg[:, 3:4], None, ALU.mult))
            for b in range(BATCH):
                ln_apply(b, 2 * b)
                normalise(b)
                if b == BATCH - 2:
                    add_mix(0)
            v.wait_ge(ld_gw, 16)
            step(V.tensor_copy(gwhi[:], gwraw[:]))
            settle()
            V.tensor_tensor(gwlo[:], gwraw[:], f32(gwhi[:]), ALU.subtract).then_inc(gws, 1)
            for b in range(1, BATCH):
                add_mix(b)
                ln_apply(4 + b - 1, 2 * b - 2)
            ln_apply(7, 6)
            xt_low(0, (0, 1), 0)
            xt_low(1, (2, 3), 1)

            def bc(ap, shape):
                return ap.unsqueeze(2).broadcast_to(shape)

            v.wait_ge(logits, TILES)
            step(V.tensor_copy(lg[:].rearrange("p a b -> p (a b)"), bank[0][:, 0:TILES * EXPERTS]))
            settle()
            step(V.tensor_reduce(s8[:], lg[:], AX.X, ALU.max))
            settle()
            V.tensor_tensor(lg[:], lg[:], bc(s8[:], [P, TILES, EXPERTS]), ALU.subtract).then_inc(lg_sub, 1)
            step(V.memset(keep8[:], 1.0))
            step(V.memset(iota32[:], 1.0))
            settle()
            step(V.memset(keep8[:, :, 0:1], 0.0))
            step(V.tensor_tensor_scan(iota32[:], iota32[:], iota32[:], -1.0, ALU.mult, ALU.add))
            settle()
            v.wait_ge(lg_exp, 1)
            step(V.tensor_reduce(s8[:], lg[:], AX.X, ALU.add))
            settle()
            step(V.reciprocal(r8[:], s8[:]))
            settle()
            step(V.tensor_tensor(lg[:], lg[:], bc(r8[:], [P, TILES, EXPERTS]), ALU.mult))
            settle()
            for tt in range(TILES):
                step(V.max(top8[:, tt, :], lg[:, tt, :]))
            settle()
            for tt in range(TILES):
                step(V.max_index(idx8[:, tt, :], top8[:, tt, :], lg[:, tt, :]))
            step(V.tensor_reduce(s8[:], top8[:], AX.X, ALU.add))
            settle()
            step(V.tensor_scalar(s8[:], s8[:], 1e-12, None, ALU.max))
            step(V.tensor_copy(idxf[:], idx8[:]))
            settle()
            step(V.reciprocal(r8[:], s8[:]))
            settle()
            step(V.tensor_tensor(ren8[:], top8[:], bc(r8[:], E8), ALU.mult))
            settle()
            step(V.tensor_tensor_scan(cum8[:].rearrange("p a b -> p (a b)"), keep8[:].rearrange("p a b -> p (a b)"),
                                      ren8[:].rearrange("p a b -> p (a b)"), 0.0, ALU.mult, ALU.add))
            settle()
            step(V.tensor_scalar(cum8[:], cum8[:], THRESHOLD, None, ALU.is_lt))
            settle()
            step(V.tensor_reduce(s8[:], cum8[:], AX.X, ALU.add))
            settle()
            step(V.tensor_scalar(s8[:], s8[:], 1.0, float(TOPK), ALU.add, ALU.min))
            settle()
            step(V.tensor_tensor(cum8[:], iota32[:, 0:TOPK].unsqueeze(1).broadcast_to(E8), bc(s8[:], E8), ALU.is_lt))
            settle()
            step(V.tensor_tensor(rw8[:], top8[:], cum8[:], ALU.mult))
            settle()
            step(V.tensor_reduce(s8[:], rw8[:], AX.X, ALU.add))
            settle()
            step(V.tensor_scalar(s8[:], s8[:], 1e-12, None, ALU.max))
            settle()
            step(V.reciprocal(r8[:], s8[:]))
            settle()
            step(V.tensor_tensor(rw8[:], rw8[:], bc(r8[:], E8), ALU.mult))
            settle()
            full = [P, TILES, EXPERTS, TOPK]
            step(V.tensor_tensor(eq[:], idxf[:].unsqueeze(2).broadcast_to(full),
                                 iota32[:].unsqueeze(1).unsqueeze(3).broadcast_to(full), ALU.is_equal))
            settle()
            step(V.tensor_tensor(eq[:], eq[:], rw8[:].unsqueeze(2).broadcast_to(full), ALU.mult))
            settle()
            V.tensor_reduce(comb[:], eq[:], AX.X, ALU.add).then_inc(comb_ok, 1)

            def hidden(m, n2, h):
                v.wait_ge(silu, n2 + 1)
                V.tensor_tensor(act[h][:], act[h][:], CE[:, bass.ds(m, 1), tile_cols(h, HALF)].rearrange("p a b -> p (a b)"),
                                ALU.mult).then_inc(weighted, 1)
                v.wait_ge(u_mm, n2 + 1)
                v.wait_ge(weighted, n2 + 1)
                V.tensor_tensor(hid[h][:], bank[5 + 2 * h][:], act[h][:], ALU.mult).then_inc(h_ok, 1)

            def hidden_low(n2, h):
                v.wait_ge(h_hi, n2 + 1)
                V.tensor_tensor(hidlo[h][:], hid[h][:], f32(hidhi[h][:]), ALU.subtract).then_inc(h_lo, 1)

            def key_sums(m, c):
                v.wait_ge(sq_ok, m * 4 + c + 1)
                V.tensor_reduce(kst[:], ksq[:].rearrange("p (h d) -> p h d", d=HD), AX.X, ALU.add).then_inc(sq_raw, 1)
                v.wait_ge(sq_raw, m * 4 + c + 1)
                V.tensor_scalar(kss[:, bass.ds(m, 1), c * 4:(c + 1) * 4].rearrange("p a b -> p (a b)"), kst[:],
                                HD * EPS, None, ALU.add).then_inc(sq_sum, 1)

            def moe_vec(m, last=False):
                v.wait_ge(ce_ld, 16 * (m + 1))
                for t in range(PARTS):
                    for h in range(2):
                        n2 = (m * PARTS + t) * 2 + h
                        hidden(m, n2, h)
                        if not last and (h == 0 or t == PARTS - 1):
                            key_sums(m + 1, t + h)
                        hidden_low(n2, h)

            for c in range(4):
                key_sums(0, c)
            with v.Fori(0, GROUPS - 1) as m:
                moe_vec(m)
            moe_vec(GROUPS - 1, last=True)

            def block_end(k, acc, scale):
                V.tensor_scalar(OT[k % 2][:, 1, :], bank[acc][:], scale, None, ALU.mult).then_inc(ot_v, 1)

            def residual(k, i, b):
                tt = (k % 2) * HTILES + 2 * i
                v.wait_ge(ot_tr, 2 * k + i + 1)
                xb = x[:, tt:tt + 2, :].rearrange("p a b -> p (a b)")
                V.tensor_tensor(xb, bank[b][:], xb, ALU.add).then_inc(x_new, 1)
                if k < 4:
                    v.wait_ge(x_new, 4 + 2 * k + i + 1)
                    ln_stats(tt)

            def ln_half(k):
                for i in range(2):
                    ln_apply(2 * k + 4 + i, (k % 2) * HTILES + 2 * i)

            for h in range(2):
                v.wait_ge(down, 2 * NIT - 1 + h)
                block_end(h, 2 + h, tg[:, 1:2])

            def head_product_low(j):
                v.wait_ge(p_hi, j + 1)
                ph = PHhi[:, 2 * j:2 * j + 2, :].rearrange("p a b -> p (a b)")
                pl = PHlo[:, 2 * j:2 * j + 2, :].rearrange("p a b -> p (a b)")
                V.tensor_tensor(pl, bank[HPB[j]][:], f32(ph), ALU.subtract).then_inc(p_lo, 1)

            def query_weights_high(N, ld):
                v.wait_ge(wq_ld, ld)
                if not (isinstance(N, int) and N == 0):
                    v.wait_ge(q_mm, N)
                w = wqhi[:].rearrange("p a b -> p (a b)")
                V.tensor_copy(w, wqraw[:]).then_inc(wq_h, 1)

            def keys_low(N):
                v.wait_ge(k_hi, N + 1)
                V.scalar_tensor_tensor(out=klo[:], in0=bank[3][:], scalar=gain[:, 0:1], in1=f32(khi[:]),
                                       op0=ALU.mult, op1=ALU.subtract).then_inc(k_lo, 1)

            def query_low(N):
                v.wait_ge(q_sq, N + 1)
                V.tensor_tensor(qlo[:], bank[2][:], f32(qhi[:]), ALU.subtract).then_inc(q_lo, 1)

            def query_squares(N):
                v.wait_ge(q_ss, N + 1)
                V.tensor_scalar(qss[:], bank[6][:, 0:HTILES], HD * EPS, None, ALU.add).then_inc(q_ssout, 1)

            def softmax_bias(N, par, b):
                v.wait_ge(s_mm, 2 * N + b + 1)
                V.tensor_reduce(smax[:, b, :], bank[4 + b][:].rearrange("p (i m) -> p i m", i=2), AX.X,
                                ALU.max).then_inc(s_max, 1)
                v.wait_ge(s_max, 2 * N + b + 1)
                v.wait_ge(q_sc, N + 1)
                V.scalar_tensor_tensor(out=nbias[:, b, :], in0=smax[:, b, :], scalar=-1.0, in1=qsc[par][:, 2 * b:2 * b + 2],
                                       op0=ALU.mult, op1=ALU.mult).then_inc(s_bias, 1)

            def softmax_recip(N, par, b):
                v.wait_ge(s_exp, 4 * N + 2 * b + 2)
                V.reciprocal(prec[par][:, b, :], psumr[:, b, :]).then_inc(s_rec, 1)

            def probs_low(N, b):
                v.wait_ge(pt_hi, 2 * N + b + 1)
                V.tensor_tensor(PTlo[:, b].rearrange("p a b -> p (a b)"), bank[6 + b][:],
                                f32(PThi[:, b].rearrange("p a b -> p (a b)")), ALU.subtract).then_inc(pt_lo, 1)

            def out_low(N):
                v.wait_ge(o_hi, N + 1)
                V.tensor_tensor(olo[:], bank[3][:], f32(ohi[:]), ALU.subtract).then_inc(o_lo, 1)

            flat = "p a b -> p (a b)"

            def head_vec(n, h, par, at):
                N = n + h * HEADS
                if at in (HEADS - 2, LAST - 1):
                    ln_half(TURN[at][0])
                if at is None or at >= 2:
                    out_low(N - 2)
                softmax_bias(N, par, 0)
                softmax_bias(N, par, 1)
                if at != LAST:
                    keys_low(N + 1)
                if at in BACK:
                    residual(*BACK[at], 2)
                if at in TURN:
                    k, kt = TURN[at]
                    xt_low(k, (2, 2), k % 2, [kt])
                if at == 0:
                    head_product_low(7)
                else:
                    probs_low(N - 1, 0)
                    probs_low(N - 1, 1)
                softmax_recip(N, par, 0)
                if at == HEADS + 1:
                    v.wait_ge(omm, HEADS)
                    block_end(2, 1, tg[:, 2:3])
                if at != LAST:
                    query_low(N + 1)
                    query_squares(N + 1)
                if at is None or at + 2 <= LAST:
                    query_weights_high(N + 2, 16 * (N + 3))
                if h == 1 and at is None:
                    v.wait_ge(ld_ff, 32)
                    c = bass.ts(n - 2, PIECE)
                    V.tensor_copy(wfhi[:].rearrange(flat)[:, c], wff[:].rearrange(flat)[:, c]).then_inc(ff_hi, 1)
                if at == 2 * HEADS - 4:
                    V.tensor_copy(wfhi[:, WFT - 1, :], wff[:, WFT - 1, :]).then_inc(ff_hi, 1)
                    V.tensor_copy(wfhi[FFR:2 * FFR, WFT, :], wff[FFR:2 * FFR, WFT, :]).then_inc(ff_hi, 1)
                softmax_recip(N, par, 1)

            query_weights_high(0, 16)
            residual(0, 0, 0)
            residual(0, 1, 2)
            head_product_low(0)
            ln_half(2)
            for j in range(1, 4):
                head_product_low(j)
            xt_low(2, (0, 2), 0)
            keys_low(0)
            head_product_low(4)
            head_product_low(5)
            query_low(0)
            query_weights_high(1, 32)
            head_product_low(6)
            query_squares(0)
            all_heads(v, head_vec)
            out_low(LAST - 1)
            for b in range(2):
                probs_low(LAST, b)
            out_low(LAST)
            v.wait_ge(omm, 2 * HEADS)
            block_end(3, 1, tg[:, 2:3])

            def ff_vec(H, i):
                k = H * (FFT + 1) + i
                G, U = 4 + 2 * (i % 2), 5 + 2 * (i % 2)
                if i < FFT:
                    v.wait_ge(f_u, H * FFT + i + 1)
                v.wait_ge(f_silu, k + 1)
                if k >= 2:
                    v.wait_ge(f_hi, k - 1)
                if i < FFT:
                    V.scalar_tensor_tensor(out=hid[i % 2][:], in0=bank[U][:], scalar=cols[:, US + i:US + i + 1],
                                           in1=act[i % 2][:], op0=ALU.mult, op1=ALU.mult).then_inc(f_h, 1)
                else:
                    r = slice(FFR, 2 * FFR)
                    V.scalar_tensor_tensor(out=hid[i % 2][r, :], in0=bank[G][r, :], scalar=cols[r, TAIL:NCOLS],
                                           in1=act[i % 2][r, :], op0=ALU.mult, op1=ALU.mult).then_inc(f_h, 1)
                v.wait_ge(f_hi, k + 1)
                r = slice(0, P) if i < FFT else slice(FFR, 2 * FFR)
                V.tensor_tensor(hidlo[i % 2][r, :], hid[i % 2][r, :], f32(hidhi[i % 2][r, :]), ALU.subtract).then_inc(f_lo, 1)

            for k in range(2 * (FFT + 1)):
                ff_vec(k // (FFT + 1), k % (FFT + 1))
                if k == 0:
                    residual(3, 0, 2)
                    residual(3, 1, 3)
                if k == 1:
                    ln_half(5)
                if k == 3:
                    xt_low(5, (2, 3), 1)
                if k == FFT + 1:
                    v.wait_ge(f_down, FFT + 1)
                    block_end(4, 1, dscale[:, 1:2])
                if k == FFT + 3:
                    residual(4, 0, 2)
                    residual(4, 1, 3)
            v.wait_ge(f_down, 2 * (FFT + 1))
            block_end(5, 1, dscale[:, 1:2])
            residual(5, 0, 4)
            residual(5, 1, 5)

        @block.tensor
        def _(pe):
            mm, tr = nc.tensor.matmul, nc.tensor.transpose
            pe.wait_ge(ld_ctxT, 32)
            for j in (0, 2, 1, 3):
                mm(bank[j][:], w0[:, tile_cols(j // 2)], ctxT[:, tile_cols(j % 2, HALF)],
                   start=True, stop=True).then_inc(proj, 1)
            for b in range(BATCH):
                pe.wait_ge(q0_out, b // 2 + 1)
                pe.wait_ge(k0_out, b // 2 + 1)
                for i in range(2):
                    ins = mm(bank[4 + b][:, tile_cols(i, SEQ)], q0[:, tile_cols(2 * b + i)], k0[:, tile_cols(b, SEQ)],
                             start=True, stop=True)
                ins.then_inc(energy, 1)

            def key_tiles(ck, tts, first):
                for tt in tts:
                    if not (isinstance(ck, int) and ck == 0 and tt < 4):
                        pe.wait_ge(k_out, ck * TILES + tt - 3)
                    c = tile_cols(tt)
                    three(mm, bank[first + tt % 4][:], ctxThi[:, c], ctxTlo[:, c], wkhi[:, bass.ts(ck, 512)],
                          wklo[:, bass.ts(ck, 512)], True, True).then_inc(kmm, 1)

            pe.wait_ge(csp_p, 2)
            key_tiles(0, range(TILES), 0)
            pe.wait_ge(const, 4)

            def mix_in(b):
                pe.wait_ge(xt0_out, b + 1)
                pe.wait_ge(at_out, b + 1)
                for i in range(2):
                    for j in range(2):
                        ins = mm(bank[b][:, tile_cols(i, SEQ)], XT0[:, b, j, tile_cols(i)], AT[:, b, j, :],
                                 start=(j == 0), stop=(j == 1))
                ins.then_inc(mix, 1)

            for b in range(BATCH):
                pe.wait_ge(ln_out, 2 * b + 2)
                pe.wait_ge(a_exp, 2 * b + 2)
                for j in range(2):
                    for i in range(2):
                        ins = tr(bank[4 + b][:, j * SEQ + i * P:j * SEQ + (i + 1) * P], xln[:, 2 * b + i, tile_cols(j)], ident[:])
                ins.then_inc(xt0_tr, 1)
                pe.wait_ge(a_norm, 2 * b + 2)
                pe.wait_ge(k_out, 4 + b + 1)
                for j in range(2):
                    for i in range(2):
                        ins = tr(bank[b][:, j * SEQ + i * P:j * SEQ + (i + 1) * P], A[:, 2 * b + i, tile_cols(j)], ident[:])
                ins.then_inc(at_tr, 1)
                if b:
                    mix_in(b - 1)
            mix_in(BATCH - 1)

            def xt_transpose(k, banks, half, kts=range(KT)):
                pe.wait_ge(ln_out, 8 + 4 * k + 4)
                for kt in kts:
                    for i in range(HTILES):
                        ins = tr(bank[banks[kt]][:, tile_cols(i)], xln[:, half * HTILES + i, tile_cols(kt)], ident[:])
                    ins.then_inc(xt_tr, 1)

            pe.wait_ge(csp_p, 5)
            key_tiles(1, range(4), 4)
            pe.wait_ge(x_new, 2)
            xt_transpose(0, (0, 1), 0)
            key_tiles(1, range(4, TILES), 4)
            pe.wait_ge(x_new, 4)
            xt_transpose(1, (2, 3), 1)
            pe.wait_ge(gws, 1)
            for tt in range(TILES):
                pe.wait_ge(xt_lo, 2 if tt < HTILES else 4)
                for kt in range(KT):
                    ins = three(mm, bank[0][:, tile_cols(tt, EXPERTS)], XThi[:, kt, tile_cols(tt)], XTlo[:, kt, tile_cols(tt)],
                                gwhi[:, kt, :], gwlo[:, kt, :], kt == 0, kt == KT - 1)
                ins.then_inc(logits, 1)
            with pe.Fori(2, 4) as ck:
                key_tiles(ck, range(TILES), 4)

            def gate_up(it, t, h, first):
                n2 = it * 2 + h
                c = tile_cols(h, HALF)
                if h == 0:
                    pe.wait_ge(w_lo, it + 1)
                for j, free in ((0, silu), (1, h_ok)):
                    if not first:
                        pe.wait_ge(free, n2 - 1)
                    for kt in range(KT):
                        w = slice((kt * 2 + j) * P, (kt * 2 + j + 1) * P)
                        ins = three(mm, bank[4 + 2 * h + j][:], whi[t][:, w], wlo[t][:, w], XThi[:, kt, c], XTlo[:, kt, c],
                                    kt == 0, kt == KT - 1)
                    ins.then_inc(u_mm if j else g_mm, 1)

            def down_half(it, t, h, last):
                n2 = it * 2 + h
                pe.wait_ge(h_lo, n2 + 1)
                for o in range(OT_):
                    w = slice(2 * DIM + o * P, 2 * DIM + (o + 1) * P)
                    ins = three(mm, bank[2 * o + h][:], whi[t][:, w], wlo[t][:, w], hidhi[h][:], hidlo[h][:], False, last)
                ins.then_inc(down, 1)

            pe.wait_ge(k_out, 32)
            pe.wait_ge(comb_ok, 1)
            for hh in range(2):
                for i in range(HTILES):
                    ins = tr(bank[1 + hh][0:EXPERTS, tile_cols(i)], comb[:, hh * HTILES + i, :], ident[:])
                ins.then_inc(comb_tr, 1)
            gate_up(0, 0, 0, True)
            gate_up(0, 0, 1, True)
            pe.wait_ge(combT_out, 2)
            for j in range(4):
                mm(bank[j][:], zeros[:, 0:P], zeros[:], start=True, stop=False, skip_group_check=True)

            def moe_pe(m, last=False):
                for t in range(PARTS):
                    it = m * PARTS + t
                    end = last and t == PARTS - 1
                    for h in range(2):
                        if not end:
                            gate_up(it + 1, (t + 1) % PARTS, h, False)
                        down_half(it, t, h, end)

            with pe.Fori(0, GROUPS - 1) as m:
                moe_pe(m)
            moe_pe(GROUPS - 1, last=True)

            def block_back(k, i, b):
                pe.wait_ge(ot_a, k + 1)
                pe.wait_ge(ot_v, k + 1)
                for j in range(2):
                    for o in range(OT_):
                        ins = tr(bank[b][:, j * DIM + o * P:j * DIM + (o + 1) * P],
                                 OT[k % 2][:, o, tile_cols(2 * i + j)], ident[:])
                ins.then_inc(ot_tr, 1)

            def head_product(j):
                for i in range(2):
                    ins = mm(bank[HPB[j]][:, tile_cols(i, DIM)], wv[:, 2 * j + i, :], wo[:, 2 * j + i, :],
                             start=True, stop=True)
                ins.then_inc(pmm, 1)

            block_back(0, 0, 0)
            block_back(0, 1, 2)
            pe.wait_ge(ld_v, 32)
            pe.wait_ge(weighted, 2 * NIT)
            for j in range(4):
                head_product(j)
            pe.wait_ge(x_new, 6)
            xt_transpose(2, (0, 2), 0)

            def keys_T(N):
                pe.wait_ge(kn_ok, N + 1)
                for i in range(HTILES):
                    ins = tr(bank[3][:, tile_cols(i)], kn[:, i, :], ident[:])
                ins.then_inc(kt_tr, 1)

            def queries(N, H):
                pe.wait_ge(wq_s, N + 1)
                c = tile_cols(H, HALF)
                for kt in range(KT):
                    ins = three(mm, bank[2][:], wqhi[:, kt, :], wqlo[:, kt, :], XThi[:, kt, c], XTlo[:, kt, c],
                                kt == 0, kt == KT - 1)
                ins.then_inc(q_mm, 1)

            def query_squares(N):
                pe.wait_ge(q_sq, N + 1)
                for i in range(HTILES):
                    ins = mm(bank[6][:, i:i + 1], qsq[:, tile_cols(i)], ones[:], start=True, stop=True)
                ins.then_inc(q_ss, 1)

            def scores(N):
                pe.wait_ge(k_lo, N + 1)
                pe.wait_ge(q_lo, N + 1)
                for b in range(2):
                    if not (isinstance(N, int) and N == 0):
                        pe.wait_ge(s_exp, 4 * N - 2 + 2 * b)
                    kc = tile_cols(b, SEQ)
                    for i in range(2):
                        qc = tile_cols(2 * b + i)
                        ins = three(mm, bank[4 + b][:, tile_cols(i, SEQ)], qhi[:, qc], qlo[:, qc], khi[:, kc], klo[:, kc],
                                    True, True)
                    ins.then_inc(s_mm, 1)

            def at_last(N):
                return isinstance(N, int) and N == LAST

            def probs_T(N, par):
                for b in range(2):
                    pe.wait_ge(s_norm, 2 * N + b + 1)
                    if b == 0:
                        pe.wait_ge(q_ssout, 2 * HEADS if at_last(N) else N + 2)
                    if not (isinstance(N, int) and N == 0):
                        pe.wait_ge(pt_lo, 2 * N - 1 + b)
                    for j in range(2):
                        for i in range(2):
                            ins = tr(bank[6 + b][:, j * SEQ + i * P:j * SEQ + (i + 1) * P], Pm[par][:, b, i, tile_cols(j)], ident[:])
                    ins.then_inc(pt_tr, 1)

            def weighted_context(N, H):
                pe.wait_ge(k_lo, 2 * HEADS if isinstance(N, int) and N + 2 > LAST else N + 3)
                for b in range(2):
                    pe.wait_ge(pt_lo, 2 * N + b + 1)
                    for j in range(2):
                        tt = H * HTILES + 2 * b + j
                        ins = three(mm, bank[3][:, tile_cols(b, SEQ)], ctxhi[:, tt, :], ctxlo[:, tt, :],
                                    PThi[:, b, j, :], PTlo[:, b, j, :], j == 0, j == 1)
                ins.then_inc(av, 1)

            def head_output(N, last):
                pe.wait_ge(o_lo, N + 1)
                pe.wait_ge(ph_ld, 32 * (N + 1))
                for o in range(OT_):
                    ins = three(mm, bank[o][:], phhi[:, tile_cols(o)], phlo[:, tile_cols(o)], ohi[:], olo[:], False, last)
                ins.then_inc(omm, 1)

            def open_output():
                for o in range(OT_):
                    mm(bank[o][:], zeros[:, 0:P], zeros[:], start=True, stop=False, skip_group_check=True)

            def head_pe(n, h, par, at):
                N = n + h * HEADS
                scores(N)
                if at != LAST:
                    if at not in (0, 1):
                        pe.wait_ge(o_lo, N - 1)
                    keys_T(N + 1)
                if at not in (0, 1):
                    head_output(N - 2, at == HEADS + 1)
                if at in BACK:
                    block_back(*BACK[at], 2)
                if at in TURN:
                    k, kt = TURN[at]
                    xt_transpose(k, (2, 2), k % 2, [kt])
                if at == 0:
                    head_product(7)
                else:
                    probs_T(N - 1, 1 - par)
                if at in BACK:
                    k, piece = BACK[at]
                    pe.wait_ge(x_new, 4 + 2 * k + piece + 1)
                if at in TURN:
                    k, kt = TURN[at]
                    pe.wait_ge(xt_lo, 2 * k + kt + 1)
                if at != LAST:
                    queries(N + 1, ahead(n, h, 1)[1])
                if at != 0:
                    weighted_context(N - 1, ahead(n, h, -1)[1])
                if at != LAST:
                    query_squares(N + 1)
                if at == HEADS + 1:
                    pe.wait_ge(ot_a, 3)
                    pe.wait_ge(ot_v, 3)
                    open_output()

            pe.wait_ge(ot_a, 2)
            pe.wait_ge(ot_v, 2)
            keys_T(0)
            for j in (4, 5):
                pe.wait_ge(p_lo, j - 3)
                head_product(j)
            pe.wait_ge(xt_lo, 6)
            queries(0, 0)
            open_output()
            pe.wait_ge(p_lo, 4)
            head_product(6)
            query_squares(0)
            pe.wait_ge(csp, 2)
            pe.wait_ge(p_lo, 7)
            all_heads(pe, head_pe)
            head_output(LAST - 1, False)
            probs_T(LAST, 1)
            weighted_context(LAST, 1)
            head_output(LAST, True)

            def ff_gate_up(H, i):
                k = H * (FFT + 1) + i
                G, U = 4 + 2 * (i % 2), 5 + 2 * (i % 2)
                if k >= 2:
                    pe.wait_ge(f_h, k - 1)
                c = tile_cols(H, HALF)
                for j in range(2 if i < FFT else 1):
                    for kt in range(KT):
                        ins = three(mm, bank[(G, U)[j]][:], wfhi[:, 2 * i + j, tile_cols(kt)], wflo[:, 2 * i + j, tile_cols(kt)],
                                    XThi[:, kt, c], XTlo[:, kt, c], kt == 0, kt == KT - 1)
                    ins.then_inc((f_g, f_u)[j], 1)

            def ff_down(H, i):
                k = H * (FFT + 1) + i
                pe.wait_ge(f_lo, k + 1)
                r = slice(0, P) if i < FFT else slice(FFR, 2 * FFR)
                t = 2 * FFT + 1 + i
                for o in range(OT_):
                    low = wflo[:, t, tile_cols(o)] if i < FFT - 1 else wflo2[r, i - FFT + 1, tile_cols(o)]
                    ins = three(mm, bank[o][:], wfhi[r, t, tile_cols(o)], low,
                                hidhi[i % 2][r, :], hidlo[i % 2][r, :], i == 0, i == FFT)
                ins.then_inc(f_down, 1)

            pe.wait_ge(ff_lo, 12)
            ff_gate_up(0, 0)
            ff_gate_up(0, 1)
            pe.wait_ge(xt_lo, 10)
            block_back(3, 0, 2)
            block_back(3, 1, 3)
            for k in range(2 * (FFT + 1)):
                if k == FFT + 1:
                    pe.wait_ge(ot_a, 5)
                    pe.wait_ge(ot_v, 5)
                ff_down(k // (FFT + 1), k % (FFT + 1))
                if k + 2 < 2 * (FFT + 1):
                    if k + 2 == FFT + 1:
                        pe.wait_ge(xt_lo, 12)
                    ff_gate_up((k + 2) // (FFT + 1), (k + 2) % (FFT + 1))
                if k == 2:
                    pe.wait_ge(x_new, 12)
                    xt_transpose(5, (2, 3), 1)
                if k == FFT + 2:
                    block_back(4, 0, 2)
                    block_back(4, 1, 3)
            block_back(5, 0, 4)
            block_back(5, 1, 5)


def kernel(**inputs):
    import numpy as np
    import concourse.bacc as bacc
    from concourse.bass_utils import run_bass_kernel_spmd as run

    a = {k: np.asarray(v) for k, v in inputs.items()}
    T = np.ascontiguousarray
    ctx_tok = a["ctx_1024"].reshape(TOK, CDIM)
    gu = a["L0_ffn_gate_up_proj"].reshape(GROUPS, GROUP, 2, PARTS, 32, KT, P).transpose(0, 3, 6, 5, 2, 1, 4)
    dn = a["L0_ffn_down_proj"].reshape(GROUPS, GROUP, DIM, PARTS, 32).transpose(0, 3, 1, 4, 2)
    moe = np.concatenate([gu.reshape(GROUPS * PARTS * P, 2 * DIM), dn.reshape(GROUPS * PARTS * P, DIM)], axis=1)
    gT, uT = a["L1_ffn_gate_w"].T, a["L1_ffn_up_w"].T
    tiles = []
    for i in range(FFT):
        tiles += [gT[:, i * P:(i + 1) * P], uT[:, i * P:(i + 1) * P]]
    tiles.append(np.concatenate([gT[:, FFT * P:], uT[:, FFT * P:]], axis=1))
    w13 = np.stack([t.reshape(KT, P, P) for t in tiles]).transpose(2, 0, 1, 3).reshape(P, -1)
    dT = a["L1_ffn_down_w"].T
    cols = np.concatenate([
        a["L0_xattn_bq"][:, None], a["L0_xattn_bk"][:, None], a["L1_xattn_gq"][:, None], a["L1_xattn_gk"][:, None],
        a["L1_ffn_down_s"].reshape(2, P).T, a["L1_ffn_gate_s"][:FFT * P].reshape(FFT, P).T,
        a["L1_ffn_up_s"][:FFT * P].reshape(FFT, P).T], axis=1)
    arrays = {
        "x": a["x"].reshape(TOK, DIM),
        "ctxn": ctx_tok,
        "ctxT": ctx_tok.T,
        "w0": np.concatenate([a["L0_xattn_Wq"].T, a["L0_xattn_Wk"].T], axis=1),
        "cols": cols,
        "tailg": a["L1_ffn_gate_s"][FFT * P:, None],
        "tailu": a["L1_ffn_up_s"][FFT * P:, None],
        "gates": np.stack([a["g_xattn"][0], a["g_ffn"][0], a["g_xattn"][1], a["g_ffn"][1]]),
        "gw": a["L0_ffn_gate_weight"].T,
        "moe": moe,
        "wq": a["L1_xattn_Wq"].reshape(KT, P, HEADS, HD).transpose(1, 2, 0, 3).reshape(P, -1),
        "wk": a["L1_xattn_Wk"],
        "wv": a["L1_xattn_Wv"].reshape(CDIM, HEADS, HD).transpose(2, 1, 0).reshape(P, -1),
        "wo": a["L1_xattn_Wo"].reshape(HEADS, HD, DIM).transpose(1, 0, 2).reshape(P, -1),
        "wff": np.concatenate([w13, dT[:FFT * P].reshape(FFT, P, DIM).transpose(1, 0, 2).reshape(P, -1)], axis=1),
        "w2t": dT[FFT * P:],
    }
    arrays = {f"in_{k}": T(v) for k, v in arrays.items()}
    nc = bacc.Bacc("TRN2", target_bir_lowering=False, num_devices=1)
    args = [nc.dram_tensor(k, v.shape, F32, kind="ExternalInput").ap() for k, v in arrays.items()]
    args.append(nc.dram_tensor("result", (TOK, DIM), F32, kind="ExternalOutput").ap())
    args.append(nc.dram_tensor("combine", (EXPERTS, TOK), F32, kind="Internal").ap())
    flamingo(nc, *args)
    r = run(nc, [arrays], core_ids=[0])
    return r.results[0]["result"].reshape(BATCH, SEQ, DIM)
```

```python
from contextlib import ExitStack

import concourse.bass as bass
from concourse import mybir

P = 128
BATCH, SEQ, DIM, CDIM = 4, 256, 256, 128
TOK = BATCH * SEQ
TILES = TOK // P
HALF = 512
HTILES = HALF // P
KT = DIM // P
OT_ = DIM // P
EXPERTS, TOPK, INTER = 32, 8, 96
THRESHOLD = 0.8
GROUP = 4
GROUPS = EXPERTS // GROUP
PARTS = INTER // 32
MW = 3 * DIM
HEADS, HD = 16, 128
FF = 704
FFT = FF // P
FFR = FF - FFT * P
EPS = 1e-5

F32 = mybir.dt.float32
F32R = mybir.dt.float32r
BF16 = mybir.dt.bfloat16
U32 = mybir.dt.uint32
ALU = mybir.AluOpType
ACT = mybir.ActivationFunctionType
AX = mybir.AxisListType

BQ, BK, GQ, GK, DS, GS = 0, 1, 2, 3, 4, 6
US = GS + FFT
TAIL = US + FFT
NCOLS = TAIL + 1


def flamingo(nc, x_d, ctxn_d, ctxT_d, w0_d, cols_d, tailg_d, tailu_d, gates_d, gw_d, moe_d,
             wq_d, wk_d, wv_d, wo_d, wff_d, w2t_d, out_d, comb_d):
    ctx = ExitStack()
    with ctx:
        base = (nc.sbuf_base + 31) // 32 * 32
        top = [0]

        def place(name, shape, dt=F32, at=None):
            size = 4 if dt != BF16 else 2
            for s in shape[1:]:
                size *= s
            size = (size + 31) // 32 * 32
            off = top[0] if at is None else at
            if at is None:
                top[0] += size
            ends[name] = off + size
            assert base + off + size <= nc.sbuf_usable_end, (name, off + size)
            return nc.alloc_sbuf_tensor_at(name, list(shape), dt, offset=base + off)

        ends = {}

        def sem(name):
            return ctx.enter_context(nc.semaphore(name))

        bank = [ctx.enter_context(nc.psum_tensor(f"bank{i}", [P, 512], F32)) for i in range(8)]
        x = place("x", [P, TILES, DIM])
        lnat = top[0]
        xln = place("xln", [P, TILES, DIM])
        OT = [place(f"OT{h}", [P, OT_, HALF], at=lnat + h * 4096) for h in range(2)]
        XThi = place("XThi", [P, KT, TOK], F32R)
        XTlo = place("XTlo", [P, KT, TOK], F32R)
        ctxn = place("ctxn", [P, TILES, CDIM])
        krat = top[0]
        kraw = place("kraw", [P, TILES, HEADS * HD])
        phat = top[0]
        PHhi = place("PHhi", [P, HEADS, DIM], F32R)
        PHlo = place("PHlo", [P, HEADS, DIM], F32R)
        cols = place("cols", [P, NCOLS])
        gates = place("gates", [P, 4])
        tg = place("tg", [P, 4])
        ident = place("ident", [P, P])
        mhalf = place("mhalf", [P, TILES])
        gain = place("gain", [P, 1])
        dscale = place("dscale", [P, OT_])
        ones = place("ones", [P, 1])
        table_out = place("table_out", [P, 1])
        stats = place("stats", [P, TILES, 6])
        mv = place("mv", [P, TILES, 2])
        veps = place("veps", [P, TILES])
        rstd = place("rstd", [P, TILES])
        kst = place("kst", [P, 4])
        kss = place("kss", [P, TILES, HEADS])
        rk = place("rk", [P, TILES, HEADS])
        asum = place("asum", [P, TILES])
        nmax = place("nmax", [P, TILES])
        rsum = place("rsum", [P, TILES])
        gwraw = place("gwraw", [P, KT, EXPERTS])
        gwhi = place("gwhi", [P, KT, EXPERTS], F32R)
        gwlo = place("gwlo", [P, KT, EXPERTS], F32R)
        zeros = place("zeros", [P, 512], BF16)
        R = top[0]
        q0 = place("q0", [P, TOK], at=phat)
        k0 = place("k0", [P, TOK], at=phat + 4096)
        XT0 = place("XT0", [P, BATCH, 2, SEQ], at=phat + 8192)
        A = place("A", [P, TILES, SEQ], at=phat + 16384)
        AT = place("AT", [P, BATCH, 2, SEQ], at=phat + 24576)
        ctxT = place("ctxT", [P, TOK], at=R)
        w0 = place("w0", [P, 2 * CDIM], at=R + 4096)
        wk = place("wk", [P, HEADS * HD], at=R + 5120)
        wkhi = place("wkhi", [P, HEADS * HD], F32R, at=R + 13312)
        wklo = place("wklo", [P, HEADS * HD], F32R, at=R + 21504)
        ctxThi = place("ctxThi", [P, TOK], F32R, at=R + 29696)
        ctxTlo = place("ctxTlo", [P, TOK], F32R, at=R + 33792)
        E8 = [P, TILES, TOPK]
        eq = place("eq", [P, TILES, EXPERTS, TOPK], at=phat)
        o = phat + 8192
        lg = place("lg", [P, TILES, EXPERTS], at=o)
        comb = place("comb", [P, TILES, EXPERTS], at=o + 1024)
        iota32 = place("iota32", [P, EXPERTS], at=o + 2048)
        iota8 = place("iota8", [P, TOPK], at=o + 2176)
        keep8 = place("keep8", E8, at=o + 2304)
        top8 = place("top8", E8, at=o + 2560)
        idx8 = place("idx8", E8, U32, at=o + 2816)
        idxf = place("idxf", E8, at=o + 3072)
        ren8 = place("ren8", E8, at=o + 3328)
        cum8 = place("cum8", E8, at=o + 3584)
        rw8 = place("rw8", E8, at=o + 3840)
        s8 = place("s8", [P, TILES], at=o + 4096)
        r8 = place("r8", [P, TILES], at=o + 4128)
        combT = place("combT", [EXPERTS, TOK], at=o + 4608)
        CE = place("CE", [P, GROUPS, TOK], at=phat)
        whi = [place(f"whi{t}", [P, MW], F32R, at=R + 3072 * t) for t in range(PARTS)]
        wlo = [place(f"wlo{t}", [P, MW], F32R, at=R + 9216 + 3072 * t) for t in range(PARTS)]
        act = [place(f"act{h}", [P, HALF], at=R + 18432 + 2048 * h) for h in range(2)]
        hid = [place(f"hid{h}", [P, HALF], at=R + 22528 + 2048 * h) for h in range(2)]
        hidhi = [place(f"hidhi{h}", [P, HALF], F32R, at=R + 26624 + 2048 * h) for h in range(2)]
        hidlo = [place(f"hidlo{h}", [P, HALF], F32R, at=R + 30720 + 2048 * h) for h in range(2)]
        ksq = place("ksq", [P, 4 * HD], at=lnat)
        wraw = [place(f"wraw{t}", [P, MW], at=R + 37888 + 3072 * t) for t in range(PARTS)]
        wv = place("wv", [P, HEADS, CDIM], at=R + 47104)
        wo = place("wo", [P, HEADS, DIM], at=R + 55296)
        a3 = [R]

        def put3(name, shape, dt=F32):
            t = place(name, shape, dt, at=a3[0])
            a3[0] = ends[name]
            return t
        ctxhi = put3("ctxhi", [P, TILES, CDIM], F32R)
        ctxlo = put3("ctxlo", [P, TILES, CDIM], F32R)
        qhi = put3("qhi", [P, HALF], F32R)
        qlo = put3("qlo", [P, HALF], F32R)
        qsq = put3("qsq", [P, HALF])
        kn = put3("kn", [P, HTILES, HD])
        khi = put3("khi", [P, HALF], F32R)
        klo = put3("klo", [P, HALF], F32R)
        Pm = [put3(f"Pm{i}", [P, 2, 2, SEQ]) for i in range(2)]
        PThi = put3("PThi", [P, 2, 2, SEQ], F32R)
        PTlo = put3("PTlo", [P, 2, 2, SEQ], F32R)
        ohi = put3("ohi", [P, HALF], F32R)
        olo = put3("olo", [P, HALF], F32R)
        wqraw = put3("wqraw", [P, KT * HD])
        wqhi = put3("wqhi", [P, KT, HD], F32R)
        wqlo = put3("wqlo", [P, KT, HD], F32R)
        phhi = put3("phhi", [P, DIM], F32R)
        phlo = put3("phlo", [P, DIM], F32R)
        qst = put3("qst", [P, HTILES])
        qss = put3("qss", [P, HTILES])
        qsc = [put3(f"qsc{i}", [P, HTILES]) for i in range(2)]
        smax = put3("smax", [P, 2, 2])
        nbias = put3("nbias", [P, 2, 2])
        psumr = put3("psumr", [P, 2, 2])
        prec = [put3(f"prec{i}", [P, 2, 2]) for i in range(2)]
        assert a3[0] <= R + 47104, a3[0] - R
        WFT = 2 * FFT + 1 + FFT
        wff = place("wff", [P, WFT + 1, DIM], at=a3[0])
        wfhi = place("wfhi", [P, WFT + 1, DIM], F32R, at=krat)
        wflo = place("wflo", [P, WFT - 1, DIM], F32R, at=ends["wfhi"])
        wflo2 = place("wflo2", [P, 2, DIM], F32R, at=ends["wff"])
        assert ends["wflo"] <= krat + HTILES * HEADS * HD * 4

        EXPERT_TILES = GROUPS * PARTS

        ld_small, ld_w0, ld_ctxn, ld_gw, ld_v, ld_ff = [
            sem(n) for n in ("ld_small", "ld_w0", "ld_ctxn", "ld_gw", "ld_v", "ld_ff")]
        ld_ctxT = [sem(f"ld_ctxT{h}") for h in range(2)]
        ld_x = [sem(f"ld_x{h}") for h in range(2)]
        ld_k = [sem(f"ld_k{h}") for h in range(2)]
        const = sem("const")
        vec_own = sem("vec_own")
        pool_own = sem("pool_own")
        proj = sem("proj"); q0_out = sem("q0_out"); k0_out = sem("k0_out"); energy = sem("energy")
        a_max = sem("a_max"); a_exp = sem("a_exp"); a_norm = sem("a_norm"); tanh_ok = sem("tanh_ok")
        xt0_tr = sem("xt0_tr"); xt0_out = sem("xt0_out"); at_tr = sem("at_tr"); at_out = sem("at_out")
        mix = sem("mix")
        ln_var = sem("ln_var"); ln_rstd = sem("ln_rstd"); ln_out = sem("ln_out")
        xt_tr = sem("xt_tr"); xt_hi = sem("xt_hi"); xt_lo = sem("xt_lo")
        out_first = sem("out_first"); out_second = sem("out_second"); out_back = sem("out_back"); x_new = sem("x_new")
        ctx_wk_hi = sem("ctx_wk_hi"); ctx_wk_lo = sem("ctx_wk_lo"); keys_mm = sem("keys_mm"); keys_out_ok = sem("keys_out_ok")
        gate_split = sem("gate_split"); logits = sem("logits"); lg_sub = sem("lg_sub"); lg_exp = sem("lg_exp")
        eq_made = sem("eq_made"); eq_weighted = sem("eq_weighted"); comb_ok = sem("comb_ok")
        comb_tr = sem("comb_tr"); combT_out = sem("combT_out"); comb_st = sem("comb_st"); ce_ld = sem("ce_ld")
        w_ld = [sem(f"w_ld{t}") for t in range(PARTS)]
        w_hi = sem("w_hi"); w_lo = sem("w_lo")
        gate_mm = sem("gate_mm"); up_mm = sem("up_mm"); silu = sem("silu"); weighted = sem("weighted")
        h_ok = sem("h_ok"); h_hi = sem("h_hi"); h_lo = sem("h_lo"); down = sem("down")
        k_squared = sem("k_squared"); k_summed = sem("k_summed"); k_sum_eps = sem("k_sum_eps"); k_scaled = sem("k_scaled")
        prod_mm = sem("prod_mm"); prod_hi = sem("prod_hi"); prod_lo = sem("prod_lo")
        ctx_split = sem("ctx_split"); wq_ld = sem("wq_ld"); wq_hi_ok = sem("wq_hi_ok"); wq_lo_ok = sem("wq_lo_ok")
        ph_ld = sem("ph_ld")
        kn_ok = sem("kn_ok"); k_turned = sem("k_turned"); k_hi = sem("k_hi"); k_lo = sem("k_lo")
        q_mm = sem("q_mm"); q_hi = sem("q_hi"); q_lo = sem("q_lo"); q_sq = sem("q_sq")
        q_sq_turned = sem("q_sq_turned"); q_summed = sem("q_summed"); q_sum_eps = sem("q_sum_eps"); q_scaled = sem("q_scaled")
        scores_mm = sem("scores_mm"); s_max = sem("s_max"); s_bias = sem("s_bias"); s_exp = sem("s_exp")
        s_recip = sem("s_recip"); s_norm = sem("s_norm"); p_turned = sem("p_turned"); p_hi = sem("p_hi"); p_lo = sem("p_lo")
        context_mm = sem("context_mm"); ctxo_hi = sem("ctxo_hi"); ctxo_lo = sem("ctxo_lo"); head_out = sem("head_out")
        silu_table = sem("silu_table")
        ff_hi = sem("ff_hi"); ff_lo = sem("ff_lo"); f_g = sem("f_g"); f_u = sem("f_u"); f_silu = sem("f_silu")
        f_h = sem("f_h"); f_hi = sem("f_hi"); f_lo = sem("f_lo"); f_down = sem("f_down"); st_out = sem("st_out")

        def f32(ap):
            return ap.bitcast(F32)

        def three(mm, out, wh_, wl_, mhi, mlo, start, stop):
            mm(out, wl_, mhi, start=start, stop=False, skip_group_check=True)
            mm(out, wh_, mhi, start=False, stop=False, skip_group_check=True)
            return mm(out, wh_, mlo, start=False, stop=stop, skip_group_check=True)

        def apart(engine, sem_, value):
            engine.wait_ge(sem_, value)

        def tile_cols(i, n=P):
            return slice(i * n, (i + 1) * n)

        LAST = 2 * HEADS - 1

        def all_heads(engine, step):
            for h in range(2):
                for N in ((0, 1), (HEADS, HEADS + 1))[h]:
                    step(N % HEADS, h, N % 2, N)
                with engine.Fori(1, HEADS // 2 - 2) as pair:
                    for par in range(2):
                        step(2 * pair + par, h, par, None)
                for N in range(h * HEADS + HEADS - 4, (h + 1) * HEADS):
                    step(N % HEADS, h, N % 2, N)

        def ahead(n, h, d):
            N = n + h * HEADS + d
            return (N % HEADS, N // HEADS, N) if isinstance(n, int) else (n + d, h, N)

        def context_bank(N):
            return bank[3 if isinstance(N, int) and N == LAST else 6]

        BACK = {HEADS - 4: (1, 0), HEADS - 3: (1, 1), 2 * HEADS - 4: (2, 0), 2 * HEADS - 3: (2, 1)}
        TURN = {HEADS - 2: 3, 2 * HEADS - 2: 4}
        PIECE = 384

        def gate_up_banks(k):
            return (2, None) if k == 2 * FFT + 1 else (4 + 2 * (k % 2), 5 + 2 * (k % 2))

        PRODUCT_BANKS = (3, 4, 5, 6, 7, 1, 7, 7)

        block = ctx.enter_context(nc.Block())

        @block.sync
        def _(sp):
            sp.dma_start(w0[:], w0_d).then_inc(ld_w0, 16)
            for h in range(2):
                sp.dma_start(ctxT[:, tile_cols(h, HALF)], ctxT_d[:, tile_cols(h, HALF)]).then_inc(ld_ctxT[h], 16)
            sp.dma_start(cols[:, 0:TAIL], cols_d).then_inc(ld_small, 16)
            sp.dma_start(cols[0:FFR, TAIL:NCOLS], tailg_d).then_inc(ld_small, 16)
            sp.dma_start(cols[FFR:2 * FFR, TAIL:NCOLS], tailu_d).then_inc(ld_small, 16)
            sp.dma_start(gates[:], gates_d.partition_broadcast(P)).then_inc(ld_small, 16)
            for h in range(2):
                c = slice(h * HTILES, (h + 1) * HTILES)
                sp.dma_start(x[:, c, :], x_d.rearrange("(t p) d -> p t d", p=P)[:, c, :]).then_inc(ld_x[h], 16)
                c = tile_cols(h, HEADS * HD // 2)
                sp.dma_start(wk[:, c], wk_d[:, c]).then_inc(ld_k[h], 16)
            sp.dma_start(gwraw[:], gw_d.rearrange("(k p) e -> p k e", p=P)).then_inc(ld_gw, 16)
            sp.dma_start(ctxn[:], ctxn_d.rearrange("(t p) d -> p t d", p=P)).then_inc(ld_ctxn, 16)

            def load_expert_tile(m, t, first):
                if not first:
                    apart(sp, ld_x[0], 16)
                    sp.wait_ge(w_lo, (m - 1) * PARTS + t + 1)
                sp.dma_start(wraw[t][:], moe_d[bass.ts(m * PARTS + t, P), :]).then_inc(w_ld[t], 16)

            for t in range(PARTS):
                load_expert_tile(0, t, True)
            sp.dma_start(wv[:].rearrange("p h c -> p (h c)"), wv_d).then_inc(ld_v, 16)
            sp.dma_start(wo[:].rearrange("p h c -> p (h c)"), wo_d).then_inc(ld_v, 16)
            sp.wait_ge(combT_out, 2)
            sp.dma_start(CE[:, 0, :], combT[0:GROUP, :].unsqueeze(1).broadcast_to([GROUP, 32, TOK])).then_inc(ce_ld, 16)
            sp.dma_start(comb_d, combT[:]).then_inc(comb_st, 16)
            sp.wait_ge(comb_st, 16)

            def load_combine(m):
                src = comb_d[bass.ds(m * GROUP, GROUP), :].unsqueeze(1).broadcast_to([GROUP, 32, TOK])
                sp.dma_start(CE[:, bass.ds(m, 1), :].rearrange("p a b -> p (a b)"), src).then_inc(ce_ld, 16)

            with sp.Fori(1, GROUPS) as m:
                apart(sp, ld_x[0], 16)
                sp.wait_ge(ce_ld, 16 * m)
                load_combine(m)
                for t in range(PARTS):
                    load_expert_tile(m, t, False)

            def load_wq(n, N):
                if not (isinstance(N, int) and N == 0):
                    apart(sp, ld_x[0], 16)
                    sp.wait_ge(wq_lo_ok, N)
                sp.dma_start(wqraw[:], wq_d[:, bass.ts(n, KT * HD)]).then_inc(wq_ld, 16)

            def load_ph(n, N):
                if not (isinstance(N, int) and N == 0):
                    apart(sp, ld_x[0], 16)
                    sp.wait_ge(head_out, N)
                for dst, src in ((phhi, PHhi), (phlo, PHlo)):
                    sp.dma_start(f32(dst[:]), f32(src[:].rearrange("p h o -> p (h o)")[:, bass.ts(n, DIM)])).then_inc(ph_ld, 16)

            def head_loads(n, h, par, at):
                n2, _, N2 = ahead(n, h, 2)
                if not isinstance(N2, int) or N2 <= LAST:
                    load_wq(n2, N2)
                if at == 0:
                    sp.wait_ge(prod_lo, 4)
                else:
                    n0, _, N0 = ahead(n, h, -1)
                    load_ph(n0, N0)
                if at == 1:
                    sp.wait_ge(prod_lo, 8)
                if h == 0 and at is None:
                    c = bass.ts(n - 2, PIECE)
                    sp.dma_start(wff[:].rearrange("p a b -> p (a b)")[:, c], wff_d[:, c]).then_inc(ld_ff, 16)
                if at == HEADS - 4:
                    sp.dma_start(wff[:, WFT - 1, :], wff_d[:, (WFT - 1) * DIM:]).then_inc(ld_ff, 16)
                    sp.dma_start(wff[FFR:2 * FFR, WFT, :], w2t_d).then_inc(ld_ff, 16)

            sp.wait_ge(down, 2 * EXPERT_TILES)
            load_wq(0, 0)
            load_wq(1, 1)
            all_heads(sp, head_loads)
            load_ph(HEADS - 1, LAST)
            for i in range(4):
                sp.wait_ge(x_new, 4 * 3 + i + 1)
                sp.dma_start(out_d.rearrange("(t p) d -> p t d", p=P)[:, 2 * i:2 * i + 2, :],
                             x[:, 2 * i:2 * i + 2, :]).then_inc(st_out, 16)
            sp.wait_ge(st_out, 64)

        @block.gpsimd
        def _(pool):
            nc.gpsimd.memset(ident[:], 0.0).then_inc(pool_own, 1)
            nc.gpsimd.memset(mhalf[:], -0.5).then_inc(const, 1)
            nc.gpsimd.memset(ones[:], 1.0).then_inc(const, 1)
            nc.gpsimd.memset(zeros[:].bitcast(F32), 0.0).then_inc(const, 1)
            pool.wait_ge(pool_own, 1)
            nc.gpsimd.affine_select(out=ident[:], in_=ident[:], compare_op=ALU.not_equal, fill=1.0, base=0,
                                    pattern=[[-1, P]], channel_multiplier=1).then_inc(const, 1)
            pool.wait_ge(ctx_wk_hi, 1)
            nc.gpsimd.tensor_tensor(ctxTlo[:], ctxT[:], f32(ctxThi[:]), ALU.subtract).then_inc(ctx_wk_lo, 1)

            def key_weights_low(ck):
                pool.wait_ge(ctx_wk_hi, ck + 2)
                c = tile_cols(ck, 512)
                nc.gpsimd.tensor_tensor(wklo[:, c], wk[:, c], f32(wkhi[:, c]), ALU.subtract).then_inc(ctx_wk_lo, 1)

            for ck in range(2):
                key_weights_low(ck)
            ch = [1]

            def rstd_of(group):
                k, tt = group
                pool.wait_ge(ln_var, k + 1)
                nc.gpsimd.tensor_scalar(veps[:, tt:tt + 2], mv[:, tt:tt + 2, 1], EPS, 1.0, ALU.add, ALU.mult).then_inc(pool_own, 1)
                ch[0] += 1
                pool.wait_ge(pool_own, ch[0])
                nc.gpsimd.tensor_tensor(rstd[:, tt:tt + 2], veps[:, tt:tt + 2], mhalf[:, 0:2], ALU.pow).then_inc(ln_rstd, 1)

            for b in range(BATCH):
                rstd_of((b, 2 * b))
            for ck in range(2, 4):
                key_weights_low(ck)
            for b in range(BATCH):
                rstd_of((4 + b, 2 * b))

            def split_low(it, t):
                pool.wait_ge(w_hi, it + 1)
                nc.gpsimd.tensor_tensor(wlo[t][:], wraw[t][:], f32(whi[t][:]), ALU.subtract).then_inc(w_lo, 1)

            def key_scale(m, c):
                nc.gpsimd.tensor_tensor(rk[:, bass.ds(m, 1), c * 4:(c + 1) * 4].rearrange("p a b -> p (a b)"),
                                        kss[:, bass.ds(m, 1), c * 4:(c + 1) * 4].rearrange("p a b -> p (a b)"),
                                        mhalf[:, 0:4], ALU.pow).then_inc(k_scaled, 1)

            def key_squares(m, c, first=False):
                if not first:
                    pool.wait_ge(k_sum_eps, m * 4 + c)
                kv = kraw[:, bass.ds(m, 1), c * 512:(c + 1) * 512].rearrange("p a b -> p (a b)")
                nc.gpsimd.tensor_tensor(ksq[:], kv, kv, ALU.mult).then_inc(k_squared, 1)

            def moe_pool(m, last=False):
                for t in range(PARTS):
                    it = m * PARTS + t
                    if not last:
                        for c in ([t] if t < PARTS - 1 else [t, t + 1]):
                            key_squares(m + 1, c)
                            key_scale(*((m + 1, c - 1) if c else (m, 3)))
                    if not (last and t > 0):
                        split_low(it + 2, (t + 2) % PARTS)

            pool.wait_ge(xt_tr, 4)
            for c in range(4):
                if c == 3:
                    pool.wait_ge(eq_made, 1)
                    nc.gpsimd.tensor_tensor(eq[:, TILES - 2:], eq[:, TILES - 2:],
                                            rw8[:, TILES - 2:].unsqueeze(2).broadcast_to([P, 2, EXPERTS, TOPK]),
                                            ALU.mult).then_inc(eq_weighted, 1)
                    for t in range(2):
                        split_low(t, t)
                pool.wait_ge(keys_out_ok, 8 * c + 1)
                key_squares(0, c, first=c == 0)
                if c:
                    key_scale(0, c - 1)
            with pool.Fori(0, GROUPS - 1) as m:
                moe_pool(m)
            moe_pool(GROUPS - 1, last=True)
            pool.wait_ge(k_sum_eps, 4 * TILES)
            key_scale(TILES - 1, 3)
            def norm_keys(n, H, N):
                nc.gpsimd.tensor_tensor(
                    kn[:], kraw[:, H * HTILES:(H + 1) * HTILES, bass.ts(n, HD)],
                    rk[:, H * HTILES:(H + 1) * HTILES, bass.ds(n, 1)].broadcast_to([P, HTILES, HD]),
                    ALU.mult).then_inc(kn_ok, 1)

            pool.wait_ge(k_scaled, 4 * TILES)
            pool.wait_ge(down, 2 * EXPERT_TILES)
            norm_keys(0, 0, 0)
            for b in range(2):
                rstd_of((8 + b, 2 * b))
            pool.wait_ge(ctx_split, 1)
            nc.gpsimd.tensor_tensor(ctxlo[:], ctxn[:], f32(ctxhi[:]), ALU.subtract).then_inc(ctx_split, 1)

            def query_scale(N, par):
                pool.wait_ge(q_sum_eps, N + 1)
                nc.gpsimd.tensor_tensor(qsc[par][:], qss[:], mhalf[:, 0:HTILES], ALU.pow).then_inc(q_scaled, 1)

            def softmax_norm(N, par, b):
                pool.wait_ge(s_recip, 2 * N + b + 1)
                pm = Pm[par][:, b]
                nc.gpsimd.tensor_tensor(pm, pm, prec[par][:, b, :].unsqueeze(2).broadcast_to([P, 2, SEQ]),
                                        ALU.mult).then_inc(s_norm, 1)

            def query_weights_low(N):
                pool.wait_ge(wq_hi_ok, N + 1)
                nc.gpsimd.tensor_tensor(wqlo[:].rearrange("p a b -> p (a b)"), wqraw[:],
                                        f32(wqhi[:].rearrange("p a b -> p (a b)")), ALU.subtract).then_inc(wq_lo_ok, 1)

            def head_pool(n, h, par, at):
                N = n + h * HEADS
                softmax_norm(N, par, 0)
                if at is None or at + 2 <= LAST:
                    pool.wait_ge(k_turned, N + 2)
                    norm_keys(*ahead(n, h, 2))
                if at is None or at + 2 <= LAST:
                    query_weights_low(N + 2)
                if at != LAST:
                    query_scale(N + 1, 1 - par)
                softmax_norm(N, par, 1)
                if h == 1 and at is None:
                    pool.wait_ge(ff_hi, n - 1)
                    flat = "p a b -> p (a b)"
                    c = bass.ts(n - 2, PIECE)
                    nc.gpsimd.tensor_tensor(wflo[:].rearrange(flat)[:, c], wff[:].rearrange(flat)[:, c],
                                            f32(wfhi[:].rearrange(flat)[:, c]), ALU.subtract).then_inc(ff_lo, 1)
                if at == 2 * HEADS - 4:
                    pool.wait_ge(ff_hi, 12)
                    nc.gpsimd.tensor_tensor(wflo2[:, 0, :], wff[:, WFT - 1, :], f32(wfhi[:, WFT - 1, :]),
                                            ALU.subtract).then_inc(ff_lo, 1)
                    pool.wait_ge(ff_lo, 11)
                    r = slice(FFR, 2 * FFR)
                    nc.gpsimd.tensor_tensor(wflo2[r, 1, :], wff[r, WFT, :], f32(wfhi[r, WFT, :]),
                                            ALU.subtract).then_inc(ff_lo, 1)
                    pool.wait_ge(ff_lo, 12)
                if at in BACK:
                    k, piece = BACK[at]
                    rstd_of((8 + 2 * k + piece, (k % 2) * HTILES + 2 * piece))

            query_weights_low(0)
            query_weights_low(1)
            query_scale(0, 0)
            pool.wait_ge(k_turned, 1)
            norm_keys(1, 0, 1)
            all_heads(pool, head_pool)
            for i in range(2):
                rstd_of((14 + i, HTILES + 2 * i))

        @block.scalar
        def _(s):
            act_ = nc.scalar.activation
            for h in range(2):
                s.wait_ge(ld_ctxT[h], 16)
            act_(ctxThi[:], ctxT[:], ACT.Copy).then_inc(ctx_wk_hi, 1)
            s.wait_ge(ld_small, 64)
            for h in range(2):
                s.wait_ge(proj, 2 * h + 1)
                act_(q0[:, tile_cols(h, HALF)], bank[h][:], ACT.Identity, bias=cols[:, BQ:BQ + 1]).then_inc(q0_out, 1)
            act_(tg[:], gates[:], ACT.Tanh).then_inc(tanh_ok, 1)

            def key_weights_high(ck):
                s.wait_ge(ld_k[ck // 2], 16)
                c = tile_cols(ck, 512)
                act_(wkhi[:, c], wk[:, c], ACT.Copy).then_inc(ctx_wk_hi, 1)

            def keys_out(ck, tts, first):
                for tt in tts:
                    s.wait_ge(keys_mm, ck * TILES + tt + 1)
                    act_(kraw[:, tt, bass.ts(ck, 512)], bank[first + tt % 4][:], ACT.Copy).then_inc(keys_out_ok, 1)

            for ck in range(2):
                key_weights_high(ck)
            for b in range(BATCH):
                s.wait_ge(a_max, b + 1)
                for i in range(2):
                    tt = 2 * b + i
                    act_(A[:, tt, :], bank[4 + b][:, tile_cols(i, SEQ)], ACT.Exp, bias=nmax[:, tt:tt + 1],
                         accum_out=asum[:, tt:tt + 1]).then_inc(a_exp, 1)
                keys_out(0, (2 * b, 2 * b + 1), 0)
            for b in range(BATCH):
                s.wait_ge(xt0_tr, b + 1)
                act_(XT0[:, b].rearrange("p a b -> p (a b)"), bank[4 + b][:], ACT.Copy).then_inc(xt0_out, 1)
                s.wait_ge(at_tr, b + 1)
                act_(AT[:, b].rearrange("p a b -> p (a b)"), bank[b][:], ACT.Copy).then_inc(at_out, 1)
                if b < 2:
                    key_weights_high(2 + b)

            def xt_high(k, banks, half, kts=range(KT)):
                for kt in kts:
                    s.wait_ge(xt_tr, 2 * k + kt + 1)
                    act_(XThi[:, kt, tile_cols(half, HALF)], bank[banks[kt]][:], ACT.Copy).then_inc(xt_hi, 1)

            keys_out(1, range(4), 4)
            xt_high(0, (0, 1), 0)
            keys_out(1, range(4, TILES), 4)
            xt_high(1, (2, 3), 1)
            s.wait_ge(lg_sub, 1)
            act_(lg[:], lg[:], ACT.Exp).then_inc(lg_exp, 1)
            with s.Fori(2, 4) as ck:
                keys_out(ck, range(TILES), 4)

            def activate(n2, h, free):
                s.wait_ge(gate_mm, n2 + 1)
                if free:
                    s.wait_ge(h_ok, n2 - 1)
                act_(act[h][:], bank[4 + 2 * h][:], ACT.Silu).then_inc(silu, 1)

            def hidden_high(n2, h, free):
                s.wait_ge(h_ok, n2 + 1)
                if free:
                    s.wait_ge(down, n2 - 1)
                act_(hidhi[h][:], hid[h][:], ACT.Copy).then_inc(h_hi, 1)

            def split_high(it, t, m, free):
                s.wait_ge(w_ld[t], 16 * (m + 1))
                if free:
                    s.wait_ge(down, it * 2 - 4)
                act_(whi[t][:], wraw[t][:], ACT.Copy).then_inc(w_hi, 1)

            def moe_act(m, first=False, last=False):
                for t in range(PARTS):
                    it = m * PARTS + t
                    start = first and t == 0
                    for h in range(2):
                        if not start:
                            activate(it * 2 + h, h, True)
                        hidden_high(it * 2 + h, h, not start)
                    if not (last and t > 0):
                        nx = t + 2
                        split_high(it + 2, nx % PARTS, m + nx // PARTS, not start)

            for t in range(2):
                split_high(t, t, 0, False)
            for h in range(2):
                s.wait_ge(comb_tr, h + 1)
                act_(combT[:, tile_cols(h, HALF)], bank[1 + h][0:EXPERTS, :], ACT.Copy).then_inc(combT_out, 1)
            for h in range(2):
                activate(h, h, False)
            moe_act(0, first=True)
            with s.Fori(1, GROUPS - 1) as m:
                moe_act(m)
            moe_act(GROUPS - 1, last=True)

            def block_end(k, acc, scale):
                act_(OT[k % 2][:, 0, :], bank[acc][:], ACT.Copy, scale=scale).then_inc(out_first, 1)

            for h in range(2):
                s.wait_ge(down, 2 * EXPERT_TILES - 1 + h)
                block_end(h, h, tg[:, 1:2])

            def head_product_high(j):
                s.wait_ge(prod_mm, j + 1)
                act_(PHhi[:, 2 * j:2 * j + 2, :].rearrange("p a b -> p (a b)"), bank[PRODUCT_BANKS[j]][:], ACT.Copy).then_inc(prod_hi, 1)

            for j in range(6):
                head_product_high(j)
            act_(ctxhi[:], ctxn[:], ACT.Copy).then_inc(ctx_split, 1)
            xt_high(2, (0, 2), 0)

            def keys_high(N):
                s.wait_ge(k_turned, N + 1)
                act_(khi[:], bank[3][:], ACT.Copy, scale=gain[:, 0:1]).then_inc(k_hi, 1)

            def query_high(N):
                s.wait_ge(q_mm, N + 1)
                act_(qhi[:], bank[2][:], ACT.Copy).then_inc(q_hi, 1)
                act_(qsq[:], bank[2][:], ACT.Square).then_inc(q_sq, 1)

            def softmax_exp(N, par, b, first):
                s.wait_ge(s_bias, 2 * N + b + 1)
                if not first:
                    s.wait_ge(p_turned, 2 * N - 3 + b)
                for i in range(2):
                    act_(Pm[par][:, b, i, :], bank[4 + b][:, tile_cols(i, SEQ)], ACT.Exp, bias=nbias[:, b, i:i + 1],
                         scale=qsc[par][:, 2 * b + i:2 * b + i + 1], accum_out=psumr[:, b, i:i + 1]).then_inc(s_exp, 1)

            def probs_high(N, b):
                s.wait_ge(p_turned, 2 * N + b + 1)
                act_(PThi[:, b].rearrange("p a b -> p (a b)"), bank[6 + b][:], ACT.Copy).then_inc(p_hi, 1)

            def out_high(N):
                s.wait_ge(context_mm, N + 1)
                act_(ohi[:], context_bank(N)[:], ACT.Copy).then_inc(ctxo_hi, 1)

            def head_act(n, h, par, at):
                N = n + h * HEADS
                if at not in (0, 1):
                    out_high(N - 2)
                softmax_exp(N, par, 0, at in (0, 1))
                if at != LAST:
                    query_high(N + 1)
                if at == 0:
                    head_product_high(7)
                else:
                    probs_high(N - 1, 0)
                    probs_high(N - 1, 1)
                if at != LAST:
                    keys_high(N + 1)
                if at == HEADS + 1:
                    s.wait_ge(head_out, HEADS)
                    block_end(2, 0, tg[:, 2:3])
                softmax_exp(N, par, 1, at in (0, 1))
                if at in TURN:
                    xt_high(TURN[at], (3, 7), TURN[at] % 2)

            keys_high(0)
            query_high(0)
            head_product_high(6)
            all_heads(s, head_act)
            out_high(LAST - 1)
            act_(table_out[:], ones[:], ACT.Silu).then_inc(silu_table, 1)
            for b in range(2):
                probs_high(LAST, b)
            out_high(LAST)

            def ff_act(H, i):
                k = H * (FFT + 1) + i
                G, U = gate_up_banks(k)
                s.wait_ge(f_g, k + 1)
                if k >= 2:
                    s.wait_ge(f_h, k - 1)
                if i < FFT:
                    act_(act[i % 2][:], bank[G][:], ACT.Silu, scale=cols[:, GS + i:GS + i + 1]).then_inc(f_silu, 1)
                else:
                    act_(act[i % 2][FFR:2 * FFR, :], bank[G][0:FFR, :], ACT.Silu,
                         scale=cols[0:FFR, TAIL:NCOLS]).then_inc(f_silu, 1)

            def ff_high(H, i):
                k = H * (FFT + 1) + i
                s.wait_ge(f_h, k + 1)
                if k >= 2:
                    s.wait_ge(f_down, k - 1)
                r = slice(0, P) if i < FFT else slice(FFR, 2 * FFR)
                act_(hidhi[i % 2][r, :], hid[i % 2][r, :], ACT.Copy).then_inc(f_hi, 1)

            for k in range(2 * (FFT + 1)):
                ff_act(k // (FFT + 1), k % (FFT + 1))
                ff_high(k // (FFT + 1), k % (FFT + 1))
                if k == 0:
                    s.wait_ge(head_out, 2 * HEADS)
                    block_end(3, 0, tg[:, 2:3])
                if k == 4:
                    xt_high(5, (2, 3), 1)
                if k == FFT + 1:
                    s.wait_ge(f_down, FFT + 1)
                    block_end(4, 0, dscale[:, 0:1])
            s.wait_ge(f_down, 2 * (FFT + 1))
            block_end(5, 0, dscale[:, 0:1])

        @block.vector
        def _(v):
            V = nc.vector
            ch = [0]

            def step(ins):
                ins.then_inc(vec_own, 1)
                ch[0] += 1

            def settle():
                v.wait_ge(vec_own, ch[0])


            def ln_stats(tt):
                for t in (tt, tt + 1):
                    step(V.bn_stats(stats[:, t, :], x[:, t, :]))
                settle()
                V.bn_aggr(mv[:, tt, :], stats[:, tt, :]).then_inc(vec_own, 1)
                V.bn_aggr(mv[:, tt + 1, :], stats[:, tt + 1, :]).then_inc(ln_var, 1)
                ch[0] += 1
                settle()

            def ln_apply(k, tt):
                v.wait_ge(ln_rstd, k + 1)
                for t in (tt, tt + 1):
                    V.tensor_scalar(xln[:, t, :], x[:, t, :], mv[:, t, 0:1], rstd[:, t:t + 1],
                                    ALU.subtract, ALU.mult).then_inc(ln_out, 1)

            def xt_low(k, banks, half, kts=range(KT)):
                for kt in kts:
                    v.wait_ge(xt_hi, 2 * k + kt + 1)
                    c = tile_cols(half, HALF)
                    V.tensor_tensor(XTlo[:, kt, c], bank[banks[kt]][:], f32(XThi[:, kt, c]), ALU.subtract).then_inc(xt_lo, 1)

            def key_sums(m, c):
                v.wait_ge(k_squared, m * 4 + c + 1)
                V.tensor_reduce(kst[:], ksq[:].rearrange("p (h d) -> p h d", d=HD), AX.X, ALU.add).then_inc(k_summed, 1)
                v.wait_ge(k_summed, m * 4 + c + 1)
                V.tensor_scalar(kss[:, bass.ds(m, 1), c * 4:(c + 1) * 4].rearrange("p a b -> p (a b)"), kst[:],
                                HD * EPS, None, ALU.add).then_inc(k_sum_eps, 1)

            v.wait_ge(ld_small, 64)
            step(V.scalar_tensor_tensor(out=gain[:], in0=cols[:, GQ:GQ + 1], scalar=float(HD) ** 0.5,
                                        in1=cols[:, GK:GK + 1], op0=ALU.mult, op1=ALU.mult))
            for h in range(2):
                v.wait_ge(proj, 2 * h + 2)
                V.tensor_scalar(k0[:, tile_cols(h, HALF)], bank[2 + h][:], cols[:, BK:BK + 1], None, ALU.add).then_inc(k0_out, 1)
            v.wait_ge(ld_x[0], 16)
            v.wait_ge(ld_x[1], 16)
            ln_stats(0)
            for b in range(BATCH):
                v.wait_ge(energy, b + 1)
                V.tensor_reduce(nmax[:, 2 * b:2 * b + 2], bank[4 + b][:].rearrange("p (i m) -> p i m", i=2), AX.X, ALU.max,
                                negate=True).then_inc(a_max, 1)
                if b:
                    ln_stats(2 * b)

            def normalise(b):
                v.wait_ge(a_exp, 2 * b + 2)
                step(V.reciprocal(rsum[:, 2 * b:2 * b + 2], asum[:, 2 * b:2 * b + 2]))
                settle()
                for i in range(2):
                    tt = 2 * b + i
                    V.tensor_scalar(A[:, tt, :], A[:, tt, :], rsum[:, tt:tt + 1], None, ALU.mult).then_inc(a_norm, 1)

            def add_mix(b):
                v.wait_ge(mix, b + 1)
                xb = x[:, 2 * b:2 * b + 2, :].rearrange("p a b -> p (a b)")
                V.scalar_tensor_tensor(out=xb, in0=bank[b][:], scalar=tg[:, 0:1], in1=xb, op0=ALU.mult,
                                       op1=ALU.add).then_inc(x_new, 1)
                v.wait_ge(x_new, b + 1)
                ln_stats(2 * b)

            v.wait_ge(tanh_ok, 1)
            step(V.tensor_scalar(dscale[:], cols[:, DS:DS + 2], tg[:, 3:4], None, ALU.mult))
            for b in range(BATCH):
                ln_apply(b, 2 * b)
                normalise(b)
                if b == BATCH - 2:
                    add_mix(0)
            v.wait_ge(ld_gw, 16)
            step(V.tensor_copy(gwhi[:], gwraw[:]))
            settle()
            V.tensor_tensor(gwlo[:], gwraw[:], f32(gwhi[:]), ALU.subtract).then_inc(gate_split, 1)
            for b in range(1, BATCH):
                add_mix(b)
                ln_apply(4 + b - 1, 2 * b - 2)
            ln_apply(7, 6)
            xt_low(0, (0, 1), 0)
            xt_low(1, (2, 3), 1)
            for c in range(2):
                key_sums(0, c)

            def bc(ap, shape):
                return ap.unsqueeze(2).broadcast_to(shape)

            v.wait_ge(logits, TILES)
            step(V.tensor_copy(lg[:].rearrange("p a b -> p (a b)"), bank[0][:, 0:TILES * EXPERTS]))
            settle()
            step(V.tensor_reduce(s8[:], lg[:], AX.X, ALU.max))
            settle()
            V.tensor_tensor(lg[:], lg[:], bc(s8[:], [P, TILES, EXPERTS]), ALU.subtract).then_inc(lg_sub, 1)
            step(V.memset(keep8[:], 1.0))
            step(V.memset(iota32[:], 1.0))
            settle()
            step(V.memset(keep8[:, :, 0:1], 0.0))
            step(V.tensor_tensor_scan(iota32[:], iota32[:], iota32[:], -1.0, ALU.mult, ALU.add))
            settle()
            v.wait_ge(lg_exp, 1)
            step(V.tensor_reduce(s8[:], lg[:], AX.X, ALU.add))
            settle()
            step(V.reciprocal(r8[:], s8[:]))
            settle()
            step(V.tensor_tensor(lg[:], lg[:], bc(r8[:], [P, TILES, EXPERTS]), ALU.mult))
            settle()
            for tt in range(TILES):
                step(V.max(top8[:, tt, :], lg[:, tt, :]))
            settle()
            for tt in range(TILES):
                step(V.max_index(idx8[:, tt, :], top8[:, tt, :], lg[:, tt, :]))
            step(V.tensor_reduce(s8[:], top8[:], AX.X, ALU.add))
            settle()
            step(V.tensor_scalar(s8[:], s8[:], 1e-12, None, ALU.max))
            step(V.tensor_copy(idxf[:], idx8[:]))
            settle()
            step(V.reciprocal(r8[:], s8[:]))
            settle()
            step(V.tensor_tensor(ren8[:], top8[:], bc(r8[:], E8), ALU.mult))
            settle()
            step(V.tensor_tensor_scan(cum8[:].rearrange("p a b -> p (a b)"), keep8[:].rearrange("p a b -> p (a b)"),
                                      ren8[:].rearrange("p a b -> p (a b)"), 0.0, ALU.mult, ALU.add))
            settle()
            step(V.tensor_scalar(cum8[:], cum8[:], THRESHOLD, None, ALU.is_lt))
            settle()
            step(V.tensor_reduce(s8[:], cum8[:], AX.X, ALU.add))
            settle()
            step(V.tensor_scalar(s8[:], s8[:], 1.0, float(TOPK), ALU.add, ALU.min))
            settle()
            step(V.tensor_tensor(cum8[:], iota32[:, 0:TOPK].unsqueeze(1).broadcast_to(E8), bc(s8[:], E8), ALU.is_lt))
            settle()
            step(V.tensor_tensor(rw8[:], top8[:], cum8[:], ALU.mult))
            settle()
            step(V.tensor_reduce(s8[:], rw8[:], AX.X, ALU.add))
            settle()
            step(V.tensor_scalar(s8[:], s8[:], 1e-12, None, ALU.max))
            settle()
            step(V.reciprocal(r8[:], s8[:]))
            settle()
            step(V.tensor_tensor(rw8[:], rw8[:], bc(r8[:], E8), ALU.mult))
            settle()
            full = [P, TILES, EXPERTS, TOPK]
            V.tensor_tensor(eq[:], idxf[:].unsqueeze(2).broadcast_to(full),
                            iota32[:].unsqueeze(1).unsqueeze(3).broadcast_to(full), ALU.is_equal).then_inc(eq_made, 1)
            v.wait_ge(eq_made, 1)

            def weigh(t0, t1):
                t = slice(t0, t1)
                return V.tensor_tensor(eq[:, t], eq[:, t],
                                            rw8[:, t].unsqueeze(2).broadcast_to([P, t1 - t0, EXPERTS, TOPK]), ALU.mult)

            step(weigh(0, HTILES))
            settle()
            V.tensor_reduce(comb[:, 0:HTILES], eq[:, 0:HTILES], AX.X, ALU.add).then_inc(comb_ok, 1)
            step(weigh(HTILES, TILES - 2))
            settle()
            v.wait_ge(eq_weighted, 1)
            V.tensor_reduce(comb[:, HTILES:TILES], eq[:, HTILES:TILES], AX.X, ALU.add).then_inc(comb_ok, 1)

            def hidden(m, n2, h):
                v.wait_ge(silu, n2 + 1)
                V.tensor_tensor(act[h][:], act[h][:], CE[:, bass.ds(m, 1), tile_cols(h, HALF)].rearrange("p a b -> p (a b)"),
                                ALU.mult).then_inc(weighted, 1)
                v.wait_ge(up_mm, n2 + 1)
                v.wait_ge(weighted, n2 + 1)
                V.tensor_tensor(hid[h][:], bank[5 + 2 * h][:], act[h][:], ALU.mult).then_inc(h_ok, 1)

            def hidden_low(n2, h):
                v.wait_ge(h_hi, n2 + 1)
                V.tensor_tensor(hidlo[h][:], hid[h][:], f32(hidhi[h][:]), ALU.subtract).then_inc(h_lo, 1)

            def moe_vec(m, last=False):
                v.wait_ge(ce_ld, 16 * (m + 1))
                for t in range(PARTS):
                    for h in range(2):
                        n2 = (m * PARTS + t) * 2 + h
                        hidden(m, n2, h)
                        if not last and (h == 0 or t == PARTS - 1):
                            key_sums(m + 1, t + h)
                        hidden_low(n2, h)

            for c in range(2, 4):
                key_sums(0, c)
            with v.Fori(0, GROUPS - 1) as m:
                moe_vec(m)
            moe_vec(GROUPS - 1, last=True)

            def block_end(k, acc, scale):
                V.tensor_scalar(OT[k % 2][:, 1, :], bank[acc][:], scale, None, ALU.mult).then_inc(out_second, 1)

            def residual(k, i, b):
                tt = (k % 2) * HTILES + 2 * i
                v.wait_ge(out_back, 2 * k + i + 1)
                xb = x[:, tt:tt + 2, :].rearrange("p a b -> p (a b)")
                V.tensor_tensor(xb, bank[b][:], xb, ALU.add).then_inc(x_new, 1)
                if k < 4:
                    v.wait_ge(x_new, 4 + 2 * k + i + 1)
                    ln_stats(tt)

            def ln_half(k):
                for i in range(2):
                    ln_apply(2 * k + 4 + i, (k % 2) * HTILES + 2 * i)

            for h in range(2):
                v.wait_ge(down, 2 * EXPERT_TILES - 1 + h)
                block_end(h, 2 + h, tg[:, 1:2])

            def head_product_low(j):
                v.wait_ge(prod_hi, j + 1)
                ph = PHhi[:, 2 * j:2 * j + 2, :].rearrange("p a b -> p (a b)")
                pl = PHlo[:, 2 * j:2 * j + 2, :].rearrange("p a b -> p (a b)")
                V.tensor_tensor(pl, bank[PRODUCT_BANKS[j]][:], f32(ph), ALU.subtract).then_inc(prod_lo, 1)

            def query_weights_high(N, ld):
                v.wait_ge(wq_ld, ld)
                if not (isinstance(N, int) and N == 0):
                    v.wait_ge(q_mm, N)
                w = wqhi[:].rearrange("p a b -> p (a b)")
                V.tensor_copy(w, wqraw[:]).then_inc(wq_hi_ok, 1)

            def keys_low(N):
                v.wait_ge(k_hi, N + 1)
                V.scalar_tensor_tensor(out=klo[:], in0=bank[3][:], scalar=gain[:, 0:1], in1=f32(khi[:]),
                                       op0=ALU.mult, op1=ALU.subtract).then_inc(k_lo, 1)

            def query_low(N):
                v.wait_ge(q_sq, N + 1)
                V.tensor_tensor(qlo[:], bank[2][:], f32(qhi[:]), ALU.subtract).then_inc(q_lo, 1)

            def query_squares(N):
                v.wait_ge(q_sq_turned, N + 1)
                V.tensor_reduce(qst[:], bank[2][:].rearrange("p (i d) -> p i d", d=HD), AX.X, ALU.add).then_inc(q_summed, 1)
                v.wait_ge(q_summed, N + 1)
                V.tensor_scalar(qss[:], qst[:], HD * EPS, None, ALU.add).then_inc(q_sum_eps, 1)

            def softmax_bias(N, par, b):
                v.wait_ge(scores_mm, 2 * N + b + 1)
                V.tensor_reduce(smax[:, b, :], bank[4 + b][:].rearrange("p (i m) -> p i m", i=2), AX.X,
                                ALU.max).then_inc(s_max, 1)
                v.wait_ge(s_max, 2 * N + b + 1)
                v.wait_ge(q_scaled, N + 1)
                V.scalar_tensor_tensor(out=nbias[:, b, :], in0=smax[:, b, :], scalar=-1.0, in1=qsc[par][:, 2 * b:2 * b + 2],
                                       op0=ALU.mult, op1=ALU.mult).then_inc(s_bias, 1)

            def softmax_recip(N, par, b):
                v.wait_ge(s_exp, 4 * N + 2 * b + 2)
                V.reciprocal(prec[par][:, b, :], psumr[:, b, :]).then_inc(s_recip, 1)

            def probs_low(N, b):
                v.wait_ge(p_hi, 2 * N + b + 1)
                V.tensor_tensor(PTlo[:, b].rearrange("p a b -> p (a b)"), bank[6 + b][:],
                                f32(PThi[:, b].rearrange("p a b -> p (a b)")), ALU.subtract).then_inc(p_lo, 1)

            def out_low(N):
                v.wait_ge(ctxo_hi, N + 1)
                V.tensor_tensor(olo[:], context_bank(N)[:], f32(ohi[:]), ALU.subtract).then_inc(ctxo_lo, 1)

            flat = "p a b -> p (a b)"

            def head_vec(n, h, par, at):
                N = n + h * HEADS
                softmax_bias(N, par, 0)
                if at not in (0, 1):
                    out_low(N - 2)
                softmax_bias(N, par, 1)
                if at in TURN:
                    k = TURN[at] - 2
                    ln_apply(9 + 2 * k, (k % 2) * HTILES + 2)
                if at is None or at + 2 <= LAST:
                    query_weights_high(N + 2, 16 * (N + 3))
                softmax_recip(N, par, 0)
                if at != LAST:
                    query_low(N + 1)
                if at == 0:
                    head_product_low(7)
                else:
                    probs_low(N - 1, 0)
                    probs_low(N - 1, 1)
                if at != LAST:
                    keys_low(N + 1)
                if at == HEADS + 1:
                    v.wait_ge(head_out, HEADS)
                    block_end(2, 1, tg[:, 2:3])
                if at != LAST:
                    query_squares(N + 1)
                softmax_recip(N, par, 1)
                if h == 1 and at is None:
                    v.wait_ge(ld_ff, 16 * 12)
                    c = bass.ts(n - 2, PIECE)
                    V.tensor_copy(wfhi[:].rearrange(flat)[:, c], wff[:].rearrange(flat)[:, c]).then_inc(ff_hi, 1)
                if at == 2 * HEADS - 4:
                    V.tensor_copy(wfhi[:, WFT - 1, :], wff[:, WFT - 1, :]).then_inc(ff_hi, 1)
                    V.tensor_copy(wfhi[FFR:2 * FFR, WFT, :], wff[FFR:2 * FFR, WFT, :]).then_inc(ff_hi, 1)
                if at in BACK:
                    k, piece = BACK[at]
                    residual(k, piece, 3)
                    if piece:
                        ln_apply(8 + 2 * k, (k % 2) * HTILES)
                if at in TURN:
                    xt_low(TURN[at], (3, 7), TURN[at] % 2)

            query_weights_high(0, 16)
            residual(0, 0, 0)
            residual(0, 1, 2)
            head_product_low(0)
            ln_half(2)
            for j in range(1, 3):
                head_product_low(j)
            xt_low(2, (0, 2), 0)
            head_product_low(3)
            keys_low(0)
            head_product_low(4)
            head_product_low(5)
            query_low(0)
            query_weights_high(1, 32)
            query_squares(0)
            head_product_low(6)
            all_heads(v, head_vec)
            out_low(LAST - 1)
            for b in range(2):
                probs_low(LAST, b)
            out_low(LAST)

            def ff_vec(H, i):
                k = H * (FFT + 1) + i
                G, U = gate_up_banks(k)
                if i < FFT:
                    v.wait_ge(f_u, H * FFT + i + 1)
                v.wait_ge(f_silu, k + 1)
                if k >= 2:
                    v.wait_ge(f_hi, k - 1)
                if i < FFT:
                    V.scalar_tensor_tensor(out=hid[i % 2][:], in0=bank[U][:], scalar=cols[:, US + i:US + i + 1],
                                           in1=act[i % 2][:], op0=ALU.mult, op1=ALU.mult).then_inc(f_h, 1)
                else:
                    r = slice(FFR, 2 * FFR)
                    V.scalar_tensor_tensor(out=hid[i % 2][r, :], in0=bank[G][r, :], scalar=cols[r, TAIL:NCOLS],
                                           in1=act[i % 2][r, :], op0=ALU.mult, op1=ALU.mult).then_inc(f_h, 1)
                v.wait_ge(f_hi, k + 1)
                r = slice(0, P) if i < FFT else slice(FFR, 2 * FFR)
                V.tensor_tensor(hidlo[i % 2][r, :], hid[i % 2][r, :], f32(hidhi[i % 2][r, :]), ALU.subtract).then_inc(f_lo, 1)

            for k in range(2 * (FFT + 1)):
                ff_vec(k // (FFT + 1), k % (FFT + 1))
                if k == 0:
                    v.wait_ge(head_out, 2 * HEADS)
                    block_end(3, 1, tg[:, 2:3])
                    residual(3, 0, 2)
                if k == 1:
                    residual(3, 1, 3)
                if k == 2:
                    ln_half(5)
                if k == 4:
                    xt_low(5, (2, 3), 1)
                if k == FFT + 1:
                    v.wait_ge(f_down, FFT + 1)
                    block_end(4, 1, dscale[:, 1:2])
                if k == FFT + 3:
                    residual(4, 0, 2)
                    residual(4, 1, 3)
            v.wait_ge(f_down, 2 * (FFT + 1))
            block_end(5, 1, dscale[:, 1:2])
            residual(5, 0, 4)
            residual(5, 1, 5)

        @block.tensor
        def _(pe):
            mm, tr = nc.tensor.matmul, nc.tensor.transpose
            pe.wait_ge(ld_w0, 16)
            for j in (0, 2, 1, 3):
                pe.wait_ge(ld_ctxT[j % 2], 16)
                mm(bank[j][:], w0[:, tile_cols(j // 2)], ctxT[:, tile_cols(j % 2, HALF)],
                   start=True, stop=True).then_inc(proj, 1)
            for b in range(BATCH):
                pe.wait_ge(q0_out, b // 2 + 1)
                pe.wait_ge(k0_out, b // 2 + 1)
                for i in range(2):
                    ins = mm(bank[4 + b][:, tile_cols(i, SEQ)], q0[:, tile_cols(2 * b + i)], k0[:, tile_cols(b, SEQ)],
                             start=True, stop=True)
                ins.then_inc(energy, 1)

            def key_tiles(ck, tts, first):
                for tt in tts:
                    if not (isinstance(ck, int) and ck == 0 and tt < 4):
                        pe.wait_ge(keys_out_ok, ck * TILES + tt - 3)
                    c = tile_cols(tt)
                    three(mm, bank[first + tt % 4][:], ctxThi[:, c], ctxTlo[:, c], wkhi[:, bass.ts(ck, 512)],
                          wklo[:, bass.ts(ck, 512)], True, True).then_inc(keys_mm, 1)

            pe.wait_ge(ctx_wk_lo, 2)
            key_tiles(0, range(TILES), 0)
            pe.wait_ge(const, 4)

            def mix_in(b):
                pe.wait_ge(xt0_out, b + 1)
                pe.wait_ge(at_out, b + 1)
                for i in range(2):
                    for j in range(2):
                        ins = mm(bank[b][:, tile_cols(i, SEQ)], XT0[:, b, j, tile_cols(i)], AT[:, b, j, :],
                                 start=(j == 0), stop=(j == 1))
                ins.then_inc(mix, 1)

            for b in range(BATCH):
                pe.wait_ge(ln_out, 2 * b + 2)
                pe.wait_ge(a_exp, 2 * b + 2)
                for j in range(2):
                    for i in range(2):
                        ins = tr(bank[4 + b][:, j * SEQ + i * P:j * SEQ + (i + 1) * P], xln[:, 2 * b + i, tile_cols(j)], ident[:])
                ins.then_inc(xt0_tr, 1)
                pe.wait_ge(a_norm, 2 * b + 2)
                pe.wait_ge(keys_out_ok, 4 + b + 1)
                for j in range(2):
                    for i in range(2):
                        ins = tr(bank[b][:, j * SEQ + i * P:j * SEQ + (i + 1) * P], A[:, 2 * b + i, tile_cols(j)], ident[:])
                ins.then_inc(at_tr, 1)
                if b:
                    mix_in(b - 1)
            mix_in(BATCH - 1)

            def xt_transpose(k, banks, half, kts=range(KT)):
                pe.wait_ge(ln_out, 8 + 4 * k + 4)
                for kt in kts:
                    for i in range(HTILES):
                        ins = tr(bank[banks[kt]][:, tile_cols(i)], xln[:, half * HTILES + i, tile_cols(kt)], ident[:])
                    ins.then_inc(xt_tr, 1)

            pe.wait_ge(ctx_wk_lo, 5)
            key_tiles(1, range(4), 4)
            pe.wait_ge(x_new, 2)
            xt_transpose(0, (0, 1), 0)
            key_tiles(1, range(4, TILES), 4)
            pe.wait_ge(x_new, 4)
            xt_transpose(1, (2, 3), 1)
            pe.wait_ge(gate_split, 1)
            for tt in range(TILES):
                pe.wait_ge(xt_lo, 2 if tt < HTILES else 4)
                for kt in range(KT):
                    ins = three(mm, bank[0][:, tile_cols(tt, EXPERTS)], XThi[:, kt, tile_cols(tt)], XTlo[:, kt, tile_cols(tt)],
                                gwhi[:, kt, :], gwlo[:, kt, :], kt == 0, kt == KT - 1)
                ins.then_inc(logits, 1)
            with pe.Fori(2, 4) as ck:
                key_tiles(ck, range(TILES), 4)

            def gate_up(it, t, h, first):
                n2 = it * 2 + h
                c = tile_cols(h, HALF)
                if h == 0:
                    pe.wait_ge(w_lo, it + 1)
                for j, free in ((0, silu), (1, h_ok)):
                    if not first:
                        pe.wait_ge(free, n2 - 1)
                    for kt in range(KT):
                        w = slice((kt * 2 + j) * P, (kt * 2 + j + 1) * P)
                        ins = three(mm, bank[4 + 2 * h + j][:], whi[t][:, w], wlo[t][:, w], XThi[:, kt, c], XTlo[:, kt, c],
                                    kt == 0, kt == KT - 1)
                    ins.then_inc(up_mm if j else gate_mm, 1)

            def down_half(it, t, h, last):
                n2 = it * 2 + h
                pe.wait_ge(h_lo, n2 + 1)
                for o in range(OT_):
                    w = slice(2 * DIM + o * P, 2 * DIM + (o + 1) * P)
                    ins = three(mm, bank[2 * o + h][:], whi[t][:, w], wlo[t][:, w], hidhi[h][:], hidlo[h][:], False, last)
                ins.then_inc(down, 1)

            pe.wait_ge(keys_out_ok, 32)
            for hh in range(2):
                pe.wait_ge(comb_ok, hh + 1)
                for i in range(HTILES):
                    ins = tr(bank[1 + hh][0:EXPERTS, tile_cols(i)], comb[:, hh * HTILES + i, :], ident[:])
                ins.then_inc(comb_tr, 1)
            gate_up(0, 0, 0, True)
            gate_up(0, 0, 1, True)
            pe.wait_ge(combT_out, 2)
            for j in range(4):
                mm(bank[j][:], zeros[:, 0:P], zeros[:], start=True, stop=False, skip_group_check=True)

            def moe_pe(m, last=False):
                for t in range(PARTS):
                    it = m * PARTS + t
                    end = last and t == PARTS - 1
                    for h in range(2):
                        if not end:
                            gate_up(it + 1, (t + 1) % PARTS, h, False)
                        down_half(it, t, h, end)

            with pe.Fori(0, GROUPS - 1) as m:
                moe_pe(m)
            moe_pe(GROUPS - 1, last=True)

            def block_back(k, i, b):
                pe.wait_ge(out_first, k + 1)
                pe.wait_ge(out_second, k + 1)
                for j in range(2):
                    for o in range(OT_):
                        ins = tr(bank[b][:, j * DIM + o * P:j * DIM + (o + 1) * P],
                                 OT[k % 2][:, o, tile_cols(2 * i + j)], ident[:])
                ins.then_inc(out_back, 1)

            def head_product(j):
                for i in range(2):
                    ins = mm(bank[PRODUCT_BANKS[j]][:, tile_cols(i, DIM)], wv[:, 2 * j + i, :], wo[:, 2 * j + i, :],
                             start=True, stop=True)
                ins.then_inc(prod_mm, 1)

            block_back(0, 0, 0)
            block_back(0, 1, 2)
            pe.wait_ge(ld_v, 32)
            pe.wait_ge(weighted, 2 * EXPERT_TILES)
            pe.wait_ge(out_first, 2)
            pe.wait_ge(out_second, 2)
            for j in range(6):
                head_product(j)
            pe.wait_ge(x_new, 6)
            xt_transpose(2, (0, 2), 0)

            def keys_T(N):
                pe.wait_ge(kn_ok, N + 1)
                for i in range(HTILES):
                    ins = tr(bank[3][:, tile_cols(i)], kn[:, i, :], ident[:])
                ins.then_inc(k_turned, 1)

            def queries(N, H):
                pe.wait_ge(wq_lo_ok, N + 1)
                if not (isinstance(N, int) and N == 0):
                    pe.wait_ge(q_sum_eps, N)
                c = tile_cols(H, HALF)
                for kt in range(KT):
                    ins = three(mm, bank[2][:], wqhi[:, kt, :], wqlo[:, kt, :], XThi[:, kt, c], XTlo[:, kt, c],
                                kt == 0, kt == KT - 1)
                ins.then_inc(q_mm, 1)

            def query_squares(N):
                pe.wait_ge(q_sq, N + 1)
                pe.wait_ge(q_lo, N + 1)
                for i in range(HTILES):
                    ins = tr(bank[2][:, tile_cols(i)], qsq[:, tile_cols(i)], ident[:])
                ins.then_inc(q_sq_turned, 1)

            def scores(N):
                pe.wait_ge(k_lo, N + 1)
                pe.wait_ge(q_lo, N + 1)
                for b in range(2):
                    if not (isinstance(N, int) and N == 0):
                        pe.wait_ge(s_exp, 4 * N - 2 + 2 * b)
                    kc = tile_cols(b, SEQ)
                    for i in range(2):
                        qc = tile_cols(2 * b + i)
                        ins = three(mm, bank[4 + b][:, tile_cols(i, SEQ)], qhi[:, qc], qlo[:, qc], khi[:, kc], klo[:, kc],
                                    True, True)
                    ins.then_inc(scores_mm, 1)

            def probs_T(N, par):
                for b in range(2):
                    pe.wait_ge(s_norm, 2 * N + b + 1)
                    if b == 0 and not (isinstance(N, int) and N == 0):
                        pe.wait_ge(ctxo_lo, N)
                    if not (isinstance(N, int) and N == 0):
                        pe.wait_ge(p_lo, 2 * N - 1 + b)
                    for j in range(2):
                        for i in range(2):
                            ins = tr(bank[6 + b][:, j * SEQ + i * P:j * SEQ + (i + 1) * P], Pm[par][:, b, i, tile_cols(j)], ident[:])
                    ins.then_inc(p_turned, 1)

            def weighted_context(N, H):
                for b in range(2):
                    pe.wait_ge(p_lo, 2 * N + b + 1)
                    for j in range(2):
                        tt = H * HTILES + 2 * b + j
                        ins = three(mm, context_bank(N)[:, tile_cols(b, SEQ)], ctxhi[:, tt, :], ctxlo[:, tt, :],
                                    PThi[:, b, j, :], PTlo[:, b, j, :], j == 0, j == 1)
                ins.then_inc(context_mm, 1)

            def head_output(N, last):
                pe.wait_ge(ctxo_lo, N + 1)
                pe.wait_ge(ph_ld, 32 * (N + 1))
                for o in range(OT_):
                    ins = three(mm, bank[o][:], phhi[:, tile_cols(o)], phlo[:, tile_cols(o)], ohi[:], olo[:], False, last)
                ins.then_inc(head_out, 1)

            def open_output():
                for o in range(OT_):
                    mm(bank[o][:], zeros[:, 0:P], zeros[:], start=True, stop=False, skip_group_check=True)

            def head_pe(n, h, par, at):
                N = n + h * HEADS
                scores(N)
                if at is not None and at - 1 in TURN:
                    pe.wait_ge(xt_lo, 2 * TURN[at - 1] + 2)
                if at != LAST:
                    queries(N + 1, ahead(n, h, 1)[1])
                if at == 0:
                    pe.wait_ge(prod_lo, 7)
                    head_product(7)
                else:
                    probs_T(N - 1, 1 - par)
                if at is not None and at - 1 in BACK:
                    k, piece = BACK[at - 1]
                    pe.wait_ge(x_new, 4 + 2 * k + piece + 1)
                if at != LAST:
                    keys_T(N + 1)
                if at not in (0, 1):
                    head_output(N - 2, at == HEADS + 1)
                if at != LAST:
                    query_squares(N + 1)
                if at != 0:
                    weighted_context(N - 1, ahead(n, h, -1)[1])
                if at in BACK:
                    pe.wait_ge(k_lo, N + 2)
                    block_back(*BACK[at], 3)
                if at in TURN:
                    pe.wait_ge(k_lo, N + 2)
                    xt_transpose(TURN[at], (3, 7), TURN[at] % 2)
                if at == HEADS + 1:
                    pe.wait_ge(out_first, 3)
                    pe.wait_ge(out_second, 3)
                    open_output()

            pe.wait_ge(prod_lo, 1)
            keys_T(0)
            pe.wait_ge(xt_lo, 6)
            queries(0, 0)
            pe.wait_ge(prod_lo, 6)
            open_output()
            head_product(6)
            query_squares(0)
            pe.wait_ge(ctx_split, 2)
            all_heads(pe, head_pe)
            def ff_gate_up(H, i):
                k = H * (FFT + 1) + i
                G, U = gate_up_banks(k)
                if 2 <= k < 2 * FFT + 1:
                    pe.wait_ge(f_h, k - 1)
                c = tile_cols(H, HALF)
                for j in range(2 if i < FFT else 1):
                    for kt in range(KT):
                        ins = three(mm, bank[(G, U)[j]][:], wfhi[:, 2 * i + j, tile_cols(kt)], wflo[:, 2 * i + j, tile_cols(kt)],
                                    XThi[:, kt, c], XTlo[:, kt, c], kt == 0, kt == KT - 1)
                    ins.then_inc((f_g, f_u)[j], 1)

            def ff_down(H, i):
                k = H * (FFT + 1) + i
                pe.wait_ge(f_lo, k + 1)
                r = slice(0, P) if i < FFT else slice(FFR, 2 * FFR)
                t = 2 * FFT + 1 + i
                for o in range(OT_):
                    low = wflo[:, t, tile_cols(o)] if i < FFT - 1 else wflo2[r, i - FFT + 1, tile_cols(o)]
                    ins = three(mm, bank[o][:], wfhi[r, t, tile_cols(o)], low,
                                hidhi[i % 2][r, :], hidlo[i % 2][r, :], i == 0, i == FFT)
                ins.then_inc(f_down, 1)

            pe.wait_ge(ff_lo, 12)
            pe.wait_ge(xt_lo, 10)
            pe.wait_ge(s_exp, 4 * (LAST + 1))
            pe.wait_ge(k_lo, LAST + 1)
            ff_gate_up(0, 0)
            head_output(LAST - 1, False)
            probs_T(LAST, 1)
            weighted_context(LAST, 1)
            ff_gate_up(0, 1)
            head_output(LAST, True)
            block_back(3, 0, 2)
            block_back(3, 1, 3)
            for k in range(2 * (FFT + 1)):
                if k == FFT + 1:
                    pe.wait_ge(out_first, 5)
                    pe.wait_ge(out_second, 5)
                ff_down(k // (FFT + 1), k % (FFT + 1))
                if k + 2 < 2 * FFT + 1:
                    if k + 2 == FFT + 1:
                        pe.wait_ge(xt_lo, 12)
                    ff_gate_up((k + 2) // (FFT + 1), (k + 2) % (FFT + 1))
                if k == 2 * FFT - 2:
                    pe.wait_ge(x_new, 14)
                    ff_gate_up(1, FFT)
                if k == 2:
                    pe.wait_ge(x_new, 12)
                    xt_transpose(5, (2, 3), 1)
                if k == FFT + 2:
                    block_back(4, 0, 2)
                    block_back(4, 1, 3)
            block_back(5, 0, 4)
            block_back(5, 1, 5)


def kernel(**inputs):
    import numpy as np
    import concourse.bacc as bacc
    from concourse.bass_utils import run_bass_kernel_spmd as run

    a = {k: np.asarray(v) for k, v in inputs.items()}
    T = np.ascontiguousarray
    ctx_tok = a["ctx_1024"].reshape(TOK, CDIM)
    gu = a["L0_ffn_gate_up_proj"].reshape(GROUPS, GROUP, 2, PARTS, 32, KT, P).transpose(0, 3, 6, 5, 2, 1, 4)
    dn = a["L0_ffn_down_proj"].reshape(GROUPS, GROUP, DIM, PARTS, 32).transpose(0, 3, 1, 4, 2)
    moe = np.concatenate([gu.reshape(GROUPS * PARTS * P, 2 * DIM), dn.reshape(GROUPS * PARTS * P, DIM)], axis=1)
    gT, uT = a["L1_ffn_gate_w"].T, a["L1_ffn_up_w"].T
    tiles = []
    for i in range(FFT):
        tiles += [gT[:, i * P:(i + 1) * P], uT[:, i * P:(i + 1) * P]]
    tiles.append(np.concatenate([gT[:, FFT * P:], uT[:, FFT * P:]], axis=1))
    w13 = np.stack([t.reshape(KT, P, P) for t in tiles]).transpose(2, 0, 1, 3).reshape(P, -1)
    dT = a["L1_ffn_down_w"].T
    cols = np.concatenate([
        a["L0_xattn_bq"][:, None], a["L0_xattn_bk"][:, None], a["L1_xattn_gq"][:, None], a["L1_xattn_gk"][:, None],
        a["L1_ffn_down_s"].reshape(2, P).T, a["L1_ffn_gate_s"][:FFT * P].reshape(FFT, P).T,
        a["L1_ffn_up_s"][:FFT * P].reshape(FFT, P).T], axis=1)
    arrays = {
        "x": a["x"].reshape(TOK, DIM),
        "ctxn": ctx_tok,
        "ctxT": ctx_tok.T,
        "w0": np.concatenate([a["L0_xattn_Wq"].T, a["L0_xattn_Wk"].T], axis=1),
        "cols": cols,
        "tailg": a["L1_ffn_gate_s"][FFT * P:, None],
        "tailu": a["L1_ffn_up_s"][FFT * P:, None],
        "gates": np.stack([a["g_xattn"][0], a["g_ffn"][0], a["g_xattn"][1], a["g_ffn"][1]]),
        "gw": a["L0_ffn_gate_weight"].T,
        "moe": moe,
        "wq": a["L1_xattn_Wq"].reshape(KT, P, HEADS, HD).transpose(1, 2, 0, 3).reshape(P, -1),
        "wk": a["L1_xattn_Wk"],
        "wv": a["L1_xattn_Wv"].reshape(CDIM, HEADS, HD).transpose(2, 1, 0).reshape(P, -1),
        "wo": a["L1_xattn_Wo"].reshape(HEADS, HD, DIM).transpose(1, 0, 2).reshape(P, -1),
        "wff": np.concatenate([w13, dT[:FFT * P].reshape(FFT, P, DIM).transpose(1, 0, 2).reshape(P, -1)], axis=1),
        "w2t": dT[FFT * P:],
    }
    arrays = {f"in_{k}": T(v) for k, v in arrays.items()}
    nc = bacc.Bacc("TRN2", target_bir_lowering=False, num_devices=1)
    args = [nc.dram_tensor(k, v.shape, F32, kind="ExternalInput").ap() for k, v in arrays.items()]
    args.append(nc.dram_tensor("result", (TOK, DIM), F32, kind="ExternalOutput").ap())
    args.append(nc.dram_tensor("combine", (EXPERTS, TOK), F32, kind="Internal").ap())
    flamingo(nc, *args)
    r = run(nc, [arrays], core_ids=[0])
    return r.results[0]["result"].reshape(BATCH, SEQ, DIM)
```
